# Optimizing a Trainium2 kernel written in Bass

```python
import numpy as np
import jax
import jax.numpy as jnp

def _softmax(x, axis=-1):
    return jax.nn.softmax(x, axis=axis)

def _gelu(x):
    return jax.nn.gelu(x, approximate=True)

def _silu(x):
    return jax.nn.silu(x)

def _sigmoid(x):
    return jax.nn.sigmoid(x)

def _layernorm(x, axis=-1, eps=1e-05):
    m = jnp.mean(x, axis=axis, keepdims=True)
    v = jnp.var(x, axis=axis, keepdims=True)
    return (x - m) / jnp.sqrt(v + eps)

def _scatter_add(tgt, idx, src, axis=0):
    return tgt.at[idx].add(src)

def _segment_sum(src, seg, n):
    return jax.ops.segment_sum(src, seg, n)
kernel_name = 'mk_decoder_postln_d2_seqx_r4_afd46f'

def setup_inputs(seed: int=0):
    np.random.seed(seed)
    _w = jnp.asarray

    def _rec_inputs():
        import jax
        import jax.numpy as jnp
        _rk = jax.random.key(seed)
        x = -0.000125 + 0.9999 * jax.random.normal(jax.random.fold_in(_rk, 1), (4, 512, 256), jnp.float32)
        _lenS = 512 - jax.random.randint(jax.random.fold_in(_rk, 7), (4,), 0, max(1, 512 // 4) + 1, jnp.int32)
        _lenS2 = 1601 - jax.random.randint(jax.random.fold_in(_rk, 8), (4,), 0, max(1, 1601 // 4) + 1, jnp.int32)
        _ctx_768P = jax.random.normal(jax.random.fold_in(_rk, 11), (4, 16, 192), jnp.float32)
        _ctx_768c = jax.random.dirichlet(jax.random.fold_in(_rk, 511), 0.3 * jnp.ones((16,), jnp.float32), (4, 1601))
        _ctx_768t = jnp.einsum('bsk,bkd->bsd', _ctx_768c, _ctx_768P)
        _ctx_768t = _ctx_768t * jax.lax.rsqrt(jnp.mean(jnp.square(_ctx_768t)) + 1e-12) * 0.953939
        ctx_768 = -7.36909e-05 + 0.999899 * (_ctx_768t + 0.3 * jax.random.normal(jax.random.fold_in(_rk, 611), (4, 1601, 192), jnp.float32))
        return (x, ctx_768)
    x, ctx_768 = _rec_inputs()

    def _L0_attn_setup():
        import jax, jax.numpy as jnp
        import numpy as np
        D = 256
        H = 16
        N = D // H
        B = 4
        T = 512
        NLAYERS = 12
        LAYER_ID = 6
        EPS = 1e-05 * 64

        def _forward(x, w_r, w_k, w_v, w_g, w_o, time_maa_k, time_maa_v, time_maa_r, time_maa_g, time_decay, time_faaaa, ln_g, ln_b):
            Bs, Ts, C = x.shape
            if Ts % 64 == 0:
                Q = 64
            elif Ts % 128 == 0:
                Q = 128
            else:
                Q = Ts
            nC = Ts // Q
            xs = jnp.pad(x, ((0, 0), (1, 0), (0, 0)))[:, :-1]
            xx = xs - x
            xk = x + xx * time_maa_k
            xv = x + xx * time_maa_v
            xr = x + xx * time_maa_r
            xg = x + xx * time_maa_g
            r = (xr @ w_r.T).reshape(Bs, Ts, H, N).transpose(0, 2, 1, 3)
            k = (xk @ w_k.T).reshape(Bs, Ts, H, N).transpose(0, 2, 3, 1)
            v = (xv @ w_v.T).reshape(Bs, Ts, H, N).transpose(0, 2, 1, 3)
            g = jax.nn.silu(xg @ w_g.T)
            w = jnp.exp(-jnp.exp(time_decay))
            u = time_faaaa
            ws = (w ** Q)[None, :, None, None]
            q = jnp.arange(Q)
            wk = (w[:, None] ** (Q - 1 - q)[None, :])[None, :, None, :]
            wb = (w[:, None] ** q[None, :])[None, :, :, None]
            ii = q[:, None]
            jj = q[None, :]
            e = jnp.maximum(ii - jj - 1, 0)
            Wmat = jnp.where((jj < ii)[None], w[:, None, None] ** e[None], 0.0)
            Wmat = Wmat + jnp.eye(Q, dtype=x.dtype)[None] * u[:, None, None]
            Wmat = Wmat[None]
            rC = r.reshape(Bs, H, nC, Q, N).transpose(2, 0, 1, 3, 4)
            kC = k.reshape(Bs, H, N, nC, Q).transpose(3, 0, 1, 2, 4)
            vC = v.reshape(Bs, H, nC, Q, N).transpose(2, 0, 1, 3, 4)

            def step(state, inp):
                rr, kk, vv = inp
                y = rr @ kk * Wmat @ vv + rr @ state * wb
                state = ws * state + kk * wk @ vv
                return (state, y)
            state0 = jnp.zeros((Bs, H, N, N), x.dtype)
            _, yC = jax.lax.scan(step, state0, (rC, kC, vC))
            y = yC.transpose(1, 2, 0, 3, 4).reshape(Bs, H, Ts, N)
            y = y.transpose(0, 2, 1, 3).reshape(Bs * Ts, H, N)
            mu = y.mean(-1, keepdims=True)
            var = y.var(-1, keepdims=True)
            y = (y - mu) / jnp.sqrt(var + EPS)
            y = y.reshape(Bs, Ts, C) * ln_g + ln_b
            y = y * g
            return y @ w_o.T
        key = jax.random.key(seed)
        ks = jax.random.split(key, 6)
        r01 = LAYER_ID / (NLAYERS - 1)
        r10 = 1.0 - LAYER_ID / NLAYERS
        ddd = np.arange(D, dtype=np.float64) / D
        maa_k = (1.0 - ddd ** r10).astype(np.float32)
        maa_v = (1.0 - (ddd ** r10 + 0.3 * r01)).astype(np.float32)
        maa_r = (1.0 - ddd ** (0.5 * r10)).astype(np.float32)
        maa_g = maa_r.copy()
        hh = np.arange(H, dtype=np.float64)
        decay = (-6.0 + 5.0 * (hh / (H - 1)) ** (0.7 + 1.3 * r01)).astype(np.float32)
        faaaa = (r01 * (1.0 - hh / (H - 1))).astype(np.float32)
        s = 0.02
        return {'x': jax.random.normal(ks[0], (B, T, D), jnp.float32), 'w_r': jax.random.normal(ks[1], (D, D), jnp.float32) * s, 'w_k': jax.random.normal(ks[2], (D, D), jnp.float32) * s, 'w_v': jax.random.normal(ks[3], (D, D), jnp.float32) * s, 'w_g': jax.random.normal(ks[4], (D, D), jnp.float32) * s, 'w_o': jax.random.normal(ks[5], (D, D), jnp.float32) * s, 'time_maa_k': jnp.asarray(maa_k), 'time_maa_v': jnp.asarray(maa_v), 'time_maa_r': jnp.asarray(maa_r), 'time_maa_g': jnp.asarray(maa_g), 'time_decay': jnp.asarray(decay), 'time_faaaa': jnpp if False else jnp.asarray(faaaa), 'ln_g': jnp.ones((D,), jnp.float32), 'ln_b': jnp.zeros((D,), jnp.float32)}
    _L0_attn_all = _L0_attn_setup()
    _L0_attn_in = {k: v for k, v in _L0_attn_all.items() if k in ('w_r', 'w_k', 'w_v', 'w_g', 'w_o', 'time_maa_k', 'time_maa_v', 'time_maa_r', 'time_maa_g', 'time_decay', 'time_faaaa', 'ln_g', 'ln_b')}
    del _L0_attn_all

    def _L0_xattn_setup():
        import jax, jax.numpy as jnp
        import numpy as np
        import math
        E = 256
        EV = 256
        FFN = 1024
        DINO = 192
        B, S, P = (64, 128, 64)

        def bitnet_linear(x, W, b):
            w_scale = jnp.maximum(jnp.mean(jnp.abs(W)), 1e-05)
            qW = jnp.sign(W) * (jnp.abs(W) > 0.5 * w_scale).astype(W.dtype)
            i_scale = jnp.maximum(jnp.max(jnp.abs(x)), 1e-08) / 127.0
            qx = jnp.clip(jnp.round(x / i_scale), -128.0, 127.0)
            out = jnp.einsum('...i,oi->...o', qx, qW) * (w_scale * i_scale)
            return out + b
        key = jax.random.key(seed)
        ks = iter(jax.random.split(key, 32))

        def lin_w(fin, fout):
            return jax.random.normal(next(ks), (fout, fin), jnp.float32) * math.sqrt(2.0 / fin)
        return {'text_embeddings': jax.random.normal(next(ks), (B, S, E), jnp.float32), 'dinov2_features': jax.random.normal(next(ks), (B, P, DINO), jnp.float32), 'W_d2v': lin_w(DINO, EV), 'b_d2v': jnp.zeros((EV,), jnp.float32), 'W_img': lin_w(EV, E), 'b_img': jnp.zeros((E,), jnp.float32), 'W_txt': lin_w(E, E), 'b_txt': jnp.zeros((E,), jnp.float32), 'W_att0': lin_w(E, E // 2), 'b_att0': jnp.zeros((E // 2,), jnp.float32), 'W_att1': lin_w(E, E // 2), 'b_att1': jnp.zeros((E // 2,), jnp.float32), 'W_f1': lin_w(2 * E, FFN), 'b_f1': jnp.zeros((FFN,), jnp.float32), 'W_f2': lin_w(FFN, E), 'b_f2': jnp.zeros((E,), jnp.float32)}
    _L0_xattn_all = _L0_xattn_setup()
    _L0_xattn_in = {k: v for k, v in _L0_xattn_all.items() if k in ('W_d2v', 'b_d2v', 'W_img', 'b_img', 'W_txt', 'b_txt', 'W_att0', 'b_att0', 'W_att1', 'b_att1', 'W_f1', 'b_f1', 'W_f2', 'b_f2')}
    del _L0_xattn_all

    def _L0_ffn_setup():
        import jax, jax.numpy as jnp
        import numpy as np
        E, K, D, F = (8, 2, 256, 1024)
        EPS = 1e-06
        B, S = (2, 256)
        key = jax.random.key(seed)
        ks = jax.random.split(key, 6)
        s_in = 1.0 / np.sqrt(D)
        s_mid = 1.0 / np.sqrt(F)
        return {'x': jax.random.normal(ks[0], (B, S, D), dtype=jnp.float32), 'Wg': jax.random.normal(ks[1], (D, E), dtype=jnp.float32) * s_in, 'gamma': jnp.ones((E, D), dtype=jnp.float32), 'beta': jnp.zeros((E, D), dtype=jnp.float32), 'W1': jax.random.normal(ks[2], (E, D, F), dtype=jnp.float32) * s_in, 'b1': jnp.zeros((E, F), dtype=jnp.float32), 'W2': jax.random.normal(ks[3], (E, F, D), dtype=jnp.float32) * s_mid, 'b2': jnp.zeros((E, D), dtype=jnp.float32)}
    _L0_ffn_all = _L0_ffn_setup()
    _L0_ffn_in = {k: v for k, v in _L0_ffn_all.items() if k in ('Wg', 'gamma', 'beta', 'W1', 'b1', 'W2', 'b2')}
    del _L0_ffn_all

    def _L1_attn_setup():
        import jax, jax.numpy as jnp
        import numpy as np
        LN_EPS = 1e-05

        def _phi(x):
            return jax.nn.elu(x) + 1.0
        key = jax.random.key(seed)
        ks = jax.random.split(key, 5)
        B, N, D = (4, 2048, 256)
        s = 1.0 / np.sqrt(D)
        return {'H': jax.random.normal(ks[0], (B, N, D), dtype=jnp.float32), 'W_qkv': jax.random.normal(ks[1], (3 * D, D), dtype=jnp.float32) * s, 'b_qkv': jax.random.normal(ks[2], (3 * D,), dtype=jnp.float32) * 0.01, 'W_proj': jax.random.normal(ks[3], (D, D), dtype=jnp.float32) * s, 'b_proj': jax.random.normal(ks[4], (D,), dtype=jnp.float32) * 0.01, 'gamma': jnp.ones((D,), dtype=jnp.float32), 'beta': jnp.zeros((D,), dtype=jnp.float32)}
    _L1_attn_all = _L1_attn_setup()
    _L1_attn_in = {k: v for k, v in _L1_attn_all.items() if k in ('W_qkv', 'b_qkv', 'W_proj', 'b_proj', 'gamma', 'beta')}
    del _L1_attn_all

    def _L1_xattn_setup():
        import jax, jax.numpy as jnp
        import numpy as np
        N_HEADS = 8
        D_EMBED = 256
        D_CROSS = 192
        D_HEAD = D_EMBED // N_HEADS
        key = jax.random.key(seed)
        ks = jax.random.split(key, 10)
        B, SQ, SKV = (8, 1024, 77)
        scale_e = 1.0 / np.sqrt(D_EMBED)
        scale_c = 1.0 / np.sqrt(D_CROSS)
        return {'x': jax.random.normal(ks[0], (B, SQ, D_EMBED), dtype=jnp.float32), 'y': jax.random.normal(ks[1], (B, SKV, D_CROSS), dtype=jnp.float32), 'Wq': jax.random.normal(ks[2], (D_EMBED, D_EMBED), dtype=jnp.float32) * scale_e, 'bq': jnp.zeros((D_EMBED,), dtype=jnp.float32), 'Wk': jax.random.normal(ks[3], (D_CROSS, D_EMBED), dtype=jnp.float32) * scale_c, 'bk': jnp.zeros((D_EMBED,), dtype=jnp.float32), 'Wv': jax.random.normal(ks[4], (D_CROSS, D_EMBED), dtype=jnp.float32) * scale_c, 'bv': jnp.zeros((D_EMBED,), dtype=jnp.float32), 'Wo': jax.random.normal(ks[5], (D_EMBED, D_EMBED), dtype=jnp.float32) * scale_e, 'bo': jnp.zeros((D_EMBED,), dtype=jnp.float32)}
    _L1_xattn_all = _L1_xattn_setup()
    _L1_xattn_in = {k: v for k, v in _L1_xattn_all.items() if k in ('Wq', 'bq', 'Wk', 'bk', 'Wv', 'bv', 'Wo', 'bo')}
    del _L1_xattn_all

    def _L1_ffn_setup():
        import jax, jax.numpy as jnp
        import numpy as np
        DIM = 256
        DEPTH = 2
        HEADS = 8
        DIM_HEAD = 64
        WINDOW = 128
        INNER = HEADS * DIM_HEAD
        HID = int(DIM * 4 * 2 / 3)
        B, N = (2, 2048)
        QK_SCALE = 8.0

        def shift_token(t):
            t1, t2 = jnp.split(t, 2, axis=-1)
            t2 = jnp.pad(t2, ((0, 0), (1, 0), (0, 0)))[:, :-1]
            return jnp.concatenate([t1, t2], axis=-1)

        def l2norm(t):
            return t / jnp.clip(jnp.linalg.norm(t, axis=-1, keepdims=True), 1e-12)

        def rotate_half(x):
            x1, x2 = jnp.split(x, 2, axis=-1)
            return jnp.concatenate([-x2, x1], axis=-1)

        def rotary_xpos(q, k):
            n = q.shape[-2]
            half_idx = jnp.arange(0, DIM_HEAD, 2, dtype=jnp.float32)
            inv_freq = 1.0 / 10000.0 ** (half_idx / DIM_HEAD)
            t = jnp.arange(n, dtype=jnp.float32)
            freqs = t[:, None] * inv_freq[None, :]
            freqs = jnp.concatenate([freqs, freqs], axis=-1)
            base = (half_idx + 0.4 * DIM_HEAD) / (1.4 * DIM_HEAD)
            power = (t - n // 2) / float(WINDOW // 2)
            scale = base[None, :] ** power[:, None]
            scale = jnp.concatenate([scale, scale], axis=-1)
            cos, sin = (jnp.cos(freqs), jnp.sin(freqs))
            q = q * cos * scale + rotate_half(q) * sin * scale
            k = k * cos / scale + rotate_half(k) * sin / scale
            return (q, k)

        def local_attention(q, k, v):
            b, h, n, d = q.shape
            w = n // WINDOW
            bq = q.reshape(b, h, w, WINDOW, d) * QK_SCALE
            bk = k.reshape(b, h, w, WINDOW, d)
            bv = v.reshape(b, h, w, WINDOW, d)

            def look_around(t):
                p = jnp.pad(t, ((0, 0), (0, 0), (1, 0), (0, 0), (0, 0)))
                return jnp.concatenate([p[:, :, :w], p[:, :, 1:]], axis=3)
            bk, bv = (look_around(bk), look_around(bv))
            bt = jnp.arange(n).reshape(w, WINDOW)
            btp = jnp.pad(bt, ((1, 0), (0, 0)), constant_values=-1)
            btk = jnp.concatenate([btp[:w], btp[1:]], axis=1)
            sim = jnp.einsum('bhwid,bhwjd->bhwij', bq, bk)
            i = bt[:, :, None]
            j = btk[:, None, :]
            mask = (i < j) | (i > j + WINDOW) | (j == -1)
            sim = jnp.where(mask, -jnp.finfo(sim.dtype).max, sim)
            attn = jax.nn.softmax(sim, axis=-1)
            out = jnp.einsum('bhwij,bhwjd->bhwid', attn, bv)
            return out.reshape(b, h, n, d)

        def _layer(x, wqkv, qs, ksc, wo, lg, lb, w1, b1, w2, b2):
            b, n, _ = x.shape
            h = shift_token(x)
            qkv = h @ wqkv
            q, k, v = jnp.split(qkv, 3, axis=-1)
            to_heads = lambda t: t.reshape(b, n, HEADS, DIM_HEAD).transpose(0, 2, 1, 3)
            q, k, v = (to_heads(q), to_heads(k), to_heads(v))
            q = l2norm(q) * qs
            k = l2norm(k) * ksc
            q, k = rotary_xpos(q, k)
            o = local_attention(q, k, v)
            o = o.transpose(0, 2, 1, 3).reshape(b, n, INNER)
            x = x + o @ wo
            h = shift_token(x)
            mu = h.mean(-1, keepdims=True)
            var = h.var(-1, keepdims=True)
            h = (h - mu) / jnp.sqrt(var + 1e-05) * lg + lb
            h = h @ w1 + b1
            a, g = jnp.split(h, 2, axis=-1)
            h = a * jax.nn.gelu(g, approximate=False)
            x = x + h @ w2 + b2
            return x
        key = jax.random.key(seed)
        ks = jax.random.split(key, 6)
        return {'x': jax.random.normal(ks[0], (B, N, DIM), jnp.float32), 'wqkv': jax.random.normal(ks[1], (DEPTH, DIM, 3 * INNER), jnp.float32) * 0.02, 'q_scale': jnp.ones((DEPTH, DIM_HEAD), jnp.float32), 'k_scale': jnp.ones((DEPTH, DIM_HEAD), jnp.float32), 'wo': jax.random.normal(ks[2], (DEPTH, INNER, DIM), jnp.float32) * 0.02, 'ln_g': jnp.ones((DEPTH, DIM), jnp.float32), 'ln_b': jnp.zeros((DEPTH, DIM), jnp.float32), 'w1': jax.random.normal(ks[3], (DEPTH, DIM, 2 * HID), jnp.float32) * 0.02, 'b1': jnp.zeros((DEPTH, 2 * HID), jnp.float32), 'w2': jax.random.normal(ks[4], (DEPTH, HID, DIM), jnp.float32) * 0.02, 'b2': jnp.zeros((DEPTH, DIM), jnp.float32)}
    _L1_ffn_all = _L1_ffn_setup()
    _L1_ffn_in = {k: v for k, v in _L1_ffn_all.items() if k in ('wqkv', 'q_scale', 'k_scale', 'wo', 'ln_g', 'ln_b', 'w1', 'b1', 'w2', 'b2')}
    del _L1_ffn_all
    return {'x': x, 'ctx_768': ctx_768, 'L0_attn_w_r': _L0_attn_in['w_r'], 'L0_attn_w_k': _L0_attn_in['w_k'], 'L0_attn_w_v': _L0_attn_in['w_v'], 'L0_attn_w_g': _L0_attn_in['w_g'], 'L0_attn_w_o': _L0_attn_in['w_o'], 'L0_attn_time_maa_k': _L0_attn_in['time_maa_k'], 'L0_attn_time_maa_v': _L0_attn_in['time_maa_v'], 'L0_attn_time_maa_r': _L0_attn_in['time_maa_r'], 'L0_attn_time_maa_g': _L0_attn_in['time_maa_g'], 'L0_attn_time_decay': _L0_attn_in['time_decay'], 'L0_attn_time_faaaa': _L0_attn_in['time_faaaa'], 'L0_attn_ln_g': _L0_attn_in['ln_g'], 'L0_attn_ln_b': _L0_attn_in['ln_b'], 'L0_xattn_W_d2v': _L0_xattn_in['W_d2v'], 'L0_xattn_b_d2v': _L0_xattn_in['b_d2v'], 'L0_xattn_W_img': _L0_xattn_in['W_img'], 'L0_xattn_b_img': _L0_xattn_in['b_img'], 'L0_xattn_W_txt': _L0_xattn_in['W_txt'], 'L0_xattn_b_txt': _L0_xattn_in['b_txt'], 'L0_xattn_W_att0': _L0_xattn_in['W_att0'], 'L0_xattn_b_att0': _L0_xattn_in['b_att0'], 'L0_xattn_W_att1': _L0_xattn_in['W_att1'], 'L0_xattn_b_att1': _L0_xattn_in['b_att1'], 'L0_xattn_W_f1': _L0_xattn_in['W_f1'], 'L0_xattn_b_f1': _L0_xattn_in['b_f1'], 'L0_xattn_W_f2': _L0_xattn_in['W_f2'], 'L0_xattn_b_f2': _L0_xattn_in['b_f2'], 'L0_ffn_Wg': _L0_ffn_in['Wg'], 'L0_ffn_gamma': _L0_ffn_in['gamma'], 'L0_ffn_beta': _L0_ffn_in['beta'], 'L0_ffn_W1': _L0_ffn_in['W1'], 'L0_ffn_b1': _L0_ffn_in['b1'], 'L0_ffn_W2': _L0_ffn_in['W2'], 'L0_ffn_b2': _L0_ffn_in['b2'], 'L1_attn_W_qkv': _L1_attn_in['W_qkv'], 'L1_attn_b_qkv': _L1_attn_in['b_qkv'], 'L1_attn_W_proj': _L1_attn_in['W_proj'], 'L1_attn_b_proj': _L1_attn_in['b_proj'], 'L1_attn_gamma': _L1_attn_in['gamma'], 'L1_attn_beta': _L1_attn_in['beta'], 'L1_xattn_Wq': _L1_xattn_in['Wq'], 'L1_xattn_bq': _L1_xattn_in['bq'], 'L1_xattn_Wk': _L1_xattn_in['Wk'], 'L1_xattn_bk': _L1_xattn_in['bk'], 'L1_xattn_Wv': _L1_xattn_in['Wv'], 'L1_xattn_bv': _L1_xattn_in['bv'], 'L1_xattn_Wo': _L1_xattn_in['Wo'], 'L1_xattn_bo': _L1_xattn_in['bo'], 'L1_ffn_wqkv': _L1_ffn_in['wqkv'], 'L1_ffn_q_scale': _L1_ffn_in['q_scale'], 'L1_ffn_k_scale': _L1_ffn_in['k_scale'], 'L1_ffn_wo': _L1_ffn_in['wo'], 'L1_ffn_ln_g': _L1_ffn_in['ln_g'], 'L1_ffn_ln_b': _L1_ffn_in['ln_b'], 'L1_ffn_w1': _L1_ffn_in['w1'], 'L1_ffn_b1': _L1_ffn_in['b1'], 'L1_ffn_w2': _L1_ffn_in['w2'], 'L1_ffn_b2': _L1_ffn_in['b2']}

def reference(x, ctx_768, L0_attn_w_r, L0_attn_w_k, L0_attn_w_v, L0_attn_w_g, L0_attn_w_o, L0_attn_time_maa_k, L0_attn_time_maa_v, L0_attn_time_maa_r, L0_attn_time_maa_g, L0_attn_time_decay, L0_attn_time_faaaa, L0_attn_ln_g, L0_attn_ln_b, L0_xattn_W_d2v, L0_xattn_b_d2v, L0_xattn_W_img, L0_xattn_b_img, L0_xattn_W_txt, L0_xattn_b_txt, L0_xattn_W_att0, L0_xattn_b_att0, L0_xattn_W_att1, L0_xattn_b_att1, L0_xattn_W_f1, L0_xattn_b_f1, L0_xattn_W_f2, L0_xattn_b_f2, L0_ffn_Wg, L0_ffn_gamma, L0_ffn_beta, L0_ffn_W1, L0_ffn_b1, L0_ffn_W2, L0_ffn_b2, L1_attn_W_qkv, L1_attn_b_qkv, L1_attn_W_proj, L1_attn_b_proj, L1_attn_gamma, L1_attn_beta, L1_xattn_Wq, L1_xattn_bq, L1_xattn_Wk, L1_xattn_bk, L1_xattn_Wv, L1_xattn_bv, L1_xattn_Wo, L1_xattn_bo, L1_ffn_wqkv, L1_ffn_q_scale, L1_ffn_k_scale, L1_ffn_wo, L1_ffn_ln_g, L1_ffn_ln_b, L1_ffn_w1, L1_ffn_b1, L1_ffn_w2, L1_ffn_b2):
    import jax
    import jax.numpy as jnp

    def _L0_attn_ref(x, w_r, w_k, w_v, w_g, w_o, time_maa_k, time_maa_v, time_maa_r, time_maa_g, time_decay, time_faaaa, ln_g, ln_b):
        import jax, jax.numpy as jnp
        import numpy as np
        D = 256
        H = 16
        N = D // H
        B = 4
        T = 512
        NLAYERS = 12
        LAYER_ID = 6
        EPS = 1e-05 * 64

        def _forward(x, w_r, w_k, w_v, w_g, w_o, time_maa_k, time_maa_v, time_maa_r, time_maa_g, time_decay, time_faaaa, ln_g, ln_b):
            Bs, Ts, C = x.shape
            if Ts % 64 == 0:
                Q = 64
            elif Ts % 128 == 0:
                Q = 128
            else:
                Q = Ts
            nC = Ts // Q
            xs = jnp.pad(x, ((0, 0), (1, 0), (0, 0)))[:, :-1]
            xx = xs - x
            xk = x + xx * time_maa_k
            xv = x + xx * time_maa_v
            xr = x + xx * time_maa_r
            xg = x + xx * time_maa_g
            r = (xr @ w_r.T).reshape(Bs, Ts, H, N).transpose(0, 2, 1, 3)
            k = (xk @ w_k.T).reshape(Bs, Ts, H, N).transpose(0, 2, 3, 1)
            v = (xv @ w_v.T).reshape(Bs, Ts, H, N).transpose(0, 2, 1, 3)
            g = jax.nn.silu(xg @ w_g.T)
            w = jnp.exp(-jnp.exp(time_decay))
            u = time_faaaa
            ws = (w ** Q)[None, :, None, None]
            q = jnp.arange(Q)
            wk = (w[:, None] ** (Q - 1 - q)[None, :])[None, :, None, :]
            wb = (w[:, None] ** q[None, :])[None, :, :, None]
            ii = q[:, None]
            jj = q[None, :]
            e = jnp.maximum(ii - jj - 1, 0)
            Wmat = jnp.where((jj < ii)[None], w[:, None, None] ** e[None], 0.0)
            Wmat = Wmat + jnp.eye(Q, dtype=x.dtype)[None] * u[:, None, None]
            Wmat = Wmat[None]
            rC = r.reshape(Bs, H, nC, Q, N).transpose(2, 0, 1, 3, 4)
            kC = k.reshape(Bs, H, N, nC, Q).transpose(3, 0, 1, 2, 4)
            vC = v.reshape(Bs, H, nC, Q, N).transpose(2, 0, 1, 3, 4)

            def step(state, inp):
                rr, kk, vv = inp
                y = rr @ kk * Wmat @ vv + rr @ state * wb
                state = ws * state + kk * wk @ vv
                return (state, y)
            state0 = jnp.zeros((Bs, H, N, N), x.dtype)
            _, yC = jax.lax.scan(step, state0, (rC, kC, vC))
            y = yC.transpose(1, 2, 0, 3, 4).reshape(Bs, H, Ts, N)
            y = y.transpose(0, 2, 1, 3).reshape(Bs * Ts, H, N)
            mu = y.mean(-1, keepdims=True)
            var = y.var(-1, keepdims=True)
            y = (y - mu) / jnp.sqrt(var + EPS)
            y = y.reshape(Bs, Ts, C) * ln_g + ln_b
            y = y * g
            return y @ w_o.T
        return _forward(x, w_r, w_k, w_v, w_g, w_o, time_maa_k, time_maa_v, time_maa_r, time_maa_g, time_decay, time_faaaa, ln_g, ln_b)

    def _L0_xattn_ref(text_embeddings, dinov2_features, W_d2v, b_d2v, W_img, b_img, W_txt, b_txt, W_att0, b_att0, W_att1, b_att1, W_f1, b_f1, W_f2, b_f2):
        import jax, jax.numpy as jnp
        import numpy as np
        import math
        E = 256
        EV = 256
        FFN = 1024
        DINO = 192
        B, S, P = (64, 128, 64)

        def bitnet_linear(x, W, b):
            w_scale = jnp.maximum(jnp.mean(jnp.abs(W)), 1e-05)
            qW = jnp.sign(W) * (jnp.abs(W) > 0.5 * w_scale).astype(W.dtype)
            i_scale = jnp.maximum(jnp.max(jnp.abs(x)), 1e-08) / 127.0
            qx = jnp.clip(jnp.round(x / i_scale), -128.0, 127.0)
            out = jnp.einsum('...i,oi->...o', qx, qW) * (w_scale * i_scale)
            return out + b
        b, s, e = text_embeddings.shape
        vis = bitnet_linear(dinov2_features, W_d2v, b_d2v)
        image_embeds = bitnet_linear(vis, W_img, b_img)
        fused = bitnet_linear(text_embeddings, W_txt, b_txt)
        inv_sqrt_e = 1.0 / math.sqrt(e)
        for Wa, ba in ((W_att0, b_att0), (W_att1, b_att1)):
            kv = bitnet_linear(image_embeds, Wa, ba)
            k = jnp.concatenate([kv, kv], axis=-1)
            scores = jnp.einsum('bse,bpe->bsp', fused, k) * inv_sqrt_e
            attn = jax.nn.softmax(scores, axis=-1)
            fused = fused + 0.1 * jnp.einsum('bsp,bpe->bse', attn, k)
        avg_img = jnp.mean(image_embeds, axis=1, keepdims=True)
        concatenated = jnp.concatenate([fused, jnp.broadcast_to(avg_img, (b, s, e))], axis=-1)
        h = jax.nn.relu(bitnet_linear(concatenated, W_f1, b_f1))
        return bitnet_linear(h, W_f2, b_f2)

    def _L0_ffn_ref(x, Wg, gamma, beta, W1, b1, W2, b2):
        import jax, jax.numpy as jnp
        import numpy as np
        E, K, D, F = (8, 2, 256, 1024)
        EPS = 1e-06
        B, S = (2, 256)
        orig_shape = x.shape
        xf = x.reshape(-1, orig_shape[-1])
        scores = xf @ Wg
        w, idx = jax.lax.top_k(scores, K)
        w = jax.nn.softmax(w, axis=-1)
        mu = jnp.mean(xf, axis=-1, keepdims=True)
        var = jnp.var(xf, axis=-1, keepdims=True)
        xhat = (xf - mu) * jax.lax.rsqrt(var + EPS)
        normed = xhat[None, :, :] * gamma[:, None, :] + beta[:, None, :]
        h = jax.nn.relu(jnp.einsum('end,edf->enf', normed, W1) + b1[:, None, :])
        out = jnp.einsum('enf,efd->end', h, W2) + b2[:, None, :] + xf[None, :, :]
        cw = jnp.sum(w[..., None] * jax.nn.one_hot(idx, E, dtype=w.dtype), axis=1)
        y = jnp.einsum('ne,end->nd', cw, out)
        return y.reshape(orig_shape)

    def _L1_attn_ref(H, W_qkv, b_qkv, W_proj, b_proj, gamma, beta):
        import jax, jax.numpy as jnp
        import numpy as np
        LN_EPS = 1e-05

        def _phi(x):
            return jax.nn.elu(x) + 1.0
        B, N, D = H.shape
        num_heads = 16
        head_dim = D // num_heads
        residual = H
        qkv = jnp.einsum('bnd,ed->bne', H, W_qkv) + b_qkv
        qkv = qkv.reshape(B, N, 3, num_heads, head_dim).transpose(2, 0, 3, 1, 4)
        q, k, v = (qkv[0], qkv[1], qkv[2])
        q = _phi(q)
        k = _phi(k)
        kv = jnp.einsum('bhnd,bhnv->bhdv', k, v)
        k1 = k.sum(axis=2)
        qkv_out = jnp.einsum('bhnd,bhdv->bhnv', q, kv)
        qk1 = jnp.sum(q * k1[:, :, None, :], axis=-1, keepdims=True)
        out = qkv_out / jnp.clip(qk1, 1e-06, None)
        out = out.reshape(B, N, D)
        out = jnp.einsum('bnd,ed->bne', out, W_proj) + b_proj
        mu = out.mean(axis=-1, keepdims=True)
        var = out.var(axis=-1, keepdims=True)
        out = (out - mu) * jax.lax.rsqrt(var + LN_EPS) * gamma + beta
        return out + residual

    def _L1_xattn_ref(x, y, Wq, bq, Wk, bk, Wv, bv, Wo, bo):
        import jax, jax.numpy as jnp
        import numpy as np
        N_HEADS = 8
        D_EMBED = 256
        D_CROSS = 192
        D_HEAD = D_EMBED // N_HEADS
        B, SQ, _ = x.shape
        q = x @ Wq + bq
        k = y @ Wk + bk
        v = y @ Wv + bv
        q = q.reshape(B, SQ, N_HEADS, D_HEAD).transpose(0, 2, 1, 3)
        k = k.reshape(B, -1, N_HEADS, D_HEAD).transpose(0, 2, 1, 3)
        v = v.reshape(B, -1, N_HEADS, D_HEAD).transpose(0, 2, 1, 3)
        scale = 1.0 / jnp.sqrt(jnp.asarray(D_HEAD, dtype=q.dtype))
        weight = jnp.einsum('bhqd,bhkd->bhqk', q, k) * scale
        weight = jax.nn.softmax(weight, axis=-1)
        out = jnp.einsum('bhqk,bhkd->bhqd', weight, v)
        out = out.transpose(0, 2, 1, 3).reshape(B, SQ, D_EMBED)
        return out @ Wo + bo

    def _L1_ffn_ref(x, wqkv, q_scale, k_scale, wo, ln_g, ln_b, w1, b1, w2, b2):
        import jax, jax.numpy as jnp
        import numpy as np
        DIM = 256
        DEPTH = 2
        HEADS = 8
        DIM_HEAD = 64
        WINDOW = 128
        INNER = HEADS * DIM_HEAD
        HID = int(DIM * 4 * 2 / 3)
        B, N = (2, 2048)
        QK_SCALE = 8.0

        def shift_token(t):
            t1, t2 = jnp.split(t, 2, axis=-1)
            t2 = jnp.pad(t2, ((0, 0), (1, 0), (0, 0)))[:, :-1]
            return jnp.concatenate([t1, t2], axis=-1)

        def l2norm(t):
            return t / jnp.clip(jnp.linalg.norm(t, axis=-1, keepdims=True), 1e-12)

        def rotate_half(x):
            x1, x2 = jnp.split(x, 2, axis=-1)
            return jnp.concatenate([-x2, x1], axis=-1)

        def rotary_xpos(q, k):
            n = q.shape[-2]
            half_idx = jnp.arange(0, DIM_HEAD, 2, dtype=jnp.float32)
            inv_freq = 1.0 / 10000.0 ** (half_idx / DIM_HEAD)
            t = jnp.arange(n, dtype=jnp.float32)
            freqs = t[:, None] * inv_freq[None, :]
            freqs = jnp.concatenate([freqs, freqs], axis=-1)
            base = (half_idx + 0.4 * DIM_HEAD) / (1.4 * DIM_HEAD)
            power = (t - n // 2) / float(WINDOW // 2)
            scale = base[None, :] ** power[:, None]
            scale = jnp.concatenate([scale, scale], axis=-1)
            cos, sin = (jnp.cos(freqs), jnp.sin(freqs))
            q = q * cos * scale + rotate_half(q) * sin * scale
            k = k * cos / scale + rotate_half(k) * sin / scale
            return (q, k)

        def local_attention(q, k, v):
            b, h, n, d = q.shape
            w = n // WINDOW
            bq = q.reshape(b, h, w, WINDOW, d) * QK_SCALE
            bk = k.reshape(b, h, w, WINDOW, d)
            bv = v.reshape(b, h, w, WINDOW, d)

            def look_around(t):
                p = jnp.pad(t, ((0, 0), (0, 0), (1, 0), (0, 0), (0, 0)))
                return jnp.concatenate([p[:, :, :w], p[:, :, 1:]], axis=3)
            bk, bv = (look_around(bk), look_around(bv))
            bt = jnp.arange(n).reshape(w, WINDOW)
            btp = jnp.pad(bt, ((1, 0), (0, 0)), constant_values=-1)
            btk = jnp.concatenate([btp[:w], btp[1:]], axis=1)
            sim = jnp.einsum('bhwid,bhwjd->bhwij', bq, bk)
            i = bt[:, :, None]
            j = btk[:, None, :]
            mask = (i < j) | (i > j + WINDOW) | (j == -1)
            sim = jnp.where(mask, -jnp.finfo(sim.dtype).max, sim)
            attn = jax.nn.softmax(sim, axis=-1)
            out = jnp.einsum('bhwij,bhwjd->bhwid', attn, bv)
            return out.reshape(b, h, n, d)

        def _layer(x, wqkv, qs, ksc, wo, lg, lb, w1, b1, w2, b2):
            b, n, _ = x.shape
            h = shift_token(x)
            qkv = h @ wqkv
            q, k, v = jnp.split(qkv, 3, axis=-1)
            to_heads = lambda t: t.reshape(b, n, HEADS, DIM_HEAD).transpose(0, 2, 1, 3)
            q, k, v = (to_heads(q), to_heads(k), to_heads(v))
            q = l2norm(q) * qs
            k = l2norm(k) * ksc
            q, k = rotary_xpos(q, k)
            o = local_attention(q, k, v)
            o = o.transpose(0, 2, 1, 3).reshape(b, n, INNER)
            x = x + o @ wo
            h = shift_token(x)
            mu = h.mean(-1, keepdims=True)
            var = h.var(-1, keepdims=True)
            h = (h - mu) / jnp.sqrt(var + 1e-05) * lg + lb
            h = h @ w1 + b1
            a, g = jnp.split(h, 2, axis=-1)
            h = a * jax.nn.gelu(g, approximate=False)
            x = x + h @ w2 + b2
            return x
        for l in range(DEPTH):
            x = _layer(x, wqkv[l], q_scale[l], k_scale[l], wo[l], ln_g[l], ln_b[l], w1[l], b1[l], w2[l], b2[l])
        return x
    x = _layernorm(x + _L0_attn_ref(x, L0_attn_w_r, L0_attn_w_k, L0_attn_w_v, L0_attn_w_g, L0_attn_w_o, L0_attn_time_maa_k, L0_attn_time_maa_v, L0_attn_time_maa_r, L0_attn_time_maa_g, L0_attn_time_decay, L0_attn_time_faaaa, L0_attn_ln_g, L0_attn_ln_b), axis=-1)
    x = _layernorm(x + _L0_xattn_ref(x, ctx_768, L0_xattn_W_d2v, L0_xattn_b_d2v, L0_xattn_W_img, L0_xattn_b_img, L0_xattn_W_txt, L0_xattn_b_txt, L0_xattn_W_att0, L0_xattn_b_att0, L0_xattn_W_att1, L0_xattn_b_att1, L0_xattn_W_f1, L0_xattn_b_f1, L0_xattn_W_f2, L0_xattn_b_f2), axis=-1)
    x = _layernorm(x + _L0_ffn_ref(x, L0_ffn_Wg, L0_ffn_gamma, L0_ffn_beta, L0_ffn_W1, L0_ffn_b1, L0_ffn_W2, L0_ffn_b2), axis=-1)
    x = _layernorm(x + _L1_attn_ref(x, L1_attn_W_qkv, L1_attn_b_qkv, L1_attn_W_proj, L1_attn_b_proj, L1_attn_gamma, L1_attn_beta), axis=-1)
    x = _layernorm(x + _L1_xattn_ref(x, ctx_768, L1_xattn_Wq, L1_xattn_bq, L1_xattn_Wk, L1_xattn_bk, L1_xattn_Wv, L1_xattn_bv, L1_xattn_Wo, L1_xattn_bo), axis=-1)
    x = _layernorm(x + _L1_ffn_ref(x, L1_ffn_wqkv, L1_ffn_q_scale, L1_ffn_k_scale, L1_ffn_wo, L1_ffn_ln_g, L1_ffn_ln_b, L1_ffn_w1, L1_ffn_b1, L1_ffn_w2, L1_ffn_b2), axis=-1)
    return x

_drawn_inputs = setup_inputs


def setup_inputs(seed=0):
    import zlib

    import numpy as np

    out = dict(_drawn_inputs(seed))
    spreads = {'L0_attn_ln_g': (1.0, 0.6),
     'L0_attn_ln_b': (0.0, 0.408),
     'L0_xattn_b_d2v': (0.0, 0.1),
     'L0_xattn_b_img': (0.0, 0.1),
     'L0_xattn_b_txt': (0.0, 0.1),
     'L0_xattn_b_att0': (0.0, 0.432),
     'L0_xattn_b_att1': (0.0, 0.468),
     'L0_xattn_b_f1': (0.0, 0.1),
     'L0_xattn_b_f2': (0.0, 0.1),
     'L0_ffn_gamma': (1.0, 0.2),
     'L0_ffn_beta': (0.0, 0.32),
     'L0_ffn_b1': (0.0, 0.302),
     'L0_ffn_b2': (0.0, 0.1),
     'L1_attn_gamma': (1.0, 0.2),
     'L1_attn_beta': (0.0, 0.1),
     'L1_xattn_bq': (0.0, 0.414),
     'L1_xattn_bk': (0.0, 0.8),
     'L1_xattn_bv': (0.0, 0.1),
     'L1_xattn_bo': (0.0, 0.1),
     'L1_ffn_q_scale': (1.0, 0.6),
     'L1_ffn_k_scale': (1.0, 0.6),
     'L1_ffn_ln_g': (1.0, 0.6),
     'L1_ffn_ln_b': (0.0, 0.8),
     'L1_ffn_b1': (0.0, 0.792),
     'L1_ffn_b2': (0.0, 0.1)}
    factors = {'L0_attn_time_maa_g': 2.774,
     'L0_attn_time_faaaa': 4.493,
     'L1_attn_b_qkv': 3.134,
     'L1_attn_b_proj': 3.343}
    for name, (base, spread) in spreads.items():
        noise = np.random.default_rng([zlib.crc32(name.encode()), seed]).standard_normal(out[name].shape)
        drawn = base * np.exp(spread * noise) if base else spread * noise
        out[name] = jnp.asarray(drawn.astype(out[name].dtype))
    for name, factor in factors.items():
        out[name] = (out[name] * factor).astype(out[name].dtype)
    return out
```

```python
from contextlib import ExitStack

import numpy as np
import concourse.bass as bass
from concourse import mybir

F32 = mybir.dt.float32
BF16 = mybir.dt.bfloat16
ALU = mybir.AluOpType
ACT = mybir.ActivationFunctionType
AX = mybir.AxisListType

P = 128
B, T, D = 4, 512, 256
NTOK = B * T
TILES = NTOK // P
TPB = T // P
HALVES = D // P
BANK = 512
S2, DC = 1601, 192
CP = DC // 2
KT = -(-S2 // P)
KLAST = S2 - (KT - 1) * P
ROUND = 12582912.0
NE, FF = 8, 1024
H0, N0 = 16, 16
HX, NX = 8, 32
HL, NL = 8, 64
INNER = HL * NL
HID = int(D * 4 * 2 / 3)
HT = -(-HID // P)
HLAST = HID - (HT - 1) * P
MASKED = -1e30


COLS = [("maa_k", 2), ("maa_v", 2), ("maa_r", 2), ("maa_g", 2), ("decay", 2),
        ("b_d2v", 2), ("b_img", 2), ("b_txt", 2), ("b_att0", 1), ("b_att1", 1), ("b_f1", 8),
        ("moe_gamma", 16), ("moe_beta", 16), ("moe_b1", 64), ("la_bq", 2), ("xa_bq", 2), ("xa_bk", 2),
        ("lg", 4), ("lb", 4), ("b1a", 2 * HT), ("b1g", 2 * HT)]
ROWS = [("decay", H0), ("faaaa", H0), ("ln_g", D), ("ln_b", D), ("b_att0", P), ("b_att1", P),
        ("b_f2", D), ("la_bkv", 2 * D), ("la_bproj", D), ("la_gamma", D), ("la_beta", D),
        ("xa_bv", D), ("xa_bo", D), ("q_scale", 2 * NL), ("k_scale", 2 * NL), ("b2", 2 * D)]
CONSTS = [("ident", P), ("expo", P), ("later", P), ("diag16", P), ("ramp", P), ("head16", 8),
          ("head32", 4), ("left", 1), ("ones", P), ("lower", 64), ("half64", 2)]


def offsets(items):
    at, n = {}, 0
    for name, width in items:
        at[name] = (n, width)
        n += width
    return at, n


COL_AT, NCOL = offsets(COLS)
ROW_AT, NROW = offsets(ROWS)
CONST_AT, NCONST = offsets(CONSTS)


def shape_constants():
    c = np.zeros((P, NCONST), np.float32)

    def put(name, a):
        o, w = CONST_AT[name]
        c[:, o:o + w] = a

    j, t = np.arange(P)[:, None], np.arange(P)[None, :]
    put("ident", j == t)
    put("expo", np.maximum(t - j - 1, 0))
    put("later", t > j)
    put("diag16", j // N0 == t // N0)
    put("ramp", t + 0 * j)
    put("head16", j // N0 == np.arange(8)[None, :])
    put("head32", j // NX == np.arange(4)[None, :])
    put("left", P - 1 - j)
    put("ones", 1.0)
    e = np.arange(NE)
    put("lower", np.tile((e[None, :] < e[:, None]).astype(np.float32).reshape(1, 64), (P, 1)))
    put("half64", j // NL == np.arange(2)[None, :])
    return c


def rotary_tables():
    f32 = np.float32
    half = np.arange(0, NL, 2, dtype=f32)
    inv = (f32(1.0) / f32(10000.0) ** (half / f32(NL))).astype(f32)
    t = np.arange(T, dtype=f32)
    fr = (t[:, None] * inv[None, :]).astype(f32)
    fr = np.concatenate([fr, fr], -1)
    base = ((half + f32(0.4 * NL)) / f32(1.4 * NL)).astype(f32)
    power = ((t - T // 2) / f32(P // 2)).astype(f32)
    sc = (base[None, :] ** power[:, None]).astype(f32)
    sc = np.concatenate([sc, sc], -1)
    sign = np.where(np.arange(NL) < NL // 2, -1.0, 1.0).astype(f32)
    cos, sin = np.cos(fr).astype(f32), np.sin(fr).astype(f32) * sign
    tab = np.stack([cos * sc, sin * sc, cos / sc, sin / sc], 1).astype(f32)
    return np.ascontiguousarray(tab.reshape(TPB, P, 4, NL).transpose(1, 0, 2, 3))


def window_mask():
    i, j = np.arange(P)[:, None], np.arange(2 * P)[None, :]
    return np.where((j >= i) & (j <= i + P), 0.0, MASKED).astype(np.float32)


class Queue:

    def __init__(self, engine, sem):
        self.engine, self.sem, self.count, self.seen = engine, sem, 0, {}

    def after(self, *tokens):
        need = {}
        for token in tokens:
            if token is not None:
                need[token[0]] = max(need.get(token[0], 0), token[1])
        for sem, value in need.items():
            if self.seen.get(sem, 0) < value:
                self.engine.wait_ge(sem, value)
                self.seen[sem] = value
        return self.engine

    def mark(self, instruction):
        instruction.then_inc(self.sem, 1)
        self.count += 1
        return self.sem, self.count

    def last(self):
        return (self.sem, self.count) if self.count else None


class Ring:

    def __init__(self, slots):
        self.slots = slots
        self.idle = [(i, ()) for i in range(len(slots))]
        self.readers = [()] * len(slots)

    def take(self, queue):
        i, tokens = self.idle.pop(0)
        self.readers[i] = tokens
        queue.after(*tokens)
        return i, self.slots[i]

    def release(self, i, *tokens):
        self.idle.append((i, tokens))


class Core:
    def __init__(self, nc, dram):
        self.nc, self.dram = nc, dram
        self.ctx = ExitStack()
        self.nsem = 0
        self.pe = Queue(nc.tensor, self.sem("pe_done"))
        self.dve = Queue(nc.vector, self.sem("dve_done"))
        self.act = Queue(nc.scalar, self.sem("act_done"))
        self.pool = Queue(nc.gpsimd, self.sem("pool_done"))
        self.sp = Queue(nc.sync, self.sem("sp_done"))
        self.loads = []
        self.tensors = 0

    def sem(self, name):
        self.nsem += 1
        return self.ctx.enter_context(self.nc.semaphore(name))

    def sb(self, ctx, name, shape, dt=F32):
        return ctx.enter_context(self.nc.sbuf_tensor(name, list(shape), dt))

    def load(self, name, *pairs, after=()):
        sem = self.sem("loaded_" + name)
        self.sp.after(*after)
        for dst, src in pairs:
            self.nc.sync.dma_start(dst, src).then_inc(sem, 16)
        token = (sem, 16 * len(pairs))
        self.loads.append(token)
        return token

    def barrier(self):
        every = [q.last() for q in (self.pe, self.dve, self.act, self.pool)] + self.loads
        self.loads = []
        for q in (self.pe, self.dve, self.act, self.pool, self.sp):
            q.after(*every)

    def matmuls(self, out, pairs, *after, first=True, last=True, skip=False):
        eng = self.pe.after(*after)
        for n, (lhsT, rhs) in enumerate(pairs):
            ins = eng.matmul(out, lhsT, rhs, start=first and n == 0, stop=last and n == len(pairs) - 1,
                             skip_group_check=skip)
        return self.pe.mark(ins)


def setup(k):
    nc, ctx = k.nc, k.ctx
    k.psum = ctx.enter_context(nc.psum_tensor("psum", [P, 8, BANK], F32))
    k.x_tok = k.sb(ctx, "x_tok", [P, TILES, D])
    k.x_ch = k.sb(ctx, "x_ch", [P, HALVES, NTOK])
    k.const = k.sb(ctx, "const", [P, NCONST])
    k.cols = k.sb(ctx, "cols", [P, NCOL])
    k.rows = k.sb(ctx, "rows", [P, NROW])
    k.stats = k.sb(ctx, "ln_stats", [P, TILES, 6])
    k.mv = k.sb(ctx, "ln_mean_var", [P, TILES, 2])
    k.std = k.sb(ctx, "ln_std", [P, TILES])
    k.rstd = k.sb(ctx, "ln_rstd", [P, TILES])
    k.eps = k.sb(ctx, "eps", [P, 4])
    k.banks = Ring([k.psum[:, 4 + n, :] for n in range(4)])
    k.score_free = ()
    for n, v in enumerate((1e-5, 1e-6, 64e-5, 0.0)):
        t = k.dve.mark(nc.vector.memset(k.eps[:, n:n + 1], v))
    k.t_eps = t
    k.t_param = k.load("params", (k.const[:], k.dram["const"]), (k.cols[:], k.dram["cols"]),
                       (k.rows[:], k.dram["rows"].partition_broadcast(P)))
    k.t_x = t_x = k.load("x", (k.x_tok[:], k.dram["x"].rearrange("(n p) d -> p n d", p=P)),
                   (k.x_ch[:], k.dram["xT"].rearrange("(h p) t -> p h t", p=P)))
    k.tok, k.ch = {i: t_x for i in range(TILES)}, {g: [t_x] for g in range(4)}


def const(k, name, rows=P):
    o, w = CONST_AT[name]
    return k.const[0:rows, o:o + w]


def col(k, name, n=0, rows=P):
    o, _ = COL_AT[name]
    return k.cols[0:rows, o + n:o + n + 1]


def row(k, name, a=0, b=None):
    o, w = ROW_AT[name]
    return k.rows[:, o + a:o + (w if b is None else b)]


def evacuate(k, n, out, bank, *after):
    if n % 2:
        return k.dve.mark(k.dve.after(*after).tensor_copy(out, bank))
    return k.act.mark(k.act.after(*after).copy(out, bank))


def layer_norm(k, src, dst, ready, eps_col, tiles=range(TILES)):
    done = {}
    tiles = list(tiles)
    for g in range(0, len(tiles), 4):
        group = tiles[g:g + 4]
        a, b = group[0], group[-1] + 1
        for i in group:
            t = k.dve.mark(k.dve.after(ready[i]).bn_stats(k.stats[:, i, :], src[:, i, :]))
        k.dve.after(t)
        for i in group:
            t = k.dve.mark(k.nc.vector.bn_aggr(k.mv[:, i, :], k.stats[:, i, :]))
        t = k.act.mark(k.act.after(t, k.t_eps, k.t_param).activation(
            k.std[:, a:b], k.mv[:, a:b, 1], ACT.Sqrt, bias=k.eps[:, eps_col:eps_col + 1]))
        t = k.dve.mark(k.dve.after(t).reciprocal(k.rstd[:, a:b], k.std[:, a:b]))
        k.dve.after(t)
        for i in group:
            done[i] = k.dve.mark(k.nc.vector.tensor_scalar(
                dst[:, i, :], src[:, i, :], k.mv[:, i, 0:1], k.rstd[:, i:i + 1],
                ALU.subtract, ALU.mult))
    return done


def to_channels(k, src, dst, ready, scale=None, bias=None, free=(), groups=range(4)):
    done = {}
    for g in groups:
        tokens = []
        for h in range(HALVES):
            i, bank = k.banks.take(k.pe)
            k.pe.after(k.t_param, *[ready[4 * g + m] for m in range(4)])
            for m in range(4):
                ins = k.nc.tensor.transpose(bank[:, m * P:(m + 1) * P],
                                            src[:, 4 * g + m, h * P:(h + 1) * P], const(k, "ident"))
            t = k.pe.mark(ins)
            out = dst[:, h, g * BANK:(g + 1) * BANK]
            if scale is None:
                t = evacuate(k, h, out, bank, t, *free)
            else:
                t = k.act.mark(k.act.after(t, *free).activation(out, bank, ACT.Identity,
                                                                scale=scale(h), bias=bias(h)))
            k.banks.release(i, t)
            tokens.append(t)
        done[g] = tokens
    return done


def post_norm(k, ready):
    k.tok = layer_norm(k, k.x_tok, k.x_tok, ready, 0)
    k.ch = to_channels(k, k.x_tok, k.x_ch, k.tok)


def rwkv(k):
    nc = k.nc
    with ExitStack() as ctx:
        sb = lambda name, shape, dt=F32: k.sb(ctx, name, shape, dt)
        w = {n: sb("w_" + n, [P, HALVES, D]) for n in "rkvgo"}
        t_w = k.load("rwkv_w", *[(w[n][:], k.dram["w_%sT" % n].rearrange("(h p) o -> p h o", p=P)) for n in "rkvgo"])
        rate_row, rate_col = sb("rate_row", [P, H0]), sb("rate_col", [P, 2])
        nrate_row, nrate_col = sb("nrate_row", [P, H0]), sb("nrate_col", [P, 2])
        wmat = sb("decay_mask", [P, H0, P])
        wkey = sb("key_decay", [P, H0])
        wquery = sb("query_decay", [P, 2, P])
        wstate = sb("state_decay", [P, 2])
        xx = sb("x_step", [P, HALVES, NTOK])

        A, V = k.act, k.dve
        t = A.mark(A.after(k.t_param).activation(rate_row[:], row(k, "decay"), ACT.Exp))
        o, _ = COL_AT["decay"]
        t = A.mark(nc.scalar.activation(rate_col[:], k.cols[:, o:o + 2], ACT.Exp))
        V.after(t)
        V.mark(nc.vector.tensor_scalar(nrate_row[:], rate_row[:], -1.0, None, ALU.mult))
        t = V.mark(nc.vector.tensor_scalar(nrate_col[:], rate_col[:], -1.0, None, ALU.mult))
        A.after(t)
        for h in range(H0):
            t = A.mark(nc.scalar.activation(wmat[:, h, :], const(k, "expo"), ACT.Exp,
                                            scale=nrate_row[:, h:h + 1]))
        for c in range(2):
            A.mark(nc.scalar.activation(wquery[:, c, :], const(k, "ramp"), ACT.Exp, scale=nrate_col[:, c:c + 1]))
        A.mark(nc.scalar.activation(wstate[:], nrate_col[:], ACT.Exp, scale=float(P)))
        t2 = A.mark(nc.scalar.activation(wkey[:], nrate_row[:], ACT.Exp, scale=const(k, "left")))
        t = V.mark(V.after(t).tensor_tensor(wmat[:], wmat[:], const(k, "later").unsqueeze(1).to_broadcast([P, H0, P]), ALU.mult))
        V.after(t)
        for h in range(H0):
            t = V.mark(nc.vector.scalar_tensor_tensor(wmat[:, h, :], const(k, "ident"), row(k, "faaaa", h, h + 1),
                                                      wmat[:, h, :], ALU.mult, ALU.add))
        t_tab = (t, t2)

        V.after(k.t_x)
        xv = k.x_ch[:].rearrange("p h (b t) -> p (h b) t", t=T)
        xxv = xx[:].rearrange("p h (b t) -> p (h b) t", t=T)
        V.mark(nc.vector.tensor_tensor(xxv[:, :, 1:T], xv[:, :, 0:T - 1], xv[:, :, 1:T], ALU.subtract))
        t_xx = V.mark(nc.vector.tensor_scalar(xxv[:, :, 0:1], xv[:, :, 0:1], -1.0, None, ALU.mult))

        mixes = Ring([sb("mix%d" % n, [P, HALVES, T]) for n in range(3)])
        two = lambda name, shape: Ring([sb("%s%d" % (name, n), shape) for n in range(2)])
        r_heads = two("r_heads", [P, 8, BANK])
        r_state = two("r_state", [P, HALVES, T])
        r_ch, k_ch = two("r_ch", [P, HALVES, T]), two("k_ch", [P, HALVES, T])
        k_tok, v_tok, gate, y_all = (two(n, [P, TPB, D]) for n in ("k_tok", "v_tok", "gate", "y_all"))
        scores = two("a_masked", [P, 4, P])
        state = [sb("state%d" % n, [P, HALVES, P]) for n in range(2)]
        outer = sb("outer", [P, HALVES, P])
        z_ch = two("z_ch", [P, HALVES, T])
        gsum, gvar = two("g_sum", [P, TPB * H0]), two("g_var", [P, TPB * H0])
        zsq = sb("z_sq", [P, TPB * D])
        t_zsq = None
        ready = {}

        for b in range(B):
            cols_b = slice(b * T, (b + 1) * T)

            def mix(name):
                i, m = mixes.take(V)
                V.after(t_xx)
                for c in range(HALVES):
                    t = V.mark(nc.vector.scalar_tensor_tensor(m[:, c, :], xx[:, c, cols_b], col(k, "maa_" + name, c),
                                                              k.x_ch[:, c, cols_b], ALU.mult, ALU.add))
                return i, m, t

            def project_channels(m, t_m, weight, ring):
                j, out = ring.take(A)
                V.after(*ring.readers[j])
                for c in range(HALVES):
                    i, bank = k.banks.take(k.pe)
                    t = k.matmuls(bank, [(weight[:, h, c * P:(c + 1) * P], m[:, h, :]) for h in range(HALVES)], t_m, t_w)
                    t = A.mark(A.after(t).copy(out[:, c, :], bank))
                    k.banks.release(i, t)
                return j, out, t

            def project_tokens(m, t_m, weight, finish):
                for pair in range(TPB // 2):
                    i, bank = k.banks.take(k.pe)
                    k.pe.after(t_m, t_w)
                    for s in range(2):
                        tl = 2 * pair + s
                        for h in range(HALVES):
                            ins = nc.tensor.matmul(bank[:, s * D:(s + 1) * D], m[:, h, tl * P:(tl + 1) * P],
                                                   weight[:, h, :], start=(h == 0), stop=(h == HALVES - 1))
                    t = k.pe.mark(ins)
                    t = finish(pair, bank, t)
                    k.banks.release(i, t)
                return t

            im, m, t_m = mix("r")
            jr, rc, t_r = project_channels(m, t_m, w["r"], r_ch)
            mixes.release(im, t_r)
            jrs, rs = r_state.take(V)
            V.after(t_r, *t_tab)
            for c in range(HALVES):
                t_rs = V.mark(nc.vector.tensor_tensor(
                    rs[:, c, :].rearrange("p (n t) -> p n t", t=P), rc[:, c, :].rearrange("p (n t) -> p n t", t=P),
                    wquery[:, c, :].unsqueeze(1).to_broadcast([P, TPB, P]), ALU.mult))
            im, m, t_m = mix("k")
            jk, kc, t_k = project_channels(m, t_m, w["k"], k_ch)
            jkt, kt = k_tok.take(V)

            def finish_k(pair, bank, t):
                wk = wkey[:].unsqueeze(1).unsqueeze(3).to_broadcast([P, 2, H0, N0])
                return V.mark(V.after(t, *t_tab).tensor_tensor(
                    kt[:, 2 * pair:2 * pair + 2, :].rearrange("p s (h n) -> p s h n", n=N0),
                    bank.rearrange("p (s h n) -> p s h n", s=2, n=N0), wk, ALU.mult))
            t_kt = project_tokens(m, t_m, w["k"], finish_k)
            mixes.release(im, t_kt)
            im, m, t_m = mix("v")
            jv, vt = v_tok.take(A)
            t_v = project_tokens(m, t_m, w["v"], lambda pair, bank, t: A.mark(
                A.after(t).copy(vt[:, 2 * pair:2 * pair + 2, :].rearrange("p s d -> p (s d)"), bank)))
            mixes.release(im, t_v)
            im, m, t_m = mix("g")
            jg, gt = gate.take(A)
            t_g = project_tokens(m, t_m, w["g"], lambda pair, bank, t: A.mark(
                A.after(t).activation(gt[:, 2 * pair:2 * pair + 2, :].rearrange("p s d -> p (s d)"), bank, ACT.Silu)))
            mixes.release(im, t_g)

            jy, ya = y_all.take(A)
            V.after(*y_all.readers[jy])
            t = V.mark(V.after(k.pe.last()).memset(state[0][:], 0.0))
            t_state = t
            heads = []
            for c in range(HALVES):
                jh, rh = r_heads.take(k.pool)
                k.pool.after(t_r)
                t_h = k.pool.mark(nc.gpsimd.tensor_tensor(
                    rh[:], rc[:, c, :].unsqueeze(1).to_broadcast([P, 8, BANK]),
                    const(k, "head16").unsqueeze(2).to_broadcast([P, 8, BANK]), ALU.mult))
                heads.append((jh, rh, t_h))
            r_ch.release(jr, t_rs, t_h)
            for c in range(TPB):
                tl = slice(c * P, (c + 1) * P)
                old, new = state[c % 2], state[(c + 1) % 2]
                iy, ybank = k.banks.take(k.pe)
                k.pe.after(t_state, t_rs)
                for h in range(HALVES):
                    nc.tensor.matmul(ybank[:, h * P:(h + 1) * P], rs[:, h, tl], old[:, h, :],
                                     start=(h == 0), stop=False, skip_group_check=True)
                for q in range(4):
                    h = q // 2
                    i, bank = k.banks.take(k.pe)
                    t = k.matmuls(bank, [(kc[:, h, tl], heads[h][1][:, 4 * (q % 2):4 * (q % 2) + 4, tl])],
                                  t_k, heads[h][2])
                    ia, am = scores.take(V)
                    t = V.mark(V.after(t, *t_tab).tensor_tensor(am[:], bank.rearrange("p (a t) -> p a t", t=P),
                                                                wmat[:, 4 * q:4 * q + 4, :], ALU.mult))
                    k.banks.release(i, t)
                    k.pe.after(t, t_v)
                    for a in range(4):
                        hd = 4 * q + a
                        ins = nc.tensor.matmul(ybank[:, hd * N0:(hd + 1) * N0], am[:, a, :],
                                               vt[:, c, hd * N0:(hd + 1) * N0], start=False, stop=False,
                                               skip_group_check=True)
                    t_y = k.pe.mark(ins)
                    scores.release(ia, t_y)
                t = A.mark(A.after(t_y).copy(ya[:, c, :], ybank[:, 0:D]))
                k.banks.release(iy, t)
                t_ya = t
                if c < TPB - 1:
                    i, bank = k.banks.take(k.pe)
                    k.pe.after(t_kt, t_v)
                    for h in range(HALVES):
                        hs = slice(h * P, (h + 1) * P)
                        ins = nc.tensor.matmul(bank[:, hs], kt[:, c, hs], vt[:, c, hs], start=True, stop=True)
                    t = k.pe.mark(ins)
                    t = V.mark(V.after(t).tensor_tensor(outer[:], bank[:, 0:D].rearrange("p (h v) -> p h v", v=P),
                                                        const(k, "diag16").unsqueeze(1).to_broadcast([P, 2, P]), ALU.mult))
                    k.banks.release(i, t)
                    V.after(t)
                    for h in range(HALVES):
                        t_state = V.mark(nc.vector.scalar_tensor_tensor(new[:, h, :], old[:, h, :], wstate[:, h:h + 1],
                                                                        outer[:, h, :], ALU.mult, ALU.add))
            last_y = k.pe.last()
            r_state.release(jrs, last_y)
            k_ch.release(jk, last_y)
            k_tok.release(jkt, last_y)
            v_tok.release(jv, last_y)
            for jh, _, _ in heads:
                r_heads.release(jh, last_y)

            G = TPB * H0
            ig, gs = gsum.take(V)
            iv, gv = gvar.take(V)
            yg = ya[:].rearrange("p n (h c) -> p (n h) c", c=N0)
            sq = zsq[:].rearrange("p (g c) -> p g c", c=N0)
            wide = lambda a: a[:].unsqueeze(2).to_broadcast([P, G, N0])
            t = V.mark(V.after(t_ya).tensor_reduce(gs[:], yg, AX.X, ALU.add))
            t = V.mark(V.after(t).tensor_scalar(gs[:], gs[:], 1.0 / N0, None, ALU.mult))
            t = V.mark(V.after(t).tensor_tensor(yg, yg, wide(gs), ALU.subtract))
            t = V.mark(V.after(t).tensor_tensor(sq, yg, yg, ALU.mult))
            t = V.mark(V.after(t).tensor_reduce(gv[:], sq, AX.X, ALU.add))
            t = A.mark(A.after(t, k.t_eps).activation(gv[:], gv[:], ACT.Sqrt, scale=1.0 / N0, bias=k.eps[:, 2:3]))
            t = V.mark(V.after(t).reciprocal(gs[:], gv[:]))
            t = V.mark(V.after(t).tensor_tensor(yg, yg, wide(gs), ALU.mult))
            gsum.release(ig, t)
            gvar.release(iv, t)
            over = lambda name: row(k, name).unsqueeze(1).to_broadcast([P, TPB, D])
            t = k.pool.mark(k.pool.after(t).tensor_tensor(ya[:], ya[:], over("ln_g"), ALU.mult))
            t = k.pool.mark(k.pool.after(t).tensor_tensor(ya[:], ya[:], over("ln_b"), ALU.add))
            t = k.pool.mark(k.pool.after(t, t_g).tensor_tensor(ya[:], ya[:], gt[:], ALU.mult))
            gate.release(jg, t)
            t_z = t
            jz, zc = z_ch.take(k.act)
            V.after(*z_ch.readers[jz])
            for h in range(HALVES):
                i, bank = k.banks.take(k.pe)
                k.pe.after(t_z)
                for n in range(TPB):
                    ins = nc.tensor.transpose(bank[:, n * P:(n + 1) * P], ya[:, n, h * P:(h + 1) * P], const(k, "ident"))
                t = k.pe.mark(ins)
                t = A.mark(A.after(t).copy(zc[:, h, :], bank))
                k.banks.release(i, t)
            y_all.release(jy, t)
            t_zc = t
            for n in range(TPB):
                i, bank = k.banks.take(k.pe)
                t = k.matmuls(bank[:, 0:D], [(zc[:, h, n * P:(n + 1) * P], w["o"][:, h, :]) for h in range(HALVES)], t_zc)
                tile = b * TPB + n
                t = V.mark(V.after(t, k.t_x).tensor_tensor(k.x_tok[:, tile, :], bank[:, 0:D], k.x_tok[:, tile, :], ALU.add))
                k.banks.release(i, t)
                ready[tile] = t
            z_ch.release(jz, k.pe.last())
        k.barrier()
        post_norm(k, ready)
        k.barrier()


def attention(k, ctx, tag, items, scale, dv):
    nc, V, A = k.nc, k.dve, k.act
    probs = Ring([k.sb(ctx, "probs%d_%s" % (n, tag), [P, S2]) for n in range(2)])
    turned = Ring([k.sb(ctx, "probs_t%d_%s" % (n, tag), [P, KT, P]) for n in range(2)])
    small = [k.sb(ctx, "softmax%d_%s" % (n, tag), [P, len(items)]) for n in range(4)]
    maxes, nmax, sums, rsums = small
    scores = k.psum[:, 0:4, :].rearrange("p b c -> p (b c)")

    def front(n, it):
        k.pe.after(*k.score_free, *it["ready"])
        for c0 in range(0, S2, BANK):
            c1 = min(c0 + BANK, S2)
            ins = nc.tensor.matmul(scores[:, c0:c1], it["query"], it["keys"](c0, c1), start=True, stop=True)
        t = k.pe.mark(ins)
        if it.get("scored"):
            it["scored"](t)
        m = slice(n, n + 1)
        t = V.mark(V.after(t).tensor_reduce(maxes[:, m], scores[:, 0:S2], AX.X, ALU.max))
        t = V.mark(V.after(t).tensor_scalar(nmax[:, m], maxes[:, m], -scale, None, ALU.mult))
        ip, pr = probs.take(A)
        t = A.mark(A.after(t).activation(pr[:], scores[:, 0:S2], ACT.Exp, bias=nmax[:, m], scale=scale,
                                         accum_out=sums[:, m]))
        k.score_free = (t,)
        t_r = V.mark(V.after(t).reciprocal(rsums[:, m], sums[:, m]))
        return ip, pr, t, t_r

    def back(n, it, ip, pr, t_exp, t_rsum):
        io, obank = k.banks.take(k.pe)
        it_, pt = turned.take(A)
        V.after(*turned.readers[it_])
        k.pe.after(t_exp)
        copied = {}

        def turn(g):
            i, bank = k.banks.take(k.pe)
            tiles = range(4 * g, min(4 * g + 4, KT))
            for kt in tiles:
                rows = P if kt < KT - 1 else KLAST
                ins = nc.tensor.transpose(bank[0:rows, (kt % 4) * P:(kt % 4 + 1) * P],
                                          pr[:, kt * P:kt * P + rows], const(k, "ident"))
            t = k.pe.mark(ins)
            rows, cnt = (P, 4) if len(tiles) == 4 else (KLAST, 1)
            t = evacuate(k, g % 2, pt[0:rows, 4 * g:4 * g + cnt, :].rearrange("p a q -> p (a q)"),
                         bank[0:rows, 0:cnt * P], t)
            k.banks.release(i, t)
            copied[g] = t

        def product(g):
            k.pe.after(copied[g])
            for kt in range(4 * g, min(4 * g + 4, KT)):
                rows = P if kt < KT - 1 else KLAST
                ins = nc.tensor.matmul(obank[:, 0:dv], pt[0:rows, kt, :], it["value"](kt, rows),
                                       start=(kt == 0), stop=(kt == KT - 1))
            return ins

        turn(0)
        turn(1)
        turn(2)
        product(0)
        turn(3)
        probs.release(ip, k.pe.last())
        product(1)
        product(2)
        t = k.pe.mark(product(3))
        turned.release(it_, t)
        it["finish"](obank, io, rsums[:, n:n + 1], (t, t_rsum))

    prev = None
    for n, it in enumerate(items):
        now = (n, it) + front(n, it)
        if prev:
            back(*prev)
        prev = now
    back(*prev)


def bitnet(k):
    nc, V, A = k.nc, k.dve, k.act
    KEYS = B * S2
    CH = [(c, min(c + BANK, KEYS)) for c in range(0, KEYS, BANK)]
    WID = {"d2v": 0, "img": 1, "txt": 2, "att0": 3, "att1": 4, "f1": 5, "f2": 6}
    with ExitStack() as outer:
        wsum = k.sb(outer, "w_abs_sum", [P, 8])
        wscale, wthr, wnthr = (k.sb(outer, n, [P, 8]) for n in ("w_scale", "w_thr", "w_nthr"))
        mcols = k.sb(outer, "max_cols", [P, 40])
        mrow, mone = k.sb(outer, "max_row", [1, P]), k.sb(outer, "max_one", [1, 1])
        iscale, inv, s_out = (k.sb(outer, n, [P, 12]) for n in ("i_scale", "i_inv", "out_scale"))
        fused = k.sb(outer, "fused", [P, HALVES, NTOK])
        avg = k.sb(outer, "avg_img", [P, HALVES * B])
        t_zero = V.mark(nc.vector.memset(wsum[:], 0.0))
        t_zero = V.mark(nc.vector.memset(mcols[:], 0.0))

        def ternary(ctx, names, shapes, space=None):
            q = {}
            tmp = k.sb(ctx, "tern_tmp_" + names[0], [P, max(c * o for _, c, o in shapes)], BF16)
            raw, at = {}, 0
            for n, (_, c, o) in zip(names, shapes):
                if space is None:
                    raw[n] = k.sb(ctx, "bn_raw_" + n, [P, c, o])
                else:
                    raw[n] = space[:, at:at + c * o].rearrange("p (c o) -> p c o", o=o)
                at += c * o
            t_l = k.load("bn_" + names[0], *[
                (raw[n][0:p], k.dram["bn_" + n].rearrange("(c p) o -> p c o", p=p)) for n, (p, c, o) in zip(names, shapes)])
            V.after(t_l, t_zero)
            for n, (p, c, o) in zip(names, shapes):
                j = WID[n]
                t = V.mark(nc.vector.tensor_reduce(wsum[0:p, j:j + 1], raw[n][0:p], AX.XY, ALU.add,
                                                   apply_absolute_value=True))
            i, bank = k.banks.take(k.pe)
            t = k.matmuls(bank[:, 0:8], [(const(k, "ones"), wsum[:])], t, k.t_param)
            V.after(t)
            for n, (p, c, o) in zip(names, shapes):
                j = slice(WID[n], WID[n] + 1)
                t = V.mark(nc.vector.tensor_scalar(wscale[:, j], bank[:, j], 1.0 / (p * c * o), 1e-5, ALU.mult, ALU.max))
            k.banks.release(i, t)
            V.after(t)
            a, b = WID[names[0]], WID[names[-1]] + 1
            V.mark(nc.vector.tensor_scalar(wthr[:, a:b], wscale[:, a:b], 0.5, None, ALU.mult))
            t = V.mark(nc.vector.tensor_scalar(wnthr[:, a:b], wscale[:, a:b], -0.5, None, ALU.mult))
            for n, (p, c, o) in zip(names, shapes):
                j = slice(WID[n], WID[n] + 1)
                q[n] = k.sb(ctx, "bn_q_" + n, [P, c, o], BF16)
                low = tmp[0:p, 0:c * o].rearrange("p (c o) -> p c o", o=o)
                t = V.mark(V.after(t).tensor_scalar(low, raw[n][0:p], wnthr[0:p, j], None, ALU.is_lt))
                t = V.mark(V.after(t).scalar_tensor_tensor(q[n][0:p], raw[n][0:p], wthr[0:p, j], low,
                                                           ALU.is_gt, ALU.subtract))
            return q, t

        def input_scale(slot, ncol, *ready):
            s = slice(slot, slot + 1)
            t = V.mark(V.after(*ready).tensor_reduce(mcols[:, 39:40], mcols[:, 0:ncol], AX.X, ALU.max))
            i, bank = k.banks.take(k.pe)
            t = k.pe.mark(k.pe.after(t).transpose(bank[0:1, 0:P], mcols[:, 39:40], const(k, "ident")))
            t = V.mark(V.after(t).tensor_reduce(mone[:], bank[0:1, 0:P], AX.X, ALU.max))
            k.banks.release(i, t)
            i, bank = k.banks.take(k.pe)
            t = k.matmuls(bank[:, 0:1], [(const(k, "ones", 1), mone[:])], t)
            t = V.mark(V.after(t).tensor_scalar(iscale[:, s], bank[:, 0:1], 1e-8, 1.0 / 127.0, ALU.max, ALU.mult))
            k.banks.release(i, t)
            return V.mark(V.after(t).reciprocal(inv[:, s], iscale[:, s]))

        def out_scale(slot, wname, use, *ready):
            t = V.mark(V.after(*ready).tensor_tensor(s_out[:, use:use + 1], iscale[:, slot:slot + 1],
                                                     wscale[:, WID[wname]:WID[wname] + 1], ALU.mult))
            return t

        def quantize(slot, dst, src, rows, *ready):
            s = slice(slot, slot + 1)
            t = V.mark(V.after(*ready).tensor_scalar(src, src, inv[0:rows, s], ROUND, ALU.mult, ALU.add))
            return V.mark(V.after(t).tensor_scalar(dst, src, ROUND, None, ALU.subtract))

        with ExitStack() as ctx:
            big = k.sb(ctx, "ctx_f32", [P, KEYS + B * KT * P])
            q8 = k.sb(ctx, "ctx_q8", [P, HALVES, KEYS], BF16)
            wide = big[:, 0:HALVES * KEYS].rearrange("p (h s) -> p h s", h=HALVES)
            t_ctx = [k.load("ctx%d" % h, (wide[0:CP, h, :], k.dram["ctxT"].rearrange("c b s -> c (b s)")[h * CP:(h + 1) * CP, :]))
                     for h in range(HALVES)]
            q, t_q = ternary(ctx, ["d2v", "img", "txt", "att0", "att1"],
                             [(CP, 2, D), (P, 2, D), (P, 2, D), (P, 2, P), (P, 2, P)])

            for h in range(HALVES):
                t = V.mark(V.after(t_ctx[h], t_zero).tensor_reduce(mcols[0:CP, h:h + 1], wide[0:CP, h, :], AX.X, ALU.max,
                                                           apply_absolute_value=True))
            t_s = input_scale(0, 2, t)
            t_s = out_scale(0, "d2v", 0, t_s)
            V.after(t_s)
            ready = [quantize(0, q8[0:CP, h, :], wide[0:CP, h, :], CP) for h in range(HALVES)]

            def dense(wname, rows, use, bname, ready, n_max):
                n = 0
                for c0, c1 in CH:
                    for o in range(HALVES):
                        i, bank = k.banks.take(k.pe)
                        bank = bank[:, 0:c1 - c0]
                        t = k.matmuls(bank, [(q[wname][0:rows, h, o * P:(o + 1) * P], q8[0:rows, h, c0:c1])
                                             for h in range(HALVES)], *ready)
                        t = A.mark(A.after(t, *ready).activation(wide[:, o, c0:c1], bank, ACT.Identity,
                                                                 scale=s_out[:, use:use + 1], bias=col(k, bname, o)))
                        k.banks.release(i, t)
                        t = V.mark(V.after(t).tensor_reduce(mcols[:, n:n + 1], wide[:, o, c0:c1], AX.X, ALU.max,
                                                            apply_absolute_value=True))
                        n += 1
                return n, t

            n, t = dense("d2v", CP, 0, "b_d2v", (ready[0], ready[1], t_q, t_s), 0)
            t = input_scale(1, n, t)
            t_s = out_scale(1, "img", 1, t)
            V.after(t_s, k.pe.last())
            ready = [quantize(1, q8[:, h, :], wide[:, h, :], P) for h in range(HALVES)]
            n, t = dense("img", P, 1, "b_img", (ready[0], ready[1], t_s), 0)
            t = input_scale(2, n, t)
            out_scale(2, "att0", 2, t)
            t_s = out_scale(2, "att1", 3, t)
            for h in range(HALVES):
                t = V.mark(nc.vector.tensor_reduce(avg[:, h * B:(h + 1) * B],
                                                   wide[:, h, :].rearrange("p (b s) -> p b s", b=B), AX.X, ALU.add))
            t_avg = V.mark(V.after(t).tensor_scalar(avg[:], avg[:], 1.0 / S2, None, ALU.mult))
            V.after(t_s, k.pe.last())
            t_q8 = [quantize(2, q8[:, h, :], wide[:, h, :], P) for h in range(HALVES)]

            with ExitStack() as tctx:
                qx = k.sb(tctx, "text_q8", [P, HALVES, NTOK], BF16)
                t = V.mark(V.after(k.pe.last(), *k.ch[3]).tensor_reduce(mcols[:, 0:1], k.x_ch[:], AX.XY, ALU.max,
                                                                        apply_absolute_value=True))
                t = input_scale(3, 1, t)
                t_s = out_scale(3, "txt", 4, t)
                V.after(t_s)
                t_x = [quantize(3, qx[:, h, :], k.x_ch[:, h, :], P) for h in range(HALVES)]
                t_fused = {}
                for g in range(4):
                    for o in range(HALVES):
                        i, bank = k.banks.take(k.pe)
                        t = k.matmuls(bank, [(q["txt"][:, h, o * P:(o + 1) * P], qx[:, h, g * BANK:(g + 1) * BANK])
                                             for h in range(HALVES)], *t_x)
                        t = A.mark(A.after(t, t_s).activation(fused[:, o, g * BANK:(g + 1) * BANK], bank, ACT.Identity,
                                                              scale=s_out[:, 4:5], bias=col(k, "b_txt", o)))
                        k.banks.release(i, t)
                k.barrier()

            keys = big[:, 0:KEYS]
            values = big[:, KEYS:KEYS + B * KT * P].rearrange("p (b t d) -> p b t d", b=B, t=KT)
            qsum = k.sb(ctx, "query_sum", [P, NTOK])
            o_tok = Ring([k.sb(ctx, "o_tok%d" % n, [P, P]) for n in range(2)])
            for layer in range(2):
                wq, sc = q["att%d" % layer], s_out[:, 2 + layer:3 + layer]
                bcol, brow = col(k, "b_att%d" % layer), row(k, "b_att%d" % layer)
                t_keys = []
                for c0, c1 in CH:
                    i, bank = k.banks.take(k.pe)
                    t = k.matmuls(bank[:, 0:c1 - c0], [(wq[:, h, :], q8[:, h, c0:c1]) for h in range(HALVES)], *t_q8)
                    t = A.mark(A.after(t, *t_q8).activation(keys[:, c0:c1], bank[:, 0:c1 - c0], ACT.Identity, scale=sc, bias=bcol))
                    k.banks.release(i, t)
                    t_keys.append(t)
                for b in range(B):
                    for g in range(0, KT, 4):
                        i, bank = k.banks.take(k.pe)
                        tiles = range(g, min(g + 4, KT))
                        for kt in tiles:
                            rows = P if kt < KT - 1 else KLAST
                            a = b * S2 + kt * P
                            for h in range(HALVES):
                                ins = nc.tensor.matmul(bank[0:rows, (kt - g) * P:(kt - g + 1) * P], q8[:, h, a:a + rows],
                                                       wq[:, h, :], start=(h == 0), stop=(h == 1))
                        t = k.pe.mark(ins)
                        rows, cnt = (P, 4) if len(tiles) == 4 else (KLAST, 1)
                        t_val = V.mark(V.after(t).scalar_tensor_tensor(
                            values[0:rows, b, g:g + cnt, :], bank[0:rows, 0:cnt * P].rearrange("p (a d) -> p a d", d=P),
                            sc[0:rows], brow[0:rows].unsqueeze(1).to_broadcast([rows, cnt, P]), ALU.mult, ALU.add))
                        k.banks.release(i, t_val)
                t_qs = V.mark(V.after(V.last()).tensor_tensor(qsum[:], fused[:, 0, :], fused[:, 1, :], ALU.add))
                items = []

                def item(b, qt):
                    tile = b * TPB + qt
                    cols_q = slice(tile * P, (tile + 1) * P)

                    def finish(obank, io, rsum, after):
                        jo, o = o_tok.take(V)
                        t = V.mark(V.after(*after).tensor_scalar(o[:], obank[:, 0:P], rsum, None, ALU.mult))
                        k.banks.release(io, t)
                        i, bank = k.banks.take(k.pe)
                        t = k.pe.mark(k.pe.after(t).transpose(bank[:, 0:P], o[:], const(k, "ident")))
                        o_tok.release(jo, t)
                        t = V.mark(V.after(t, t_qs).scalar_tensor_tensor(
                            fused[:, :, cols_q], bank[:, 0:P].unsqueeze(1).to_broadcast([P, 2, P]), 0.1,
                            fused[:, :, cols_q], ALU.mult, ALU.add))
                        k.banks.release(i, t)

                    return {"query": qsum[:, cols_q], "keys": lambda c0, c1: keys[:, b * S2 + c0:b * S2 + c1],
                            "value": lambda kt, rows: values[0:rows, b, kt, :], "finish": finish,
                            "ready": (t_qs, t_keys[-1], t_val)}

                items = [item(b, qt) for b in range(B) for qt in range(TPB)]
                with ExitStack() as actx:
                    attention(k, actx, "bn%d" % layer, items, 1.0 / 16.0, P)
                    k.barrier()

        with ExitStack() as ctx:
            qf = k.sb(ctx, "fused_q8", [P, HALVES, NTOK], BF16)
            qavg = k.sb(ctx, "avg_q8", [P, HALVES * B], BF16)
            hid = k.sb(ctx, "hidden", [P, 8, NTOK])
            q, t_q = ternary(ctx, ["f1", "f2"], [(P, 4, FF), (P, 8, D)], hid[:].rearrange("p f t -> p (f t)"))
            qh = k.sb(ctx, "hidden_q8", [P, 8, NTOK], BF16)
            hbias = k.sb(ctx, "hidden_bias", [P, 8, B])
            t = V.mark(nc.vector.tensor_reduce(mcols[:, 0:1], fused[:], AX.XY, ALU.max, apply_absolute_value=True))
            t = V.mark(nc.vector.tensor_reduce(mcols[:, 1:2], avg[:], AX.X, ALU.max, apply_absolute_value=True))
            t = input_scale(4, 2, t)
            t_s = out_scale(4, "f1", 5, t)
            V.after(t_s)
            t_f = [quantize(4, qf[:, h, :], fused[:, h, :], P) for h in range(HALVES)]
            t_a = quantize(4, qavg[:], avg[:], P)
            i, bank = k.banks.take(k.pe)
            k.pe.after(t_a, t_q)
            for ft in range(8):
                for h in range(HALVES):
                    ins = nc.tensor.matmul(bank[:, ft * B:(ft + 1) * B], q["f1"][:, 2 + h, ft * P:(ft + 1) * P],
                                           qavg[:, h * B:(h + 1) * B], start=(h == 0), stop=(h == 1))
            t = k.pe.mark(ins)
            o, _ = COL_AT["b_f1"]
            t_hb = V.mark(V.after(t).scalar_tensor_tensor(
                hbias[:], bank[:, 0:8 * B].rearrange("p (f b) -> p f b", b=B), s_out[:, 5:6],
                k.cols[:, o:o + 8].unsqueeze(2).to_broadcast([P, 8, B]), ALU.mult, ALU.add))
            k.banks.release(i, t_hb)
            n = 0
            for b in range(B):
                for ft in range(8):
                    i, bank = k.banks.take(k.pe)
                    cs = slice(b * T, (b + 1) * T)
                    t = k.matmuls(bank, [(q["f1"][:, h, ft * P:(ft + 1) * P], qf[:, h, cs]) for h in range(HALVES)], *t_f)
                    t = A.mark(A.after(t, t_hb, t_q).activation(hid[:, ft, cs], bank, ACT.Relu, scale=s_out[:, 5:6],
                                                           bias=hbias[:, ft, b:b + 1]))
                    k.banks.release(i, t)
                    t = V.mark(V.after(t).tensor_reduce(mcols[:, n:n + 1], hid[:, ft, cs], AX.X, ALU.max))
                    n += 1
            t_xb = k.pool.mark(k.pool.after(k.t_param).tensor_tensor(
                k.x_tok[:], k.x_tok[:], row(k, "b_f2").unsqueeze(1).to_broadcast([P, TILES, D]), ALU.add))
            t = input_scale(5, n, t)
            t_s = out_scale(5, "f2", 6, t)
            V.after(t_s)
            t_h = [quantize(5, qh[:, :, b * T:(b + 1) * T], hid[:, :, b * T:(b + 1) * T], P) for b in range(B)]
            ready = {}
            for tile in range(TILES):
                i, bank = k.banks.take(k.pe)
                t = k.matmuls(bank[:, 0:D], [(qh[:, ft, tile * P:(tile + 1) * P], q["f2"][:, ft, :]) for ft in range(8)],
                              t_h[tile // TPB])
                ready[tile] = V.mark(V.after(t, t_xb).scalar_tensor_tensor(
                    k.x_tok[:, tile, :], bank[:, 0:D], s_out[:, 6:7], k.x_tok[:, tile, :], ALU.mult, ALU.add))
                k.banks.release(i, ready[tile])
            k.barrier()
    post_norm(k, ready)
    k.barrier()


def experts(k):
    nc, V, A = k.nc, k.dve, k.act
    with ExitStack() as ctx:
        sb = lambda name, shape, dt=F32: k.sb(ctx, name, shape, dt)
        w1s = Ring([sb("moe_w1_%d" % n, [P, HALVES, FF]) for n in range(2)])
        w2s = Ring([sb("moe_w2_%d" % n, [P, 8, D]) for n in range(2)])
        wg, b2 = sb("moe_wg", [P, HALVES, NE]), sb("moe_b2", [NE, D])
        t_g = k.load("moe_g", (wg[:], k.dram["moe_wg"].rearrange("(h p) e -> p h e", p=P)), (b2[:], k.dram["moe_b2"]))
        xhat_tok, xhat = sb("xhat_tok", [P, TILES, D]), sb("xhat", [P, HALVES, NTOK])
        normed = Ring([sb("normed%d" % n, [P, HALVES, NTOK]) for n in range(2)])
        hidden = Ring([sb("moe_h%d" % n, [P, 8, BANK]) for n in range(2)])
        sc = sb("gate_scores", [P, TILES, NE])
        cmp1, cmp2 = sb("cmp1", [P, TILES, NE, NE]), sb("cmp2", [P, TILES, NE, NE])
        gate, top = sb("gate_w", [P, TILES, NE]), sb("gate_top", [P, TILES])
        gsum = sb("gate_sum", [P, TILES])
        gate_ch = sb("gate_ch", [NE, TILES, P])

        def load_expert(e):
            i1, w1 = w1s.take(k.sp)
            i2, w2 = w2s.take(k.sp)
            t = k.load("moe%d" % e, (w1[:], k.dram["moe_w1"][e].rearrange("(h p) f -> p h f", p=P)),
                       (w2[:], k.dram["moe_w2"][e].rearrange("(f p) d -> p f d", p=P)))
            return i1, w1, i2, w2, t
        loaded = [load_expert(0), load_expert(1)]

        i, bank = k.banks.take(k.pe)
        k.pe.after(t_g, *k.ch[3])
        for tile in range(TILES):
            for h in range(HALVES):
                ins = nc.tensor.matmul(bank[:, tile * NE:(tile + 1) * NE], k.x_ch[:, h, tile * P:(tile + 1) * P],
                                       wg[:, h, :], start=(h == 0), stop=(h == 1))
        t = k.pe.mark(ins)
        t = V.mark(V.after(t).tensor_copy(sc[:], bank[:, 0:TILES * NE].rearrange("p (t e) -> p t e", e=NE)))
        k.banks.release(i, t)
        V.after(t)
        shape = [P, TILES, NE, NE]
        mine = sc[:].unsqueeze(3).to_broadcast(shape)
        other = sc[:].unsqueeze(2).to_broadcast(shape)
        flat = lambda a: a[:].rearrange("p t a b -> p t (a b)")
        V.mark(nc.vector.tensor_tensor(cmp1[:], other, mine, ALU.is_gt))
        t = V.mark(nc.vector.tensor_tensor(cmp2[:], other, mine, ALU.is_equal))
        V.mark(nc.vector.tensor_reduce(top[:], sc[:], AX.X, ALU.max))
        t = V.mark(V.after(t).tensor_tensor(flat(cmp2), flat(cmp2), const(k, "lower").unsqueeze(1).to_broadcast([P, TILES, 64]), ALU.mult))
        t = V.mark(V.after(t).tensor_tensor(flat(cmp1), flat(cmp1), flat(cmp2), ALU.add))
        t = V.mark(V.after(t).tensor_reduce(gate[:], cmp1[:], AX.X, ALU.add))
        t1 = V.mark(V.after(t).tensor_scalar(gate[:], gate[:], 1.5, None, ALU.is_lt))
        t = V.mark(nc.vector.tensor_tensor(sc[:], sc[:], top[:].unsqueeze(2).to_broadcast([P, TILES, NE]), ALU.subtract))
        t = A.mark(A.after(t).activation(sc[:], sc[:], ACT.Exp))
        t = V.mark(V.after(t, t1).tensor_tensor(gate[:], gate[:], sc[:], ALU.mult))
        t = V.mark(V.after(t).tensor_reduce(gsum[:], gate[:], AX.X, ALU.add))
        t = V.mark(V.after(t).reciprocal(top[:], gsum[:]))
        t_gate = V.mark(V.after(t).tensor_tensor(gate[:], gate[:], top[:].unsqueeze(2).to_broadcast([P, TILES, NE]), ALU.mult))
        t = V.mark(V.after(t_gate).tensor_reduce(gsum[:], gate[:], AX.X, ALU.add))
        t_gsum = V.mark(V.after(t).tensor_scalar(gsum[:], gsum[:], 1.0, None, ALU.add))
        for g in range(4):
            i, bank = k.banks.take(k.pe)
            k.pe.after(t_gate)
            for m in range(4):
                ins = nc.tensor.transpose(bank[0:NE, m * P:(m + 1) * P], gate[:, 4 * g + m, :], const(k, "ident"))
            t = k.pe.mark(ins)
            t_gc = A.mark(A.after(t).copy(gate_ch[:, 4 * g:4 * g + 4, :].rearrange("e t q -> e (t q)"), bank[0:NE, :]))
            k.banks.release(i, t_gc)

        t_hat = layer_norm(k, k.x_tok, xhat_tok, {i: None for i in range(TILES)}, 1)
        t_hc = to_channels(k, xhat_tok, xhat, t_hat)
        ready = {}
        for tile in range(TILES):
            i, bank = k.banks.take(k.pe)
            t = k.matmuls(bank[:, 0:D], [(gate_ch[:, tile, :], b2[:])], t_gc, t_g)
            ready[tile] = V.mark(V.after(t, t_gsum, t_hat[tile]).scalar_tensor_tensor(
                k.x_tok[:, tile, :], k.x_tok[:, tile, :], gsum[:, tile:tile + 1], bank[:, 0:D], ALU.mult, ALU.add))
            k.banks.release(i, ready[tile])

        def second(e, g, ih, h, t_h, w2, t_w):
            for pair in range(2):
                i, bank = k.banks.take(k.pe)
                k.pe.after(t_w, *t_h)
                for s in range(2):
                    m = 2 * pair + s
                    for ft in range(8):
                        ins = nc.tensor.matmul(bank[:, s * D:(s + 1) * D], h[:, ft, m * P:(m + 1) * P], w2[:, ft, :],
                                               start=(ft == 0), stop=(ft == 7))
                t = k.pe.mark(ins)
                for s in range(2):
                    tile = 4 * g + 2 * pair + s
                    ready[tile] = t = V.mark(V.after(t, ready[tile]).scalar_tensor_tensor(
                        k.x_tok[:, tile, :], bank[:, s * D:(s + 1) * D], gate[:, tile, e:e + 1], k.x_tok[:, tile, :],
                        ALU.mult, ALU.add))
                k.banks.release(i, t)
            hidden.release(ih, k.pe.last())

        pending = None
        for e in range(NE):
            i1, w1, i2, w2, t_w = loaded[e]
            inn, nm = normed.take(V)
            V.after(*t_hc[3])
            for h in range(HALVES):
                t_n = V.mark(nc.vector.tensor_scalar(nm[:, h, :], xhat[:, h, :], col(k, "moe_gamma", 2 * e + h),
                                                     col(k, "moe_beta", 2 * e + h), ALU.mult, ALU.add))
            for g in range(4):
                ih, hd = hidden.take(A)
                V.after(*hidden.readers[ih])
                t_h = []
                for ft in range(8):
                    i, bank = k.banks.take(k.pe)
                    t = k.matmuls(bank, [(w1[:, h, ft * P:(ft + 1) * P], nm[:, h, g * BANK:(g + 1) * BANK])
                                         for h in range(HALVES)], t_w, t_n)
                    bias = col(k, "moe_b1", 8 * e + ft)
                    if ft % 2:
                        t = V.mark(V.after(t).tensor_scalar(hd[:, ft, :], bank, bias, 0.0, ALU.add, ALU.max))
                    else:
                        t = A.mark(A.after(t).activation(hd[:, ft, :], bank, ACT.Relu, bias=bias))
                    k.banks.release(i, t)
                    t_h.append(t)
                if pending:
                    second(*pending)
                    if g == 0:
                        w1s.release(loaded[e - 1][0], k.pe.last())
                        w2s.release(loaded[e - 1][2], k.pe.last())
                        if e + 1 < NE:
                            loaded.append(load_expert(e + 1))
                pending = (e, g, ih, hd, t_h[-2:], w2, t_w)
            normed.release(inn, k.pe.last())
        second(*pending)
        k.barrier()
    post_norm(k, ready)
    k.barrier()


def linear_attention(k):
    nc, V, A = k.nc, k.dve, k.act
    CV = P + 8
    with ExitStack() as ctx:
        sb = lambda name, shape, dt=F32: k.sb(ctx, name, shape, dt)
        two = lambda name, shape: Ring([sb("%s%d" % (name, n), shape) for n in range(2)])
        wqkv, wproj = sb("la_wqkv", [P, HALVES, 3 * D]), sb("la_wproj", [P, HALVES, D])
        t_w = k.load("la_w", (wqkv[:], k.dram["la_qkvT"].rearrange("(h p) o -> p h o", p=P)),
                     (wproj[:], k.dram["la_projT"].rearrange("(h p) o -> p h o", p=P)))
        q_ch = two("la_q", [P, HALVES, T])
        scratch = two("la_min", [P, BANK])
        kv_tok = two("la_kv", [P, 2 * D])
        k_phi = two("la_k", [P, TPB, D])
        v_aug = [sb("la_v%d" % n, [P, TPB, HALVES, P + 1]) for n in range(2)]
        kvd = two("la_kvd", [P, HALVES, CV])
        den = two("la_den", [P, H0])
        o_tok, o_ch = two("la_o", [P, TPB, D]), two("la_oc", [P, HALVES, T])
        a_tok = sb("la_out", [P, TILES, D])
        regrouped = Ring([sb("la_rg%d" % n, [P, HALVES, T]) for n in range(B)])
        regroup_of = {}
        for n in range(2):
            V.mark(nc.vector.memset(v_aug[n][:, :, :, P:P + 1], 1.0))
        v_aug = Ring(v_aug)
        done = {}
        for b in range(B):
            cs = slice(b * T, (b + 1) * T)
            jq, qc = q_ch.take(A)
            for c in range(HALVES):
                i, bank = k.banks.take(k.pe)
                t = k.matmuls(bank, [(wqkv[:, h, c * P:(c + 1) * P], k.x_ch[:, h, cs]) for h in range(HALVES)],
                              t_w, *k.ch[b])
                js, mn = scratch.take(V)
                t1 = V.mark(V.after(t).tensor_scalar(mn[:], bank, col(k, "la_bq", c), 0.0, ALU.add, ALU.min))
                A.after(t1)
                t2 = A.mark(nc.scalar.activation(qc[:, c, :], bank, ACT.Relu, bias=col(k, "la_bq", c)))
                k.banks.release(i, t2)
                t = A.mark(nc.scalar.activation(mn[:], mn[:], ACT.Exp))
                t_q = V.mark(V.after(t).tensor_tensor(qc[:, c, :], qc[:, c, :], mn[:], ALU.add))
                scratch.release(js, t_q)
            jk, kp = k_phi.take(V)
            jv, va = v_aug.take(A)
            for n in range(TPB):
                i, bank = k.banks.take(k.pe)
                tile = slice((b * TPB + n) * P, (b * TPB + n + 1) * P)
                t = k.matmuls(bank, [(k.x_ch[:, h, tile], wqkv[:, h, D:3 * D]) for h in range(HALVES)], *k.ch[b])
                jt, kv = kv_tok.take(V)
                t = V.mark(V.after(t).tensor_tensor(kv[:], bank, row(k, "la_bkv"), ALU.add))
                k.banks.release(i, t)
                t_v = A.mark(A.after(t).copy(va[:, n, :, 0:P], kv[:, D:2 * D].rearrange("p (h c) -> p h c", c=P)))
                js, mn = scratch.take(V)
                t = V.mark(V.after(t).tensor_scalar(mn[:, 0:D], kv[:, 0:D], 0.0, None, ALU.min))
                t = A.mark(A.after(t).activation(mn[:, 0:D], mn[:, 0:D], ACT.Exp))
                t_k = V.mark(V.after(t).scalar_tensor_tensor(kp[:, n, :], kv[:, 0:D], 0.0, mn[:, 0:D], ALU.max, ALU.add))
                scratch.release(js, t_k)
                kv_tok.release(jt, t_k, t_v)
            i, bank = k.banks.take(k.pe)
            k.pe.after(t_k, t_v)
            for n in range(TPB):
                for h in range(HALVES):
                    ins = nc.tensor.matmul(bank[:, h * (P + 1):(h + 1) * (P + 1)], kp[:, n, h * P:(h + 1) * P],
                                           va[:, n, h, :], start=(n == 0 and h == 0), stop=(n == TPB - 1),
                                           skip_group_check=True)
            t = k.pe.mark(ins)
            k_phi.release(jk, t)
            v_aug.release(jv, t)
            jd, kd = kvd.take(V)
            V.after(t)
            for h in range(HALVES):
                o = h * (P + 1)
                V.mark(nc.vector.tensor_tensor(kd[:, h, 0:P], bank[:, o:o + P], const(k, "diag16"), ALU.mult))
                t_kd = V.mark(nc.vector.tensor_scalar(kd[:, h, P:CV], const(k, "head16"), bank[:, o + P:o + P + 1],
                                                      None, ALU.mult))
            k.banks.release(i, t_kd)
            jo, ot = o_tok.take(V)
            for n in range(TPB):
                i, bank = k.banks.take(k.pe)
                k.pe.after(t_kd, t_q)
                for h in range(HALVES):
                    ins = nc.tensor.matmul(bank[:, h * CV:(h + 1) * CV], qc[:, h, n * P:(n + 1) * P], kd[:, h, :],
                                           start=True, stop=True)
                t = k.pe.mark(ins)
                view = bank[:, 0:2 * CV].rearrange("p (h c) -> p h c", c=CV)
                jn, dn = den.take(V)
                dv = dn[:].rearrange("p (h a) -> p h a", h=2)
                t = V.mark(V.after(t).tensor_scalar(dv, view[:, :, P:CV], 1e-6, None, ALU.max))
                t = V.mark(V.after(t).reciprocal(dn[:], dn[:]))
                V.after(t)
                for h in range(HALVES):
                    t_o = V.mark(nc.vector.tensor_tensor(
                        ot[:, n, h * P:(h + 1) * P].rearrange("p (a c) -> p a c", c=N0),
                        view[:, h, 0:P].rearrange("p (a c) -> p a c", c=N0),
                        dn[:, 8 * h:8 * h + 8].unsqueeze(2).to_broadcast([P, 8, N0]), ALU.mult))
                den.release(jn, t_o)
                k.banks.release(i, t_o)
            kvd.release(jd, k.pe.last())
            q_ch.release(jq, k.pe.last())
            jc, oc = o_ch.take(A)
            for h in range(HALVES):
                i, bank = k.banks.take(k.pe)
                k.pe.after(t_o)
                for n in range(TPB):
                    ins = nc.tensor.transpose(bank[:, n * P:(n + 1) * P], ot[:, n, h * P:(h + 1) * P], const(k, "ident"))
                t = k.pe.mark(ins)
                t_oc = A.mark(A.after(t).copy(oc[:, h, :].rearrange("p (s m) -> p s m", s=N0),
                                              bank.rearrange("p (m s) -> p s m", s=N0)))
                k.banks.release(i, t_oc)
            o_tok.release(jo, k.pe.last())
            sem = k.sem("regrouped%d" % b)
            k.sp.after(t_oc)
            for hd in range(H0):
                nc.sync.dma_start(k.dram["regroup"][b, :, :, hd, :].rearrange("s v m -> v s m"),
                                  oc[(hd % 8) * N0:(hd % 8 + 1) * N0, hd // 8, :].rearrange("v (s m) -> v s m", s=N0)
                                  ).then_inc(sem, 16)
            t_out = (sem, 16 * H0)
            o_ch.release(jc, t_out)
            jr, rg = regrouped.take(k.sp)
            t_rg = k.load("regrouped%d" % b, (rg[:], k.dram["regroup"][b].rearrange("(g s) v h m -> (s v) g (h m)", g=2)),
                          after=(t_out,))
            regroup_of[b] = (jr, rg, t_rg)
        for b in range(B):
            jr, rg, t_rg = regroup_of[b]
            for n in range(TPB):
                i, bank = k.banks.take(k.pe)
                tile = b * TPB + n
                t = k.matmuls(bank[:, 0:D], [(rg[:, h, n * P:(n + 1) * P], wproj[:, h, :]) for h in range(HALVES)], t_rg)
                done[tile] = V.mark(V.after(t).tensor_tensor(a_tok[:, tile, :], bank[:, 0:D], row(k, "la_bproj"), ALU.add))
                k.banks.release(i, done[tile])
        done = layer_norm(k, a_tok, a_tok, done, 0)
        ready = {}
        over = lambda name: row(k, name).unsqueeze(1).to_broadcast([P, TPB, D])
        for b in range(B):
            a = a_tok[:, b * TPB:(b + 1) * TPB, :]
            xs = k.x_tok[:, b * TPB:(b + 1) * TPB, :]
            G = k.pool
            t = G.mark(G.after(*[done[b * TPB + n] for n in range(TPB)]).tensor_tensor(a, a, over("la_gamma"), ALU.mult))
            t = G.mark(G.after(t).tensor_tensor(a, a, over("la_beta"), ALU.add))
            t = V.mark(V.after(t).scalar_tensor_tensor(xs, xs, 2.0, a, ALU.mult, ALU.add))
            for n in range(TPB):
                ready[b * TPB + n] = t
        k.barrier()
    post_norm(k, ready)
    k.barrier()


def cross_attention(k):
    nc, V, A = k.nc, k.dve, k.act
    with ExitStack() as ctx:
        sb = lambda name, shape, dt=F32: k.sb(ctx, name, shape, dt)
        two = lambda name, shape: Ring([sb("%s%d" % (name, n), shape) for n in range(2)])
        wq, wo = sb("xa_wq", [P, HALVES, D]), sb("xa_wo", [P, HALVES, D])
        wk, wv = sb("xa_wk", [CP, HALVES, D]), sb("xa_wv", [CP, HALVES, D])
        t_w = k.load("xa_w", *[(w[:], k.dram["xa_" + n].rearrange("(h p) o -> p h o", h=2))
                               for n, w in (("q", wq), ("o", wo), ("k", wk), ("v", wv))])
        ctxs = Ring([sb("xa_ctx%d" % n, [CP, HALVES, S2]) for n in range(1)])
        keys, values = two("xa_keys", [P, HALVES, S2]), two("xa_values", [P, KT, D])
        q_ch = sb("xa_q_ch", [P, HALVES, NTOK])
        q_head = [[sb("xa_qh%d_%d" % (n, h), [P, 4, T]) for h in range(HALVES)] for n in range(1)]
        q_head = Ring(q_head)
        o_tok, o_ch = two("xa_o", [P, TPB, D]), two("xa_oc", [P, HALVES, T])
        t_q = {}
        for g in range(B):
            for c in range(HALVES):
                i, bank = k.banks.take(k.pe)
                cs = slice(g * T, (g + 1) * T)
                t = k.matmuls(bank, [(wq[:, h, c * P:(c + 1) * P], k.x_ch[:, h, cs]) for h in range(HALVES)], t_w, *k.ch[g])
                t_q[g] = A.mark(A.after(t).activation(q_ch[:, c, cs], bank, ACT.Identity, bias=col(k, "xa_bq", c)))
                k.banks.release(i, t_q[g])

        ready = {}
        state = {}

        def prepare(b):
            jc, cx = ctxs.take(k.sp)
            t_c = k.load("xa_ctx%d" % b, (cx[:], k.dram["ctxT"][:, b, :].rearrange("(h p) s -> p h s", h=2)))
            jk, kc = keys.take(A)
            for c0 in range(0, S2, BANK):
                c1 = min(c0 + BANK, S2)
                for o in range(HALVES):
                    i, bank = k.banks.take(k.pe)
                    t = k.matmuls(bank[:, 0:c1 - c0], [(wk[:, h, o * P:(o + 1) * P], cx[:, h, c0:c1]) for h in range(HALVES)], t_c, t_w)
                    t_k = A.mark(A.after(t).activation(kc[:, o, c0:c1], bank[:, 0:c1 - c0], ACT.Identity, bias=col(k, "xa_bk", o)))
                    k.banks.release(i, t_k)
            jv, vc = values.take(V)
            for kt in range(KT):
                rows = P if kt < KT - 1 else KLAST
                i, bank = k.banks.take(k.pe)
                t = k.matmuls(bank[0:rows, 0:D], [(cx[:, h, kt * P:kt * P + rows], wv[:, h, :]) for h in range(HALVES)], t_c)
                t_v = V.mark(V.after(t).tensor_tensor(vc[0:rows, kt, :], bank[0:rows, 0:D], row(k, "xa_bv")[0:rows], ALU.add))
                k.banks.release(i, t_v)
            ctxs.release(jc, k.pe.last())
            jh, qh = q_head.take(k.pool)
            k.pool.after(t_q[b])
            for h in range(HALVES):
                t_h = k.pool.mark(nc.gpsimd.tensor_tensor(
                    qh[h][:], q_ch[:, h, b * T:(b + 1) * T].unsqueeze(1).to_broadcast([P, 4, T]),
                    const(k, "head32").unsqueeze(2).to_broadcast([P, 4, T]), ALU.mult))
            jo, ot = o_tok.take(V)
            state[b] = (kc, vc, qh, ot, (t_k, t_v, t_h))
            return jk, jv, jh, jo

        def project(b, t_o, jo):
            _, _, _, ot, _ = state[b]
            jc, oc = o_ch.take(A)
            for h in range(HALVES):
                i, bank = k.banks.take(k.pe)
                k.pe.after(t_o)
                for n in range(TPB):
                    ins = nc.tensor.transpose(bank[:, n * P:(n + 1) * P], ot[:, n, h * P:(h + 1) * P], const(k, "ident"))
                t = k.pe.mark(ins)
                t_oc = A.mark(A.after(t).copy(oc[:, h, :], bank))
                k.banks.release(i, t_oc)
            o_tok.release(jo, k.pe.last())
            for n in range(TPB):
                i, bank = k.banks.take(k.pe)
                tile = b * TPB + n
                t = k.matmuls(bank[:, 0:D], [(oc[:, h, n * P:(n + 1) * P], wo[:, h, :]) for h in range(HALVES)], t_oc)
                ready[tile] = V.mark(V.after(t, t_bias).tensor_tensor(k.x_tok[:, tile, :], bank[:, 0:D], k.x_tok[:, tile, :], ALU.add))
                k.banks.release(i, ready[tile])
            o_ch.release(jc, k.pe.last())

        t_bias = k.pool.mark(k.pool.after(*[k.tok[i] for i in range(TILES)]).tensor_tensor(
            k.x_tok[:], k.x_tok[:], row(k, "xa_bo").unsqueeze(1).to_broadcast([P, TILES, D]), ALU.add))

        class Items:

            def __len__(self):
                return B * HX * TPB

            def __iter__(self):
                for b in range(B):
                    slots = prepare(b)
                    for hd in range(HX):
                        for qt in range(TPB):
                            yield self.item(b, hd, qt, slots)

            def item(self, b, hd, qt, slots):
                kc, vc, qh, ot, tokens = state[b]
                h, a = hd // 4, hd % 4

                def finish(obank, io, rsum, after):
                    t = V.mark(V.after(*after).tensor_scalar(ot[:, qt, hd * NX:(hd + 1) * NX], obank[:, 0:NX], rsum,
                                                             None, ALU.mult))
                    k.banks.release(io, t)
                    if (hd, qt) == (HX - 1, TPB - 1):
                        last = k.pe.last()
                        keys.release(slots[0], last)
                        values.release(slots[1], last)
                        project(b, t, slots[3])

                return {"query": qh[h][:, a, qt * P:(qt + 1) * P], "keys": lambda c0, c1: kc[:, h, c0:c1],
                        "value": lambda kt, rows: vc[0:rows, kt, hd * NX:(hd + 1) * NX], "finish": finish,
                        "ready": tokens,
                        "scored": (lambda t: q_head.release(slots[2], t)) if (hd, qt) == (HX - 1, TPB - 1) else None}

        attention(k, ctx, "xa", Items(), 1.0 / float(np.sqrt(np.float32(NX))), NX)
        k.barrier()
    post_norm(k, ready)
    k.barrier()


def windowed(k):
    with ExitStack() as ctx:
        x_in = k.sb(ctx, "x_in", [P, TILES, D])
        k.pool.mark(k.pool.after(*[k.tok[i] for i in range(TILES)]).tensor_copy(x_in[:], k.x_tok[:]))
        k.barrier()
        for layer in range(2):
            windowed_layer(k, layer)
            k.barrier()
        ready = {i: k.dve.mark(k.nc.vector.tensor_tensor(k.x_tok[:, i, :], k.x_tok[:, i, :], x_in[:, i, :], ALU.add))
                 for i in range(TILES)}
        k.tok = layer_norm(k, k.x_tok, k.x_tok, ready, 0)
        k.barrier()


def windowed_layer(k, layer):
    nc, V, A, G = k.nc, k.dve, k.act, k.pool
    with ExitStack() as ctx:
        sb = lambda name, shape, dt=F32: k.sb(ctx, name + "_l%d" % layer, shape, dt)
        two = lambda name, shape: Ring([sb("%s%d" % (name, n), shape) for n in range(2)])
        wqkv, wo = sb("wqkv", [P, HALVES, 3 * INNER]), sb("wo", [P, 4, D])
        rot, tab = sb("rotary", [P, TPB, 4, NL]), sb("rotary_scaled", [P, TPB, 4, NL])
        mask, mask_b, ident_b = sb("mask", [P, 2 * P]), sb("mask_b", [P, 2 * P], BF16), sb("ident_b", [P, P], BF16)
        t_w = k.load("win%d" % layer, (wqkv[:], k.dram["wqkv"][layer].rearrange("(h p) o -> p h o", p=P)),
                     (wo[:], k.dram["wo"][layer].rearrange("(c p) o -> p c o", p=P)),
                     (rot[:], k.dram["rotary"]), (mask[:], k.dram["mask"]))
        V.after(t_w)
        V.mark(nc.vector.tensor_copy(mask_b[:], mask[:]))
        V.mark(nc.vector.tensor_copy(ident_b[:], const(k, "ident")))
        half = NL // 2
        for n, name in ((0, "q_scale"), (2, "k_scale")):
            s = row(k, name, layer * NL, (layer + 1) * NL)
            wide = lambda a, w: a.unsqueeze(1).to_broadcast([P, TPB, w])
            V.mark(nc.vector.tensor_tensor(tab[:, :, n, :], rot[:, :, n, :], wide(s, NL), ALU.mult))
            V.mark(nc.vector.tensor_tensor(tab[:, :, n + 1, 0:half], rot[:, :, n + 1, 0:half], wide(s[:, half:NL], half), ALU.mult))
            t_tab = V.mark(nc.vector.tensor_tensor(tab[:, :, n + 1, half:NL], rot[:, :, n + 1, half:NL], wide(s[:, 0:half], half), ALU.mult))
        late = sb("late", [P, B, T + 1])
        V.after(*k.ch[3], *k.ch[2], *k.ch[1], *k.ch[0])
        V.mark(nc.vector.memset(late[:, :, 0:1], 0.0))
        t_late = V.mark(nc.vector.tensor_copy(late[:, :, 1:T + 1], k.x_ch[:, 1, :].rearrange("p (b t) -> p b t", t=T)))

        raw = two("qk_raw", [P, INNER])
        square = two("qk_sq", [P, INNER])
        norm = two("qk_norm", [P, HL])
        turned = two("qk_rot", [P, INNER])
        other = two("qk_other", [P, INNER])
        q_ch, k_ch, v_tok = two("w_q", [P, 4, T]), two("w_k", [P, 4, T]), two("w_v", [P, TPB, INNER])
        probs, probs_t = two("w_p", [P, HL, 2 * P]), two("w_pt", [P, HL, 2, P])
        maxes, sums = two("w_max", [P, HL]), two("w_sum", [P, HL])
        o_tok, o_ch = two("w_o", [P, INNER]), two("w_oc", [P, 4, P])
        heads3 = lambda a: a.rearrange("p (h c) -> p h c", c=NL)
        ready = {}

        def rotate(b, w, which, dst):
            tile = b * TPB + w
            i, bank = k.banks.take(k.pe)
            t = k.matmuls(bank, [(k.x_ch[:, 0, tile * P:(tile + 1) * P], wqkv[:, 0, which * INNER:(which + 1) * INNER]),
                                 (late[:, b, w * P:(w + 1) * P], wqkv[:, 1, which * INNER:(which + 1) * INNER])],
                          t_w, t_late)
            jr, rw = raw.take(A)
            t_raw = A.mark(A.after(t).copy(rw[:], bank))
            k.banks.release(i, t_raw)
            js, sq = square.take(A)
            t = A.mark(A.after(t_raw).activation(sq[:], rw[:], ACT.Square))
            jn, nm = norm.take(V)
            t = V.mark(V.after(t).tensor_reduce(nm[:], heads3(sq[:]), AX.X, ALU.add))
            square.release(js, t)
            t = A.mark(A.after(t).activation(nm[:], nm[:], ACT.Sqrt))
            t = V.mark(V.after(t).tensor_scalar(nm[:], nm[:], 1e-12, None, ALU.max))
            t_n = V.mark(V.after(t).reciprocal(nm[:], nm[:]))
            jt, tn = turned.take(V)
            jo, ot = other.take(G)
            x3 = heads3(rw[:])
            o3 = heads3(ot[:])
            wide = lambda a, n: a.unsqueeze(1).to_broadcast([P, HL, n])
            G.after(t_raw, t_tab)
            G.mark(nc.gpsimd.tensor_tensor(o3[:, :, 0:half], x3[:, :, half:NL], wide(tab[:, w, 2 * which + 1, 0:half], half), ALU.mult))
            t2 = G.mark(nc.gpsimd.tensor_tensor(o3[:, :, half:NL], x3[:, :, 0:half], wide(tab[:, w, 2 * which + 1, half:NL], half), ALU.mult))
            t1 = V.mark(V.after(t_raw, t_tab).tensor_tensor(heads3(tn[:]), x3, wide(tab[:, w, 2 * which, :], NL), ALU.mult))
            t = V.mark(V.after(t1, t2).tensor_tensor(tn[:], tn[:], ot[:], ALU.add))
            raw.release(jr, t1, t2)
            other.release(jo, t)
            t = V.mark(V.after(t, t_n).tensor_tensor(heads3(tn[:]), heads3(tn[:]), nm[:].unsqueeze(2).to_broadcast([P, HL, NL]), ALU.mult))
            norm.release(jn, t)
            i, bank = k.banks.take(k.pe)
            k.pe.after(t)
            for c in range(4):
                ins = nc.tensor.transpose(bank[:, c * P:(c + 1) * P], tn[:, c * P:(c + 1) * P], const(k, "ident"))
            t = k.pe.mark(ins)
            turned.release(jt, t)
            t = A.mark(A.after(t).copy(dst[:, :, w * P:(w + 1) * P], bank.rearrange("p (c t) -> p c t", t=P)))
            k.banks.release(i, t)
            return t

        def produce(b, w, bufs):
            qc, kc, vt = bufs
            tile = b * TPB + w
            t_q = rotate(b, w, 0, qc)
            t_k = rotate(b, w, 1, kc)
            i, bank = k.banks.take(k.pe)
            t = k.matmuls(bank, [(k.x_ch[:, 0, tile * P:(tile + 1) * P], wqkv[:, 0, 2 * INNER:3 * INNER]),
                                 (late[:, b, w * P:(w + 1) * P], wqkv[:, 1, 2 * INNER:3 * INNER])])
            t_v = A.mark(A.after(t).copy(vt[:, w, :], bank))
            k.banks.release(i, t_v)
            return t_q, t_k, t_v

        def score(b, w, bufs, tokens):
            qc, kc, vt = bufs
            a = 0 if w else 1
            lo = a * P
            k.pe.after(*k.score_free, *tokens, t_tab)
            for bk in range(4):
                out = k.psum[:, bk, :].rearrange("p (x j) -> p x j", x=2)[:, :, lo:2 * P]
                nc.tensor.matmul(out, ident_b[:], mask_b[:, lo:2 * P].unsqueeze(1).to_broadcast([P, 2, 2 * P - lo]),
                                 start=True, stop=False, skip_group_check=True)
            for s in range(2):
                for p in range(4):
                    out = k.psum[:, 2 * s + p // 2, (p % 2) * 2 * P + lo:(p % 2 + 1) * 2 * P]
                    ins = nc.tensor.matmul(out, qc[64 * s:64 * s + 64, p, w * P:(w + 1) * P],
                                           kc[64 * s:64 * s + 64, p, (w - 1) * P + lo:(w + 1) * P],
                                           start=False, stop=True, skip_group_check=True)
            t = k.pe.mark(ins)
            sc = k.psum[:, 0:4, :].rearrange("p b (x j) -> p (b x) j", x=2)[:, :, lo:2 * P]
            jm, mx = maxes.take(V)
            t = V.mark(V.after(t).tensor_reduce(mx[:], sc, AX.X, ALU.max))
            t = V.mark(V.after(t).tensor_scalar(mx[:], mx[:], -8.0, None, ALU.mult))
            jp, pr = probs.take(A)
            js, sm = sums.take(A)
            A.after(t)
            for x in range(HL):
                t = A.mark(nc.scalar.activation(pr[:, x, lo:2 * P], sc[:, x, :], ACT.Exp, bias=mx[:, x:x + 1], scale=8.0,
                                                accum_out=sm[:, x:x + 1]))
            k.score_free = (t,)
            maxes.release(jm, t)
            t_s = V.mark(V.after(t).reciprocal(sm[:], sm[:]))
            return (b, w, bufs, a, jp, pr, js, sm, t, t_s)

        def combine(b, w, bufs, a, jp, pr, js, sm, t_p, t_s):
            qc, kc, vt = bufs
            jt, pt = probs_t.take(A)
            V.after(*probs_t.readers[jt])
            per = 2 - a
            k.pe.after(t_p)
            copied = []
            blocks = [(x, kk) for x in range(HL) for kk in range(a, 2)]
            for g in range(0, len(blocks), 4):
                i, bank = k.banks.take(k.pe)
                for n, (x, kk) in enumerate(blocks[g:g + 4]):
                    ins = nc.tensor.transpose(bank[:, n * P:(n + 1) * P], pr[:, x, kk * P:(kk + 1) * P], const(k, "ident"))
                t = k.pe.mark(ins)
                x0, cnt = blocks[g][0], 4 // per
                t = evacuate(k, g // 4, pt[:, x0:x0 + cnt, a:2, :], bank.rearrange("p (x c q) -> p x c q", x=cnt, q=P), t)
                k.banks.release(i, t)
                copied.append(t)
            probs.release(jp, k.pe.last())
            io, obank = k.banks.take(k.pe)
            k.pe.after(*copied)
            for x in range(HL):
                hd = 2 * (x % 4) + x // 4
                for kk in range(a, 2):
                    ins = nc.tensor.matmul(obank[:, hd * NL:(hd + 1) * NL], pt[:, x, kk, :],
                                           vt[:, w - 1 + kk, hd * NL:(hd + 1) * NL], start=(kk == a), stop=(kk == 1))
            t = k.pe.mark(ins)
            probs_t.release(jt, t)
            jo, ot = o_tok.take(V)
            V.after(t, t_s)
            for s in range(2):
                t = V.mark(nc.vector.tensor_tensor(
                    ot[:].rearrange("p (x s c) -> p s x c", s=2, c=NL)[:, s],
                    obank.rearrange("p (x s c) -> p s x c", s=2, c=NL)[:, s],
                    sm[:, 4 * s:4 * s + 4].unsqueeze(2).to_broadcast([P, 4, NL]), ALU.mult))
            k.banks.release(io, t)
            sums.release(js, t)
            i, bank = k.banks.take(k.pe)
            k.pe.after(t)
            for c in range(4):
                ins = nc.tensor.transpose(bank[:, c * P:(c + 1) * P], ot[:, c * P:(c + 1) * P], const(k, "ident"))
            t = k.pe.mark(ins)
            o_tok.release(jo, t)
            jc, oc = o_ch.take(A)
            t = A.mark(A.after(t).copy(oc[:].rearrange("p c t -> p (c t)"), bank))
            k.banks.release(i, t)
            i, bank = k.banks.take(k.pe)
            t = k.matmuls(bank[:, 0:D], [(oc[:, c, :], wo[:, c, :]) for c in range(4)], t)
            o_ch.release(jc, t)
            tile = b * TPB + w
            ready[tile] = V.mark(V.after(t).tensor_tensor(k.x_tok[:, tile, :], bank[:, 0:D], k.x_tok[:, tile, :], ALU.add))
            k.banks.release(i, ready[tile])

        waiting = None
        for b in range(B):
            slots = (q_ch.take(A), k_ch.take(A), v_tok.take(A))
            bufs = tuple(s[1] for s in slots)
            for w in range(TPB):
                tokens = produce(b, w, bufs)
                scored = score(b, w, bufs, tokens)
                if waiting:
                    combine(*waiting[0])
                    if waiting[1]:
                        for ring, s in zip((q_ch, k_ch, v_tok), waiting[1]):
                            ring.release(s[0], k.pe.last())
                waiting = (scored, slots if w == TPB - 1 else None)
        combine(*waiting[0])
        k.barrier()

    with ExitStack() as ctx:
        sb = lambda name, shape, dt=F32: k.sb(ctx, name + "_f%d" % layer, shape, dt)
        w1, w2 = sb("w1", [P, HALVES, 2 * HID]), sb("w2", [P, HT, D])
        full = (HT - 1) * P
        t_w = k.load("ffn%d" % layer, (w1[:], k.dram["w1"][layer].rearrange("(h p) o -> p h o", p=P)),
                     (w2[:, 0:HT - 1, :], k.dram["w2"][layer][0:full].rearrange("(c p) o -> p c o", p=P)),
                     (w2[0:HLAST, HT - 1, :], k.dram["w2"][layer][full:HID]))
        late = sb("late_tok", [P, TILES, P])
        h_tok, h_ch = sb("h_tok", [P, TILES, D]), sb("h_ch", [P, HALVES, NTOK])
        stats = sb("late_stats", [P, TILES, 2, 6])
        gl = Ring([sb("gelu%d" % n, [P, BANK]) for n in range(2)])
        hidden = Ring([sb("hidden%d" % n, [P, HT, BANK]) for n in range(2)])
        t = V.mark(nc.vector.memset(late[0:1], 0.0))
        src = k.x_tok[:, :, P:D]
        pairs = [(late[1:P], src[0:P - 1])]
        pairs += [(late[0:1, b * TPB + 1:(b + 1) * TPB, :], src[P - 1:P, b * TPB:(b + 1) * TPB - 1, :]) for b in range(B)]
        t_late = k.load("late%d" % layer, *pairs, after=(t, *[ready[i] for i in range(TILES)]))
        V.after(t_late)
        for i in range(TILES):
            V.mark(nc.vector.bn_stats(stats[:, i, 0, :], k.x_tok[:, i, 0:P]))
            t = V.mark(nc.vector.bn_stats(stats[:, i, 1, :], late[:, i, :]))
        V.after(t)
        for i in range(TILES):
            t = V.mark(nc.vector.bn_aggr(k.mv[:, i, :], stats[:, i, :, :].rearrange("p a s -> p (a s)")))
        t = A.mark(A.after(t, k.t_eps).activation(k.std[:], k.mv[:, :, 1], ACT.Sqrt, bias=k.eps[:, 0:1]))
        t = V.mark(V.after(t).reciprocal(k.rstd[:], k.std[:]))
        V.after(t)
        done = {}
        for i in range(TILES):
            for c, s in ((0, k.x_tok[:, i, 0:P]), (1, late[:, i, :])):
                done[i] = V.mark(nc.vector.tensor_scalar(h_tok[:, i, c * P:(c + 1) * P], s, k.mv[:, i, 0:1],
                                                         k.rstd[:, i:i + 1], ALU.subtract, ALU.mult))
        t_b2 = G.mark(G.after(*[done[i] for i in range(TILES)]).tensor_tensor(
            k.x_tok[:], k.x_tok[:], row(k, "b2", layer * D, (layer + 1) * D).unsqueeze(1).to_broadcast([P, TILES, D]), ALU.add))
        h_ready = to_channels(k, h_tok, h_ch, done, scale=lambda h: col(k, "lg", 2 * layer + h),
                              bias=lambda h: col(k, "lb", 2 * layer + h))

        def second(g, jh, hd, t_h):
            for pair in range(2):
                i, bank = k.banks.take(k.pe)
                k.pe.after(t_h)
                for s in range(2):
                    m = 2 * pair + s
                    for ft in range(HT):
                        rows = P if ft < HT - 1 else HLAST
                        ins = nc.tensor.matmul(bank[:, s * D:(s + 1) * D], hd[0:rows, ft, m * P:(m + 1) * P],
                                               w2[0:rows, ft, :], start=(ft == 0), stop=(ft == HT - 1))
                t = k.pe.mark(ins)
                for s in range(2):
                    tile = 4 * g + 2 * pair + s
                    ready[tile] = V.mark(V.after(t, t_b2).tensor_tensor(
                        k.x_tok[:, tile, :], bank[:, s * D:(s + 1) * D], k.x_tok[:, tile, :], ALU.add))
                k.banks.release(i, ready[tile])
            hidden.release(jh, k.pe.last())

        pending = None
        for g in range(4):
            jh, hd = hidden.take(V)
            for ft in range(HT):
                rows = P if ft < HT - 1 else HLAST
                got = []
                for part in range(2):
                    i, bank = k.banks.take(k.pe)
                    o = part * HID + ft * P
                    t = k.matmuls(bank[0:rows, :], [(w1[:, h, o:o + rows], h_ch[:, h, g * BANK:(g + 1) * BANK])
                                                    for h in range(HALVES)], t_w, *h_ready[g])
                    got.append((i, bank, t))
                jg, gg = gl.take(A)
                t = A.mark(A.after(got[1][2]).activation(gg[0:rows, :], got[1][1][0:rows, :], ACT.Gelu,
                                                         bias=col(k, "b1g", HT * layer + ft, rows)))
                k.banks.release(got[1][0], t)
                t_h = V.mark(V.after(t, got[0][2]).scalar_tensor_tensor(
                    hd[0:rows, ft, :], got[0][1][0:rows, :], col(k, "b1a", HT * layer + ft, rows), gg[0:rows, :],
                    ALU.add, ALU.mult))
                k.banks.release(got[0][0], t_h)
                gl.release(jg, t_h)
            if pending:
                second(*pending)
            pending = (g, jh, hd, t_h)
        second(*pending)
        if layer == 0:
            k.ch = to_channels(k, k.x_tok, k.x_ch, ready)
        k.barrier()


STAGES = [rwkv, bitnet, experts, linear_attention, cross_attention, windowed]


def store(k):
    sem = k.sem("stored")
    k.sp.after(*[k.tok[i] for i in range(TILES)])
    k.nc.sync.dma_start(k.dram["out"].rearrange("(n p) d -> p n d", p=P), k.x_tok[:]).then_inc(sem, 16)
    k.nc.sync.wait_ge(sem, 16)


def build(nc, dram, stages=range(6)):
    dram["regroup"] = nc.dram_tensor("regroup", (B, N0, N0, H0, T // N0), F32, kind="Internal").ap()
    k = Core(nc, dram)
    with k.ctx:
        setup(k)
        for n in stages:
            STAGES[n](k)
        store(k)


def host_layout(inp):
    f = lambda n: np.asarray(inp[n])
    chan = lambda a: np.asarray(a).reshape(-1, P).T

    def hidden(a):
        z = np.zeros((HT * P,), a.dtype)
        z[:HID] = a
        return z.reshape(HT, P).T

    b1 = f("L1_ffn_b1")
    cols = {
        "maa_k": chan(f("L0_attn_time_maa_k")), "maa_v": chan(f("L0_attn_time_maa_v")),
        "maa_r": chan(f("L0_attn_time_maa_r")), "maa_g": chan(f("L0_attn_time_maa_g")),
        "decay": chan(np.repeat(f("L0_attn_time_decay"), N0)),
        "b_d2v": chan(f("L0_xattn_b_d2v")), "b_img": chan(f("L0_xattn_b_img")), "b_txt": chan(f("L0_xattn_b_txt")),
        "b_att0": chan(f("L0_xattn_b_att0")), "b_att1": chan(f("L0_xattn_b_att1")), "b_f1": chan(f("L0_xattn_b_f1")),
        "moe_gamma": chan(f("L0_ffn_gamma")), "moe_beta": chan(f("L0_ffn_beta")), "moe_b1": chan(f("L0_ffn_b1")),
        "la_bq": chan(f("L1_attn_b_qkv")[:D]), "xa_bq": chan(f("L1_xattn_bq")), "xa_bk": chan(f("L1_xattn_bk")),
        "lg": chan(f("L1_ffn_ln_g")), "lb": chan(f("L1_ffn_ln_b")),
        "b1a": np.concatenate([hidden(b1[l, :HID]) for l in range(2)], 1),
        "b1g": np.concatenate([hidden(b1[l, HID:]) for l in range(2)], 1),
    }
    rows = {
        "decay": f("L0_attn_time_decay"), "faaaa": f("L0_attn_time_faaaa"), "ln_g": f("L0_attn_ln_g"),
        "ln_b": f("L0_attn_ln_b"), "b_att0": f("L0_xattn_b_att0"), "b_att1": f("L0_xattn_b_att1"),
        "b_f2": f("L0_xattn_b_f2"), "la_bkv": f("L1_attn_b_qkv")[D:], "la_bproj": f("L1_attn_b_proj"),
        "la_gamma": f("L1_attn_gamma"), "la_beta": f("L1_attn_beta"), "xa_bv": f("L1_xattn_bv"),
        "xa_bo": f("L1_xattn_bo"), "q_scale": f("L1_ffn_q_scale").reshape(-1),
        "k_scale": f("L1_ffn_k_scale").reshape(-1), "b2": f("L1_ffn_b2").reshape(-1),
    }
    x = f("x").reshape(NTOK, D)
    return {
        "const": shape_constants(), "rotary": rotary_tables(), "mask": window_mask(),
        "cols": np.concatenate([cols[n] for n, _ in COLS], 1), "rows": np.concatenate([rows[n] for n, _ in ROWS]),
        "x": x, "xT": x.T, "ctxT": f("ctx_768").transpose(2, 0, 1),
        **{"w_%sT" % n: f("L0_attn_w_" + n).T for n in "rkvgo"},
        **{"bn_" + n: f("L0_xattn_W_" + n).T for n in ("d2v", "img", "txt", "att0", "att1", "f1", "f2")},
        "moe_wg": f("L0_ffn_Wg"), "moe_w1": f("L0_ffn_W1"), "moe_w2": f("L0_ffn_W2"), "moe_b2": f("L0_ffn_b2"),
        "la_qkvT": f("L1_attn_W_qkv").T, "la_projT": f("L1_attn_W_proj").T,
        "xa_q": f("L1_xattn_Wq"), "xa_k": f("L1_xattn_Wk"), "xa_v": f("L1_xattn_Wv"), "xa_o": f("L1_xattn_Wo"),
        "wqkv": f("L1_ffn_wqkv"), "wo": f("L1_ffn_wo"), "w1": f("L1_ffn_w1"), "w2": f("L1_ffn_w2"),
    }


def kernel(**inputs):
    import concourse.bacc as bacc
    from concourse.bass_utils import run_bass_kernel_spmd

    nc = bacc.Bacc("TRN2", target_bir_lowering=False, num_devices=1)
    arrays = {n: np.ascontiguousarray(a) for n, a in host_layout(inputs).items()}
    dram = {n: nc.dram_tensor("in_" + n, a.shape, mybir.dt.from_np(a.dtype), kind="ExternalInput").ap()
            for n, a in arrays.items()}
    dram["out"] = nc.dram_tensor("out", (NTOK, D), F32, kind="ExternalOutput").ap()
    build(nc, dram)
    r = run_bass_kernel_spmd(nc, [{"in_" + n: a for n, a in arrays.items()}], core_ids=[0])
    return r.results[0]["out"].reshape(B, T, D)
```

```python
from contextlib import ExitStack

import numpy as np
import concourse.bass as bass
from concourse import mybir

F32 = mybir.dt.float32
BF16 = mybir.dt.bfloat16
ALU = mybir.AluOpType
ACT = mybir.ActivationFunctionType
AX = mybir.AxisListType

P = 128
B, T, D = 4, 512, 256
NTOK = B * T
TILES = NTOK // P
TPB = T // P
HALVES = D // P
BANK = 512
S2, DC = 1601, 192
CP = DC // 2
KT = -(-S2 // P)
KLAST = S2 - (KT - 1) * P
ROUND = 12582912.0
NE, FF = 8, 1024
H0, N0 = 16, 16
HX, NX = 8, 32
HL, NL = 8, 64
INNER = HL * NL
HID = int(D * 4 * 2 / 3)
HT = -(-HID // P)
HLAST = HID - (HT - 1) * P
MASKED = -1e30


COLS = [("maa_k", 2), ("maa_v", 2), ("maa_r", 2), ("maa_g", 2), ("decay", 2),
        ("b_d2v", 2), ("b_img", 2), ("b_txt", 2), ("b_att0", 1), ("b_att1", 1), ("b_f1", 8),
        ("moe_gamma", 16), ("moe_beta", 16), ("moe_b1", 64), ("la_bq", 2), ("xa_bq", 2), ("xa_bk", 2),
        ("lg", 4), ("lb", 4), ("b1a", 2 * HT), ("b1g", 2 * HT)]
ROWS = [("decay", H0), ("faaaa", H0), ("ln_g", D), ("ln_b", D), ("b_att0", P), ("b_att1", P),
        ("b_f2", D), ("la_bkv", 2 * D), ("la_bproj", D), ("la_gamma", D), ("la_beta", D),
        ("xa_bv", D), ("xa_bo", D), ("q_scale", 2 * NL), ("k_scale", 2 * NL), ("b2", 2 * D)]
CONSTS = [("ident", P), ("expo", P), ("later", P), ("diag16", P), ("ramp", P), ("head16", 8),
          ("head32", 4), ("left", 1), ("ones", P), ("lower", 64), ("half64", 2), ("fold", NX + 1)]


def offsets(items):
    at, n = {}, 0
    for name, width in items:
        at[name] = (n, width)
        n += width
    return at, n


COL_AT, NCOL = offsets(COLS)
ROW_AT, NROW = offsets(ROWS)
CONST_AT, NCONST = offsets(CONSTS)


def shape_constants():
    c = np.zeros((P, NCONST), np.float32)

    def put(name, a):
        o, w = CONST_AT[name]
        c[:, o:o + w] = a

    j, t = np.arange(P)[:, None], np.arange(P)[None, :]
    put("ident", j == t)
    put("expo", np.maximum(t - j - 1, 0))
    put("later", t > j)
    put("diag16", j // N0 == t // N0)
    put("ramp", t + 0 * j)
    put("head16", j // N0 == np.arange(8)[None, :])
    put("head32", j // NX == np.arange(4)[None, :])
    put("left", P - 1 - j)
    put("ones", 1.0)
    e = np.arange(NE)
    put("lower", np.tile((e[None, :] < e[:, None]).astype(np.float32).reshape(1, 64), (P, 1)))
    put("half64", j // NL == np.arange(2)[None, :])
    put("fold", j % (NX + 1) == np.arange(NX + 1)[None, :])
    return c


def rotary_tables():
    f32 = np.float32
    half = np.arange(0, NL, 2, dtype=f32)
    inv = (f32(1.0) / f32(10000.0) ** (half / f32(NL))).astype(f32)
    t = np.arange(T, dtype=f32)
    fr = (t[:, None] * inv[None, :]).astype(f32)
    fr = np.concatenate([fr, fr], -1)
    base = ((half + f32(0.4 * NL)) / f32(1.4 * NL)).astype(f32)
    power = ((t - T // 2) / f32(P // 2)).astype(f32)
    sc = (base[None, :] ** power[:, None]).astype(f32)
    sc = np.concatenate([sc, sc], -1)
    sign = np.where(np.arange(NL) < NL // 2, -1.0, 1.0).astype(f32)
    cos, sin = np.cos(fr).astype(f32), np.sin(fr).astype(f32) * sign
    tab = np.stack([cos * sc, sin * sc, cos / sc, sin / sc], 1).astype(f32)
    return np.ascontiguousarray(tab.reshape(TPB, P, 4, NL).transpose(1, 0, 2, 3))


def window_mask():
    i, j = np.arange(P)[:, None], np.arange(2 * P)[None, :]
    return np.where((j >= i) & (j <= i + P), 0.0, MASKED).astype(np.float32)


class Queue:

    def __init__(self, engine, sem):
        self.engine, self.sem, self.count, self.seen = engine, sem, 0, {}

    def after(self, *tokens):
        need = {}
        for token in tokens:
            if token is not None:
                need[token[0]] = max(need.get(token[0], 0), token[1])
        for sem, value in need.items():
            if self.seen.get(sem, 0) < value:
                self.engine.wait_ge(sem, value)
                self.seen[sem] = value
        return self.engine

    def mark(self, instruction):
        instruction.then_inc(self.sem, 1)
        self.count += 1
        return self.sem, self.count

    def last(self):
        return (self.sem, self.count) if self.count else None


class Ring:

    def __init__(self, slots):
        self.slots = slots
        self.idle = [(i, ()) for i in range(len(slots))]
        self.readers = [()] * len(slots)

    def take(self, queue):
        i, tokens = self.idle.pop(0)
        self.readers[i] = tokens
        queue.after(*tokens)
        return i, self.slots[i]

    def release(self, i, *tokens):
        self.idle.append((i, tokens))


class Core:
    def __init__(self, nc, dram):
        self.nc, self.dram = nc, dram
        self.ctx = ExitStack()
        self.nsem = 0
        self.pe = Queue(nc.tensor, self.sem("pe_done"))
        self.dve = Queue(nc.vector, self.sem("dve_done"))
        self.act = Queue(nc.scalar, self.sem("act_done"))
        self.pool = Queue(nc.gpsimd, self.sem("pool_done"))
        self.sp = Queue(nc.sync, self.sem("sp_done"))
        self.loads = []
        self.tensors = 0

    def sem(self, name):
        self.nsem += 1
        return self.ctx.enter_context(self.nc.semaphore(name))

    def sb(self, ctx, name, shape, dt=F32):
        return ctx.enter_context(self.nc.sbuf_tensor(name, list(shape), dt))

    def load(self, name, *pairs, after=()):
        sem = self.sem("loaded_" + name)
        self.sp.after(*after)
        for dst, src in pairs:
            self.nc.sync.dma_start(dst, src).then_inc(sem, 16)
        token = (sem, 16 * len(pairs))
        self.loads.append(token)
        return token

    def barrier(self):
        every = [q.last() for q in (self.pe, self.dve, self.act, self.pool)] + self.loads
        self.loads = []
        for q in (self.pe, self.dve, self.act, self.pool, self.sp):
            q.after(*every)

    def matmuls(self, out, pairs, *after, first=True, last=True, skip=False):
        eng = self.pe.after(*after)
        for n, (lhsT, rhs) in enumerate(pairs):
            ins = eng.matmul(out, lhsT, rhs, start=first and n == 0, stop=last and n == len(pairs) - 1,
                             skip_group_check=skip)
        return self.pe.mark(ins)


def setup(k):
    nc, ctx = k.nc, k.ctx
    k.psum = ctx.enter_context(nc.psum_tensor("psum", [P, 8, BANK], F32))
    k.x_tok = k.sb(ctx, "x_tok", [P, TILES, D])
    k.x_ch = k.sb(ctx, "x_ch", [P, HALVES, NTOK])
    k.const = k.sb(ctx, "const", [P, NCONST])
    k.cols = k.sb(ctx, "cols", [P, NCOL])
    k.rows = k.sb(ctx, "rows", [P, NROW])
    k.stats = k.sb(ctx, "ln_stats", [P, TILES, 6])
    k.mv = k.sb(ctx, "ln_mean_var", [P, TILES, 2])
    k.std = k.sb(ctx, "ln_std", [P, TILES])
    k.rstd = k.sb(ctx, "ln_rstd", [P, TILES])
    k.eps = k.sb(ctx, "eps", [P, 4])
    k.banks = Ring([k.psum[:, 4 + n, :] for n in range(4)])
    k.score_free = ()
    for n, v in enumerate((1e-5, 1e-6, 64e-5, 0.0)):
        t = k.dve.mark(nc.vector.memset(k.eps[:, n:n + 1], v))
    k.t_eps = t
    k.t_param = k.load("params", (k.const[:], k.dram["const"]), (k.cols[:], k.dram["cols"]),
                       (k.rows[:], k.dram["rows"].partition_broadcast(P)))
    k.t_x = t_x = k.load("x", (k.x_tok[:], k.dram["x"].rearrange("(n p) d -> p n d", p=P)),
                   (k.x_ch[:], k.dram["xT"].rearrange("(h p) t -> p h t", p=P)))
    k.tok, k.ch = {i: t_x for i in range(TILES)}, {g: [t_x] for g in range(4)}


def const(k, name, rows=P):
    o, w = CONST_AT[name]
    return k.const[0:rows, o:o + w]


def col(k, name, n=0, rows=P):
    o, _ = COL_AT[name]
    return k.cols[0:rows, o + n:o + n + 1]


def row(k, name, a=0, b=None):
    o, w = ROW_AT[name]
    return k.rows[:, o + a:o + (w if b is None else b)]


def evacuate(k, n, out, bank, *after):
    if n % 2:
        return k.dve.mark(k.dve.after(*after).tensor_copy(out, bank))
    return k.act.mark(k.act.after(*after).copy(out, bank))


def layer_norm(k, src, dst, ready, eps_col, tiles=range(TILES)):
    done = {}
    tiles = list(tiles)
    for g in range(0, len(tiles), 4):
        group = tiles[g:g + 4]
        a, b = group[0], group[-1] + 1
        for i in group:
            t = k.dve.mark(k.dve.after(ready[i]).bn_stats(k.stats[:, i, :], src[:, i, :]))
        k.dve.after(t)
        for i in group:
            t = k.dve.mark(k.nc.vector.bn_aggr(k.mv[:, i, :], k.stats[:, i, :]))
        t = k.act.mark(k.act.after(t, k.t_eps, k.t_param).activation(
            k.std[:, a:b], k.mv[:, a:b, 1], ACT.Sqrt, bias=k.eps[:, eps_col:eps_col + 1]))
        t = k.dve.mark(k.dve.after(t).reciprocal(k.rstd[:, a:b], k.std[:, a:b]))
        k.dve.after(t)
        for i in group:
            done[i] = k.dve.mark(k.nc.vector.tensor_scalar(
                dst[:, i, :], src[:, i, :], k.mv[:, i, 0:1], k.rstd[:, i:i + 1],
                ALU.subtract, ALU.mult))
    return done


def to_channels(k, src, dst, ready, scale=None, bias=None, free=(), groups=range(4)):
    done = {}
    for g in groups:
        tokens = []
        for h in range(HALVES):
            i, bank = k.banks.take(k.pe)
            k.pe.after(k.t_param, *[ready[4 * g + m] for m in range(4)])
            for m in range(4):
                ins = k.nc.tensor.transpose(bank[:, m * P:(m + 1) * P],
                                            src[:, 4 * g + m, h * P:(h + 1) * P], const(k, "ident"))
            t = k.pe.mark(ins)
            out = dst[:, h, g * BANK:(g + 1) * BANK]
            if scale is None:
                t = evacuate(k, h, out, bank, t, *free)
            else:
                t = k.act.mark(k.act.after(t, *free).activation(out, bank, ACT.Identity,
                                                                scale=scale(h), bias=bias(h)))
            k.banks.release(i, t)
            tokens.append(t)
        done[g] = tokens
    return done


def post_norm(k, ready):
    k.tok = layer_norm(k, k.x_tok, k.x_tok, ready, 0)
    k.ch = to_channels(k, k.x_tok, k.x_ch, k.tok)


def rwkv(k):
    nc = k.nc
    with ExitStack() as ctx:
        sb = lambda name, shape, dt=F32: k.sb(ctx, name, shape, dt)
        w = {n: sb("w_" + n, [P, HALVES, D]) for n in "rkvgo"}
        t_w = k.load("rwkv_w", *[(w[n][:], k.dram["w_%sT" % n].rearrange("(h p) o -> p h o", p=P)) for n in "rkvgo"])
        rate_row, rate_col = sb("rate_row", [P, H0]), sb("rate_col", [P, 2])
        nrate_row, nrate_col = sb("nrate_row", [P, H0]), sb("nrate_col", [P, 2])
        wmat = sb("decay_mask", [P, H0, P])
        wkey = sb("key_decay", [P, H0])
        wquery = sb("query_decay", [P, 2, P])
        wstate = sb("state_decay", [P, 2])
        xx = sb("x_step", [P, HALVES, NTOK])

        A, V = k.act, k.dve
        t = A.mark(A.after(k.t_param).activation(rate_row[:], row(k, "decay"), ACT.Exp))
        o, _ = COL_AT["decay"]
        t = A.mark(nc.scalar.activation(rate_col[:], k.cols[:, o:o + 2], ACT.Exp))
        V.after(t)
        V.mark(nc.vector.tensor_scalar(nrate_row[:], rate_row[:], -1.0, None, ALU.mult))
        t = V.mark(nc.vector.tensor_scalar(nrate_col[:], rate_col[:], -1.0, None, ALU.mult))
        A.after(t)
        for h in range(H0):
            t = A.mark(nc.scalar.activation(wmat[:, h, :], const(k, "expo"), ACT.Exp,
                                            scale=nrate_row[:, h:h + 1]))
        for c in range(2):
            A.mark(nc.scalar.activation(wquery[:, c, :], const(k, "ramp"), ACT.Exp, scale=nrate_col[:, c:c + 1]))
        A.mark(nc.scalar.activation(wstate[:], nrate_col[:], ACT.Exp, scale=float(P)))
        t2 = A.mark(nc.scalar.activation(wkey[:], nrate_row[:], ACT.Exp, scale=const(k, "left")))
        t = V.mark(V.after(t).tensor_tensor(wmat[:], wmat[:], const(k, "later").unsqueeze(1).to_broadcast([P, H0, P]), ALU.mult))
        V.after(t)
        for h in range(H0):
            t = V.mark(nc.vector.scalar_tensor_tensor(wmat[:, h, :], const(k, "ident"), row(k, "faaaa", h, h + 1),
                                                      wmat[:, h, :], ALU.mult, ALU.add))
        t_tab = (t, t2)

        V.after(k.t_x)
        xv = k.x_ch[:].rearrange("p h (b t) -> p (h b) t", t=T)
        xxv = xx[:].rearrange("p h (b t) -> p (h b) t", t=T)
        V.mark(nc.vector.tensor_tensor(xxv[:, :, 1:T], xv[:, :, 0:T - 1], xv[:, :, 1:T], ALU.subtract))
        t_xx = V.mark(nc.vector.tensor_scalar(xxv[:, :, 0:1], xv[:, :, 0:1], -1.0, None, ALU.mult))

        mixes = Ring([sb("mix%d" % n, [P, HALVES, T]) for n in range(3)])
        two = lambda name, shape: Ring([sb("%s%d" % (name, n), shape) for n in range(2)])
        r_heads = two("r_heads", [P, 8, BANK])
        r_state = two("r_state", [P, HALVES, T])
        r_ch, k_ch = two("r_ch", [P, HALVES, T]), two("k_ch", [P, HALVES, T])
        k_tok, v_tok, gate, y_all = (two(n, [P, TPB, D]) for n in ("k_tok", "v_tok", "gate", "y_all"))
        scores = two("a_masked", [P, 4, P])
        state = [sb("state%d" % n, [P, HALVES, P]) for n in range(2)]
        outer = sb("outer", [P, HALVES, P])
        z_ch = two("z_ch", [P, HALVES, T])
        gsum, gvar = two("g_sum", [P, TPB * H0]), two("g_var", [P, TPB * H0])
        zsq = sb("z_sq", [P, TPB * D])
        t_zsq = None
        ready = {}

        for b in range(B):
            cols_b = slice(b * T, (b + 1) * T)

            def mix(name):
                i, m = mixes.take(V)
                V.after(t_xx)
                for c in range(HALVES):
                    t = V.mark(nc.vector.scalar_tensor_tensor(m[:, c, :], xx[:, c, cols_b], col(k, "maa_" + name, c),
                                                              k.x_ch[:, c, cols_b], ALU.mult, ALU.add))
                return i, m, t

            def project_channels(m, t_m, weight, ring):
                j, out = ring.take(A)
                V.after(*ring.readers[j])
                for c in range(HALVES):
                    i, bank = k.banks.take(k.pe)
                    t = k.matmuls(bank, [(weight[:, h, c * P:(c + 1) * P], m[:, h, :]) for h in range(HALVES)], t_m, t_w)
                    t = A.mark(A.after(t).copy(out[:, c, :], bank))
                    k.banks.release(i, t)
                return j, out, t

            def project_tokens(m, t_m, weight, finish):
                for pair in range(TPB // 2):
                    i, bank = k.banks.take(k.pe)
                    k.pe.after(t_m, t_w)
                    for s in range(2):
                        tl = 2 * pair + s
                        for h in range(HALVES):
                            ins = nc.tensor.matmul(bank[:, s * D:(s + 1) * D], m[:, h, tl * P:(tl + 1) * P],
                                                   weight[:, h, :], start=(h == 0), stop=(h == HALVES - 1))
                    t = k.pe.mark(ins)
                    t = finish(pair, bank, t)
                    k.banks.release(i, t)
                return t

            im, m, t_m = mix("r")
            jr, rc, t_r = project_channels(m, t_m, w["r"], r_ch)
            mixes.release(im, t_r)
            jrs, rs = r_state.take(V)
            V.after(t_r, *t_tab)
            for c in range(HALVES):
                t_rs = V.mark(nc.vector.tensor_tensor(
                    rs[:, c, :].rearrange("p (n t) -> p n t", t=P), rc[:, c, :].rearrange("p (n t) -> p n t", t=P),
                    wquery[:, c, :].unsqueeze(1).to_broadcast([P, TPB, P]), ALU.mult))
            im, m, t_m = mix("k")
            jk, kc, t_k = project_channels(m, t_m, w["k"], k_ch)
            jkt, kt = k_tok.take(V)

            def finish_k(pair, bank, t):
                wk = wkey[:].unsqueeze(1).unsqueeze(3).to_broadcast([P, 2, H0, N0])
                return V.mark(V.after(t, *t_tab).tensor_tensor(
                    kt[:, 2 * pair:2 * pair + 2, :].rearrange("p s (h n) -> p s h n", n=N0),
                    bank.rearrange("p (s h n) -> p s h n", s=2, n=N0), wk, ALU.mult))
            t_kt = project_tokens(m, t_m, w["k"], finish_k)
            mixes.release(im, t_kt)
            im, m, t_m = mix("v")
            jv, vt = v_tok.take(A)
            t_v = project_tokens(m, t_m, w["v"], lambda pair, bank, t: A.mark(
                A.after(t).copy(vt[:, 2 * pair:2 * pair + 2, :].rearrange("p s d -> p (s d)"), bank)))
            mixes.release(im, t_v)
            im, m, t_m = mix("g")
            jg, gt = gate.take(A)
            t_g = project_tokens(m, t_m, w["g"], lambda pair, bank, t: A.mark(
                A.after(t).activation(gt[:, 2 * pair:2 * pair + 2, :].rearrange("p s d -> p (s d)"), bank, ACT.Silu)))
            mixes.release(im, t_g)

            jy, ya = y_all.take(A)
            V.after(*y_all.readers[jy])
            t = V.mark(V.after(k.pe.last()).memset(state[0][:], 0.0))
            t_state = t
            heads = []
            for c in range(HALVES):
                jh, rh = r_heads.take(k.pool)
                k.pool.after(t_r)
                t_h = k.pool.mark(nc.gpsimd.tensor_tensor(
                    rh[:], rc[:, c, :].unsqueeze(1).to_broadcast([P, 8, BANK]),
                    const(k, "head16").unsqueeze(2).to_broadcast([P, 8, BANK]), ALU.mult))
                heads.append((jh, rh, t_h))
            r_ch.release(jr, t_rs, t_h)
            for c in range(TPB):
                tl = slice(c * P, (c + 1) * P)
                old, new = state[c % 2], state[(c + 1) % 2]
                iy, ybank = k.banks.take(k.pe)
                k.pe.after(t_state, t_rs)
                for h in range(HALVES):
                    nc.tensor.matmul(ybank[:, h * P:(h + 1) * P], rs[:, h, tl], old[:, h, :],
                                     start=(h == 0), stop=False, skip_group_check=True)
                for q in range(4):
                    h = q // 2
                    i, bank = k.banks.take(k.pe)
                    t = k.matmuls(bank, [(kc[:, h, tl], heads[h][1][:, 4 * (q % 2):4 * (q % 2) + 4, tl])],
                                  t_k, heads[h][2])
                    ia, am = scores.take(V)
                    t = V.mark(V.after(t, *t_tab).tensor_tensor(am[:], bank.rearrange("p (a t) -> p a t", t=P),
                                                                wmat[:, 4 * q:4 * q + 4, :], ALU.mult))
                    k.banks.release(i, t)
                    k.pe.after(t, t_v)
                    for a in range(4):
                        hd = 4 * q + a
                        ins = nc.tensor.matmul(ybank[:, hd * N0:(hd + 1) * N0], am[:, a, :],
                                               vt[:, c, hd * N0:(hd + 1) * N0], start=False, stop=False,
                                               skip_group_check=True)
                    t_y = k.pe.mark(ins)
                    scores.release(ia, t_y)
                t = A.mark(A.after(t_y).copy(ya[:, c, :], ybank[:, 0:D]))
                k.banks.release(iy, t)
                t_ya = t
                if c < TPB - 1:
                    i, bank = k.banks.take(k.pe)
                    k.pe.after(t_kt, t_v)
                    for h in range(HALVES):
                        hs = slice(h * P, (h + 1) * P)
                        ins = nc.tensor.matmul(bank[:, hs], kt[:, c, hs], vt[:, c, hs], start=True, stop=True)
                    t = k.pe.mark(ins)
                    t = V.mark(V.after(t).tensor_tensor(outer[:], bank[:, 0:D].rearrange("p (h v) -> p h v", v=P),
                                                        const(k, "diag16").unsqueeze(1).to_broadcast([P, 2, P]), ALU.mult))
                    k.banks.release(i, t)
                    V.after(t)
                    for h in range(HALVES):
                        t_state = V.mark(nc.vector.scalar_tensor_tensor(new[:, h, :], old[:, h, :], wstate[:, h:h + 1],
                                                                        outer[:, h, :], ALU.mult, ALU.add))
            last_y = k.pe.last()
            r_state.release(jrs, last_y)
            k_ch.release(jk, last_y)
            k_tok.release(jkt, last_y)
            v_tok.release(jv, last_y)
            for jh, _, _ in heads:
                r_heads.release(jh, last_y)

            G = TPB * H0
            ig, gs = gsum.take(V)
            iv, gv = gvar.take(V)
            yg = ya[:].rearrange("p n (h c) -> p (n h) c", c=N0)
            sq = zsq[:].rearrange("p (g c) -> p g c", c=N0)
            wide = lambda a: a[:].unsqueeze(2).to_broadcast([P, G, N0])
            t = V.mark(V.after(t_ya).tensor_reduce(gs[:], yg, AX.X, ALU.add))
            t = V.mark(V.after(t).tensor_scalar(gs[:], gs[:], 1.0 / N0, None, ALU.mult))
            t = V.mark(V.after(t).tensor_tensor(yg, yg, wide(gs), ALU.subtract))
            t = V.mark(V.after(t).tensor_tensor(sq, yg, yg, ALU.mult))
            t = V.mark(V.after(t).tensor_reduce(gv[:], sq, AX.X, ALU.add))
            t = A.mark(A.after(t, k.t_eps).activation(gv[:], gv[:], ACT.Sqrt, scale=1.0 / N0, bias=k.eps[:, 2:3]))
            t = V.mark(V.after(t).reciprocal(gs[:], gv[:]))
            t = V.mark(V.after(t).tensor_tensor(yg, yg, wide(gs), ALU.mult))
            gsum.release(ig, t)
            gvar.release(iv, t)
            over = lambda name: row(k, name).unsqueeze(1).to_broadcast([P, TPB, D])
            t = k.pool.mark(k.pool.after(t).tensor_tensor(ya[:], ya[:], over("ln_g"), ALU.mult))
            t = k.pool.mark(k.pool.after(t).tensor_tensor(ya[:], ya[:], over("ln_b"), ALU.add))
            t = k.pool.mark(k.pool.after(t, t_g).tensor_tensor(ya[:], ya[:], gt[:], ALU.mult))
            gate.release(jg, t)
            t_z = t
            jz, zc = z_ch.take(k.act)
            V.after(*z_ch.readers[jz])
            for h in range(HALVES):
                i, bank = k.banks.take(k.pe)
                k.pe.after(t_z)
                for n in range(TPB):
                    ins = nc.tensor.transpose(bank[:, n * P:(n + 1) * P], ya[:, n, h * P:(h + 1) * P], const(k, "ident"))
                t = k.pe.mark(ins)
                t = A.mark(A.after(t).copy(zc[:, h, :], bank))
                k.banks.release(i, t)
            y_all.release(jy, t)
            t_zc = t
            for n in range(TPB):
                i, bank = k.banks.take(k.pe)
                t = k.matmuls(bank[:, 0:D], [(zc[:, h, n * P:(n + 1) * P], w["o"][:, h, :]) for h in range(HALVES)], t_zc)
                tile = b * TPB + n
                t = V.mark(V.after(t, k.t_x).tensor_tensor(k.x_tok[:, tile, :], bank[:, 0:D], k.x_tok[:, tile, :], ALU.add))
                k.banks.release(i, t)
                ready[tile] = t
            z_ch.release(jz, k.pe.last())
        k.barrier()
        post_norm(k, ready)
        k.barrier()


def attention(k, ctx, tag, items, scale, dv):
    nc, V, A = k.nc, k.dve, k.act
    probs = Ring([k.sb(ctx, "probs%d_%s" % (n, tag), [P, S2]) for n in range(2)])
    turned = Ring([k.sb(ctx, "probs_t%d_%s" % (n, tag), [P, KT, P]) for n in range(2)])
    small = [k.sb(ctx, "softmax%d_%s" % (n, tag), [P, len(items)]) for n in range(4)]
    maxes, nmax, sums, rsums = small
    scores = k.psum[:, 0:4, :].rearrange("p b c -> p (b c)")

    def front(n, it):
        k.pe.after(*k.score_free, *it["ready"])
        for c0 in range(0, S2, BANK):
            c1 = min(c0 + BANK, S2)
            ins = nc.tensor.matmul(scores[:, c0:c1], it["query"], it["keys"](c0, c1), start=True, stop=True)
        t = k.pe.mark(ins)
        if it.get("scored"):
            it["scored"](t)
        m = slice(n, n + 1)
        t = V.mark(V.after(t).tensor_reduce(maxes[:, m], scores[:, 0:S2], AX.X, ALU.max))
        t = V.mark(V.after(t).tensor_scalar(nmax[:, m], maxes[:, m], -scale, None, ALU.mult))
        ip, pr = probs.take(A)
        t = A.mark(A.after(t).activation(pr[:], scores[:, 0:S2], ACT.Exp, bias=nmax[:, m], scale=scale,
                                         accum_out=sums[:, m]))
        k.score_free = (t,)
        t_r = V.mark(V.after(t).reciprocal(rsums[:, m], sums[:, m]))
        return ip, pr, t, t_r

    def back(n, it, ip, pr, t_exp, t_rsum):
        io, obank = k.banks.take(k.pe)
        it_, pt = turned.take(A)
        V.after(*turned.readers[it_])
        k.pe.after(t_exp)
        copied = {}

        def turn(g):
            i, bank = k.banks.take(k.pe)
            tiles = range(4 * g, min(4 * g + 4, KT))
            for kt in tiles:
                rows = P if kt < KT - 1 else KLAST
                ins = nc.tensor.transpose(bank[0:rows, (kt % 4) * P:(kt % 4 + 1) * P],
                                          pr[:, kt * P:kt * P + rows], const(k, "ident"))
            t = k.pe.mark(ins)
            rows, cnt = (P, 4) if len(tiles) == 4 else (KLAST, 1)
            t = evacuate(k, g % 2, pt[0:rows, 4 * g:4 * g + cnt, :].rearrange("p a q -> p (a q)"),
                         bank[0:rows, 0:cnt * P], t)
            k.banks.release(i, t)
            copied[g] = t

        def product(g):
            k.pe.after(copied[g])
            for kt in range(4 * g, min(4 * g + 4, KT)):
                rows = P if kt < KT - 1 else KLAST
                ins = nc.tensor.matmul(obank[:, 0:dv], pt[0:rows, kt, :], it["value"](kt, rows),
                                       start=(kt == 0), stop=(kt == KT - 1))
            return ins

        turn(0)
        turn(1)
        turn(2)
        product(0)
        turn(3)
        probs.release(ip, k.pe.last())
        product(1)
        product(2)
        t = k.pe.mark(product(3))
        turned.release(it_, t)
        it["finish"](obank, io, rsums[:, n:n + 1], (t, t_rsum))

    prev = None
    for n, it in enumerate(items):
        now = (n, it) + front(n, it)
        if prev:
            back(*prev)
        prev = now
    back(*prev)


def bitnet(k):
    nc, V, A = k.nc, k.dve, k.act
    KEYS = B * S2
    CH = [(c, min(c + BANK, KEYS)) for c in range(0, KEYS, BANK)]
    WID = {"d2v": 0, "img": 1, "txt": 2, "att0": 3, "att1": 4, "f1": 5, "f2": 6}
    with ExitStack() as outer:
        wsum = k.sb(outer, "w_abs_sum", [P, 8])
        wscale, wthr, wnthr = (k.sb(outer, n, [P, 8]) for n in ("w_scale", "w_thr", "w_nthr"))
        mcols = k.sb(outer, "max_cols", [P, 40])
        mrow, mone = k.sb(outer, "max_row", [1, P]), k.sb(outer, "max_one", [1, 1])
        iscale, inv, s_out = (k.sb(outer, n, [P, 12]) for n in ("i_scale", "i_inv", "out_scale"))
        fused = k.sb(outer, "fused", [P, HALVES, NTOK])
        avg = k.sb(outer, "avg_img", [P, HALVES * B])
        t_zero = V.mark(nc.vector.memset(wsum[:], 0.0))
        t_zero = V.mark(nc.vector.memset(mcols[:], 0.0))

        def ternary(ctx, names, shapes, space=None):
            q = {}
            tmp = k.sb(ctx, "tern_tmp_" + names[0], [P, max(c * o for _, c, o in shapes)], BF16)
            raw, at = {}, 0
            for n, (_, c, o) in zip(names, shapes):
                if space is None:
                    raw[n] = k.sb(ctx, "bn_raw_" + n, [P, c, o])
                else:
                    raw[n] = space[:, at:at + c * o].rearrange("p (c o) -> p c o", o=o)
                at += c * o
            t_l = k.load("bn_" + names[0], *[
                (raw[n][0:p], k.dram["bn_" + n].rearrange("(c p) o -> p c o", p=p)) for n, (p, c, o) in zip(names, shapes)])
            V.after(t_l, t_zero)
            for n, (p, c, o) in zip(names, shapes):
                j = WID[n]
                t = V.mark(nc.vector.tensor_reduce(wsum[0:p, j:j + 1], raw[n][0:p], AX.XY, ALU.add,
                                                   apply_absolute_value=True))
            i, bank = k.banks.take(k.pe)
            t = k.matmuls(bank[:, 0:8], [(const(k, "ones"), wsum[:])], t, k.t_param)
            V.after(t)
            for n, (p, c, o) in zip(names, shapes):
                j = slice(WID[n], WID[n] + 1)
                t = V.mark(nc.vector.tensor_scalar(wscale[:, j], bank[:, j], 1.0 / (p * c * o), 1e-5, ALU.mult, ALU.max))
            k.banks.release(i, t)
            V.after(t)
            a, b = WID[names[0]], WID[names[-1]] + 1
            V.mark(nc.vector.tensor_scalar(wthr[:, a:b], wscale[:, a:b], 0.5, None, ALU.mult))
            t = V.mark(nc.vector.tensor_scalar(wnthr[:, a:b], wscale[:, a:b], -0.5, None, ALU.mult))
            for n, (p, c, o) in zip(names, shapes):
                j = slice(WID[n], WID[n] + 1)
                q[n] = k.sb(ctx, "bn_q_" + n, [P, c, o], BF16)
                low = tmp[0:p, 0:c * o].rearrange("p (c o) -> p c o", o=o)
                t = V.mark(V.after(t).tensor_scalar(low, raw[n][0:p], wnthr[0:p, j], None, ALU.is_lt))
                t = V.mark(V.after(t).scalar_tensor_tensor(q[n][0:p], raw[n][0:p], wthr[0:p, j], low,
                                                           ALU.is_gt, ALU.subtract))
            return q, t

        def input_scale(slot, ncol, *ready):
            s = slice(slot, slot + 1)
            t = V.mark(V.after(*ready).tensor_reduce(mcols[:, 39:40], mcols[:, 0:ncol], AX.X, ALU.max))
            i, bank = k.banks.take(k.pe)
            t = k.pe.mark(k.pe.after(t).transpose(bank[0:1, 0:P], mcols[:, 39:40], const(k, "ident")))
            t = V.mark(V.after(t).tensor_reduce(mone[:], bank[0:1, 0:P], AX.X, ALU.max))
            k.banks.release(i, t)
            i, bank = k.banks.take(k.pe)
            t = k.matmuls(bank[:, 0:1], [(const(k, "ones", 1), mone[:])], t)
            t = V.mark(V.after(t).tensor_scalar(iscale[:, s], bank[:, 0:1], 1e-8, 1.0 / 127.0, ALU.max, ALU.mult))
            k.banks.release(i, t)
            return V.mark(V.after(t).reciprocal(inv[:, s], iscale[:, s]))

        def out_scale(slot, wname, use, *ready):
            t = V.mark(V.after(*ready).tensor_tensor(s_out[:, use:use + 1], iscale[:, slot:slot + 1],
                                                     wscale[:, WID[wname]:WID[wname] + 1], ALU.mult))
            return t

        def quantize(slot, dst, src, rows, *ready):
            s = slice(slot, slot + 1)
            t = V.mark(V.after(*ready).tensor_scalar(src, src, inv[0:rows, s], ROUND, ALU.mult, ALU.add))
            return V.mark(V.after(t).tensor_scalar(dst, src, ROUND, None, ALU.subtract))

        with ExitStack() as ctx:
            big = k.sb(ctx, "ctx_f32", [P, KEYS + B * KT * P])
            q8 = k.sb(ctx, "ctx_q8", [P, HALVES, KEYS], BF16)
            wide = big[:, 0:HALVES * KEYS].rearrange("p (h s) -> p h s", h=HALVES)
            t_ctx = [k.load("ctx%d" % h, (wide[0:CP, h, :], k.dram["ctxT"].rearrange("c b s -> c (b s)")[h * CP:(h + 1) * CP, :]))
                     for h in range(HALVES)]
            q, t_q = ternary(ctx, ["d2v", "img", "txt", "att0", "att1"],
                             [(CP, 2, D), (P, 2, D), (P, 2, D), (P, 2, P), (P, 2, P)])

            for h in range(HALVES):
                t = V.mark(V.after(t_ctx[h], t_zero).tensor_reduce(mcols[0:CP, h:h + 1], wide[0:CP, h, :], AX.X, ALU.max,
                                                           apply_absolute_value=True))
            t_s = input_scale(0, 2, t)
            t_s = out_scale(0, "d2v", 0, t_s)
            V.after(t_s)
            ready = [quantize(0, q8[0:CP, h, :], wide[0:CP, h, :], CP) for h in range(HALVES)]

            def dense(wname, rows, use, bname, ready, n_max):
                n = 0
                for c0, c1 in CH:
                    for o in range(HALVES):
                        i, bank = k.banks.take(k.pe)
                        bank = bank[:, 0:c1 - c0]
                        t = k.matmuls(bank, [(q[wname][0:rows, h, o * P:(o + 1) * P], q8[0:rows, h, c0:c1])
                                             for h in range(HALVES)], *ready)
                        t = A.mark(A.after(t, *ready).activation(wide[:, o, c0:c1], bank, ACT.Identity,
                                                                 scale=s_out[:, use:use + 1], bias=col(k, bname, o)))
                        k.banks.release(i, t)
                        t = V.mark(V.after(t).tensor_reduce(mcols[:, n:n + 1], wide[:, o, c0:c1], AX.X, ALU.max,
                                                            apply_absolute_value=True))
                        n += 1
                return n, t

            n, t = dense("d2v", CP, 0, "b_d2v", (ready[0], ready[1], t_q, t_s), 0)
            t = input_scale(1, n, t)
            t_s = out_scale(1, "img", 1, t)
            V.after(t_s, k.pe.last())
            ready = [quantize(1, q8[:, h, :], wide[:, h, :], P) for h in range(HALVES)]
            n, t = dense("img", P, 1, "b_img", (ready[0], ready[1], t_s), 0)
            t = input_scale(2, n, t)
            out_scale(2, "att0", 2, t)
            t_s = out_scale(2, "att1", 3, t)
            for h in range(HALVES):
                t = V.mark(nc.vector.tensor_reduce(avg[:, h * B:(h + 1) * B],
                                                   wide[:, h, :].rearrange("p (b s) -> p b s", b=B), AX.X, ALU.add))
            t_avg = V.mark(V.after(t).tensor_scalar(avg[:], avg[:], 1.0 / S2, None, ALU.mult))
            V.after(t_s, k.pe.last())
            t_q8 = [quantize(2, q8[:, h, :], wide[:, h, :], P) for h in range(HALVES)]

            with ExitStack() as tctx:
                qx = k.sb(tctx, "text_q8", [P, HALVES, NTOK], BF16)
                t = V.mark(V.after(k.pe.last(), *k.ch[3]).tensor_reduce(mcols[:, 0:1], k.x_ch[:], AX.XY, ALU.max,
                                                                        apply_absolute_value=True))
                t = input_scale(3, 1, t)
                t_s = out_scale(3, "txt", 4, t)
                V.after(t_s)
                t_x = [quantize(3, qx[:, h, :], k.x_ch[:, h, :], P) for h in range(HALVES)]
                t_fused = {}
                for g in range(4):
                    for o in range(HALVES):
                        i, bank = k.banks.take(k.pe)
                        t = k.matmuls(bank, [(q["txt"][:, h, o * P:(o + 1) * P], qx[:, h, g * BANK:(g + 1) * BANK])
                                             for h in range(HALVES)], *t_x)
                        t = A.mark(A.after(t, t_s).activation(fused[:, o, g * BANK:(g + 1) * BANK], bank, ACT.Identity,
                                                              scale=s_out[:, 4:5], bias=col(k, "b_txt", o)))
                        k.banks.release(i, t)
                k.barrier()

            keys = big[:, 0:KEYS]
            values = big[:, KEYS:KEYS + B * KT * P].rearrange("p (b t d) -> p b t d", b=B, t=KT)
            qsum = k.sb(ctx, "query_sum", [P, NTOK])
            o_tok = Ring([k.sb(ctx, "o_tok%d" % n, [P, P]) for n in range(2)])
            for layer in range(2):
                wq, sc = q["att%d" % layer], s_out[:, 2 + layer:3 + layer]
                bcol, brow = col(k, "b_att%d" % layer), row(k, "b_att%d" % layer)
                t_keys = []
                for c0, c1 in CH:
                    i, bank = k.banks.take(k.pe)
                    t = k.matmuls(bank[:, 0:c1 - c0], [(wq[:, h, :], q8[:, h, c0:c1]) for h in range(HALVES)], *t_q8)
                    t = A.mark(A.after(t, *t_q8).activation(keys[:, c0:c1], bank[:, 0:c1 - c0], ACT.Identity, scale=sc, bias=bcol))
                    k.banks.release(i, t)
                    t_keys.append(t)
                for b in range(B):
                    for g in range(0, KT, 4):
                        i, bank = k.banks.take(k.pe)
                        tiles = range(g, min(g + 4, KT))
                        for kt in tiles:
                            rows = P if kt < KT - 1 else KLAST
                            a = b * S2 + kt * P
                            for h in range(HALVES):
                                ins = nc.tensor.matmul(bank[0:rows, (kt - g) * P:(kt - g + 1) * P], q8[:, h, a:a + rows],
                                                       wq[:, h, :], start=(h == 0), stop=(h == 1))
                        t = k.pe.mark(ins)
                        rows, cnt = (P, 4) if len(tiles) == 4 else (KLAST, 1)
                        t_val = V.mark(V.after(t).scalar_tensor_tensor(
                            values[0:rows, b, g:g + cnt, :], bank[0:rows, 0:cnt * P].rearrange("p (a d) -> p a d", d=P),
                            sc[0:rows], brow[0:rows].unsqueeze(1).to_broadcast([rows, cnt, P]), ALU.mult, ALU.add))
                        k.banks.release(i, t_val)
                t_qs = V.mark(V.after(V.last()).tensor_tensor(qsum[:], fused[:, 0, :], fused[:, 1, :], ALU.add))
                items = []

                def item(b, qt):
                    tile = b * TPB + qt
                    cols_q = slice(tile * P, (tile + 1) * P)

                    def finish(obank, io, rsum, after):
                        jo, o = o_tok.take(V)
                        t = V.mark(V.after(*after).tensor_scalar(o[:], obank[:, 0:P], rsum, None, ALU.mult))
                        k.banks.release(io, t)
                        i, bank = k.banks.take(k.pe)
                        t = k.pe.mark(k.pe.after(t).transpose(bank[:, 0:P], o[:], const(k, "ident")))
                        o_tok.release(jo, t)
                        t = V.mark(V.after(t, t_qs).scalar_tensor_tensor(
                            fused[:, :, cols_q], bank[:, 0:P].unsqueeze(1).to_broadcast([P, 2, P]), 0.1,
                            fused[:, :, cols_q], ALU.mult, ALU.add))
                        k.banks.release(i, t)

                    return {"query": qsum[:, cols_q], "keys": lambda c0, c1: keys[:, b * S2 + c0:b * S2 + c1],
                            "value": lambda kt, rows: values[0:rows, b, kt, :], "finish": finish,
                            "ready": (t_qs, t_keys[-1], t_val)}

                items = [item(b, qt) for b in range(B) for qt in range(TPB)]
                with ExitStack() as actx:
                    attention(k, actx, "bn%d" % layer, items, 1.0 / 16.0, P)
                    k.barrier()

        with ExitStack() as ctx:
            qf = k.sb(ctx, "fused_q8", [P, HALVES, NTOK], BF16)
            qavg = k.sb(ctx, "avg_q8", [P, HALVES * B], BF16)
            hid = k.sb(ctx, "hidden", [P, 8, NTOK])
            q, t_q = ternary(ctx, ["f1", "f2"], [(P, 4, FF), (P, 8, D)], hid[:].rearrange("p f t -> p (f t)"))
            qh = k.sb(ctx, "hidden_q8", [P, 8, NTOK], BF16)
            hbias = k.sb(ctx, "hidden_bias", [P, 8, B])
            t = V.mark(nc.vector.tensor_reduce(mcols[:, 0:1], fused[:], AX.XY, ALU.max, apply_absolute_value=True))
            t = V.mark(nc.vector.tensor_reduce(mcols[:, 1:2], avg[:], AX.X, ALU.max, apply_absolute_value=True))
            t = input_scale(4, 2, t)
            t_s = out_scale(4, "f1", 5, t)
            V.after(t_s)
            t_f = [quantize(4, qf[:, h, :], fused[:, h, :], P) for h in range(HALVES)]
            t_a = quantize(4, qavg[:], avg[:], P)
            i, bank = k.banks.take(k.pe)
            k.pe.after(t_a, t_q)
            for ft in range(8):
                for h in range(HALVES):
                    ins = nc.tensor.matmul(bank[:, ft * B:(ft + 1) * B], q["f1"][:, 2 + h, ft * P:(ft + 1) * P],
                                           qavg[:, h * B:(h + 1) * B], start=(h == 0), stop=(h == 1))
            t = k.pe.mark(ins)
            o, _ = COL_AT["b_f1"]
            t_hb = V.mark(V.after(t).scalar_tensor_tensor(
                hbias[:], bank[:, 0:8 * B].rearrange("p (f b) -> p f b", b=B), s_out[:, 5:6],
                k.cols[:, o:o + 8].unsqueeze(2).to_broadcast([P, 8, B]), ALU.mult, ALU.add))
            k.banks.release(i, t_hb)
            n = 0
            for b in range(B):
                for ft in range(8):
                    i, bank = k.banks.take(k.pe)
                    cs = slice(b * T, (b + 1) * T)
                    t = k.matmuls(bank, [(q["f1"][:, h, ft * P:(ft + 1) * P], qf[:, h, cs]) for h in range(HALVES)], *t_f)
                    t = A.mark(A.after(t, t_hb, t_q).activation(hid[:, ft, cs], bank, ACT.Relu, scale=s_out[:, 5:6],
                                                           bias=hbias[:, ft, b:b + 1]))
                    k.banks.release(i, t)
                    t = V.mark(V.after(t).tensor_reduce(mcols[:, n:n + 1], hid[:, ft, cs], AX.X, ALU.max))
                    n += 1
            t_xb = k.pool.mark(k.pool.after(k.t_param).tensor_tensor(
                k.x_tok[:], k.x_tok[:], row(k, "b_f2").unsqueeze(1).to_broadcast([P, TILES, D]), ALU.add))
            t = input_scale(5, n, t)
            t_s = out_scale(5, "f2", 6, t)
            V.after(t_s)
            t_h = [quantize(5, qh[:, :, b * T:(b + 1) * T], hid[:, :, b * T:(b + 1) * T], P) for b in range(B)]
            ready = {}
            for tile in range(TILES):
                i, bank = k.banks.take(k.pe)
                t = k.matmuls(bank[:, 0:D], [(qh[:, ft, tile * P:(tile + 1) * P], q["f2"][:, ft, :]) for ft in range(8)],
                              t_h[tile // TPB])
                ready[tile] = V.mark(V.after(t, t_xb).scalar_tensor_tensor(
                    k.x_tok[:, tile, :], bank[:, 0:D], s_out[:, 6:7], k.x_tok[:, tile, :], ALU.mult, ALU.add))
                k.banks.release(i, ready[tile])
            k.barrier()
    post_norm(k, ready)
    k.barrier()


def experts(k):
    nc, V, A = k.nc, k.dve, k.act
    with ExitStack() as ctx:
        sb = lambda name, shape, dt=F32: k.sb(ctx, name, shape, dt)
        w1s = Ring([sb("moe_w1_%d" % n, [P, HALVES, FF]) for n in range(2)])
        w2s = Ring([sb("moe_w2_%d" % n, [P, 8, D]) for n in range(2)])
        wg, b2 = sb("moe_wg", [P, HALVES, NE]), sb("moe_b2", [NE, D])
        t_g = k.load("moe_g", (wg[:], k.dram["moe_wg"].rearrange("(h p) e -> p h e", p=P)), (b2[:], k.dram["moe_b2"]))
        xhat_tok, xhat = sb("xhat_tok", [P, TILES, D]), sb("xhat", [P, HALVES, NTOK])
        normed = Ring([sb("normed%d" % n, [P, HALVES, NTOK]) for n in range(2)])
        hidden = Ring([sb("moe_h%d" % n, [P, 8, BANK]) for n in range(2)])
        sc = sb("gate_scores", [P, TILES, NE])
        cmp1, cmp2 = sb("cmp1", [P, TILES, NE, NE]), sb("cmp2", [P, TILES, NE, NE])
        gate, top = sb("gate_w", [P, TILES, NE]), sb("gate_top", [P, TILES])
        gsum = sb("gate_sum", [P, TILES])
        gate_ch = sb("gate_ch", [NE, TILES, P])

        def load_expert(e):
            i1, w1 = w1s.take(k.sp)
            i2, w2 = w2s.take(k.sp)
            t = k.load("moe%d" % e, (w1[:], k.dram["moe_w1"][e].rearrange("(h p) f -> p h f", p=P)),
                       (w2[:], k.dram["moe_w2"][e].rearrange("(f p) d -> p f d", p=P)))
            return i1, w1, i2, w2, t
        loaded = [load_expert(0), load_expert(1)]

        i, bank = k.banks.take(k.pe)
        k.pe.after(t_g, *k.ch[3])
        for tile in range(TILES):
            for h in range(HALVES):
                ins = nc.tensor.matmul(bank[:, tile * NE:(tile + 1) * NE], k.x_ch[:, h, tile * P:(tile + 1) * P],
                                       wg[:, h, :], start=(h == 0), stop=(h == 1))
        t = k.pe.mark(ins)
        t = V.mark(V.after(t).tensor_copy(sc[:], bank[:, 0:TILES * NE].rearrange("p (t e) -> p t e", e=NE)))
        k.banks.release(i, t)
        V.after(t)
        shape = [P, TILES, NE, NE]
        mine = sc[:].unsqueeze(3).to_broadcast(shape)
        other = sc[:].unsqueeze(2).to_broadcast(shape)
        flat = lambda a: a[:].rearrange("p t a b -> p t (a b)")
        V.mark(nc.vector.tensor_tensor(cmp1[:], other, mine, ALU.is_gt))
        t = V.mark(nc.vector.tensor_tensor(cmp2[:], other, mine, ALU.is_equal))
        V.mark(nc.vector.tensor_reduce(top[:], sc[:], AX.X, ALU.max))
        t = V.mark(V.after(t).tensor_tensor(flat(cmp2), flat(cmp2), const(k, "lower").unsqueeze(1).to_broadcast([P, TILES, 64]), ALU.mult))
        t = V.mark(V.after(t).tensor_tensor(flat(cmp1), flat(cmp1), flat(cmp2), ALU.add))
        t = V.mark(V.after(t).tensor_reduce(gate[:], cmp1[:], AX.X, ALU.add))
        t1 = V.mark(V.after(t).tensor_scalar(gate[:], gate[:], 1.5, None, ALU.is_lt))
        t = V.mark(nc.vector.tensor_tensor(sc[:], sc[:], top[:].unsqueeze(2).to_broadcast([P, TILES, NE]), ALU.subtract))
        t = A.mark(A.after(t).activation(sc[:], sc[:], ACT.Exp))
        t = V.mark(V.after(t, t1).tensor_tensor(gate[:], gate[:], sc[:], ALU.mult))
        t = V.mark(V.after(t).tensor_reduce(gsum[:], gate[:], AX.X, ALU.add))
        t = V.mark(V.after(t).reciprocal(top[:], gsum[:]))
        t_gate = V.mark(V.after(t).tensor_tensor(gate[:], gate[:], top[:].unsqueeze(2).to_broadcast([P, TILES, NE]), ALU.mult))
        t = V.mark(V.after(t_gate).tensor_reduce(gsum[:], gate[:], AX.X, ALU.add))
        t_gsum = V.mark(V.after(t).tensor_scalar(gsum[:], gsum[:], 1.0, None, ALU.add))
        for g in range(4):
            i, bank = k.banks.take(k.pe)
            k.pe.after(t_gate)
            for m in range(4):
                ins = nc.tensor.transpose(bank[0:NE, m * P:(m + 1) * P], gate[:, 4 * g + m, :], const(k, "ident"))
            t = k.pe.mark(ins)
            t_gc = A.mark(A.after(t).copy(gate_ch[:, 4 * g:4 * g + 4, :].rearrange("e t q -> e (t q)"), bank[0:NE, :]))
            k.banks.release(i, t_gc)

        t_hat = layer_norm(k, k.x_tok, xhat_tok, {i: None for i in range(TILES)}, 1)
        t_hc = to_channels(k, xhat_tok, xhat, t_hat)
        ready = {}
        for tile in range(TILES):
            i, bank = k.banks.take(k.pe)
            t = k.matmuls(bank[:, 0:D], [(gate_ch[:, tile, :], b2[:])], t_gc, t_g)
            ready[tile] = V.mark(V.after(t, t_gsum, t_hat[tile]).scalar_tensor_tensor(
                k.x_tok[:, tile, :], k.x_tok[:, tile, :], gsum[:, tile:tile + 1], bank[:, 0:D], ALU.mult, ALU.add))
            k.banks.release(i, ready[tile])

        def second(e, g, ih, h, t_h, w2, t_w):
            for pair in range(2):
                i, bank = k.banks.take(k.pe)
                k.pe.after(t_w, *t_h)
                for s in range(2):
                    m = 2 * pair + s
                    for ft in range(8):
                        ins = nc.tensor.matmul(bank[:, s * D:(s + 1) * D], h[:, ft, m * P:(m + 1) * P], w2[:, ft, :],
                                               start=(ft == 0), stop=(ft == 7))
                t = k.pe.mark(ins)
                for s in range(2):
                    tile = 4 * g + 2 * pair + s
                    ready[tile] = t = V.mark(V.after(t, ready[tile]).scalar_tensor_tensor(
                        k.x_tok[:, tile, :], bank[:, s * D:(s + 1) * D], gate[:, tile, e:e + 1], k.x_tok[:, tile, :],
                        ALU.mult, ALU.add))
                k.banks.release(i, t)
            hidden.release(ih, k.pe.last())

        pending = None
        for e in range(NE):
            i1, w1, i2, w2, t_w = loaded[e]
            inn, nm = normed.take(V)
            V.after(*t_hc[3])
            for h in range(HALVES):
                t_n = V.mark(nc.vector.tensor_scalar(nm[:, h, :], xhat[:, h, :], col(k, "moe_gamma", 2 * e + h),
                                                     col(k, "moe_beta", 2 * e + h), ALU.mult, ALU.add))
            for g in range(4):
                ih, hd = hidden.take(A)
                V.after(*hidden.readers[ih])
                t_h = []
                for ft in range(8):
                    i, bank = k.banks.take(k.pe)
                    t = k.matmuls(bank, [(w1[:, h, ft * P:(ft + 1) * P], nm[:, h, g * BANK:(g + 1) * BANK])
                                         for h in range(HALVES)], t_w, t_n)
                    bias = col(k, "moe_b1", 8 * e + ft)
                    if ft % 2:
                        t = V.mark(V.after(t).tensor_scalar(hd[:, ft, :], bank, bias, 0.0, ALU.add, ALU.max))
                    else:
                        t = A.mark(A.after(t).activation(hd[:, ft, :], bank, ACT.Relu, bias=bias))
                    k.banks.release(i, t)
                    t_h.append(t)
                if pending:
                    second(*pending)
                    if g == 0:
                        w1s.release(loaded[e - 1][0], k.pe.last())
                        w2s.release(loaded[e - 1][2], k.pe.last())
                        if e + 1 < NE:
                            loaded.append(load_expert(e + 1))
                pending = (e, g, ih, hd, t_h[-2:], w2, t_w)
            normed.release(inn, k.pe.last())
        second(*pending)
        k.barrier()
    post_norm(k, ready)
    k.barrier()


def linear_attention(k):
    nc, V, A = k.nc, k.dve, k.act
    CV = P + 8
    with ExitStack() as ctx:
        sb = lambda name, shape, dt=F32: k.sb(ctx, name, shape, dt)
        two = lambda name, shape: Ring([sb("%s%d" % (name, n), shape) for n in range(2)])
        wqkv, wproj = sb("la_wqkv", [P, HALVES, 3 * D]), sb("la_wproj", [P, HALVES, D])
        t_w = k.load("la_w", (wqkv[:], k.dram["la_qkvT"].rearrange("(h p) o -> p h o", p=P)),
                     (wproj[:], k.dram["la_projT"].rearrange("(h p) o -> p h o", p=P)))
        q_ch = two("la_q", [P, HALVES, T])
        scratch = two("la_min", [P, BANK])
        kv_tok = two("la_kv", [P, 2 * D])
        k_phi = two("la_k", [P, TPB, D])
        v_aug = [sb("la_v%d" % n, [P, TPB, HALVES, P + 1]) for n in range(2)]
        kvd = two("la_kvd", [P, HALVES, CV])
        den = two("la_den", [P, H0])
        o_tok, o_ch = two("la_o", [P, TPB, D]), two("la_oc", [P, HALVES, T])
        a_tok = sb("la_out", [P, TILES, D])
        regrouped = Ring([sb("la_rg%d" % n, [P, HALVES, T]) for n in range(B)])
        regroup_of = {}
        for n in range(2):
            V.mark(nc.vector.memset(v_aug[n][:, :, :, P:P + 1], 1.0))
        v_aug = Ring(v_aug)
        done = {}
        for b in range(B):
            cs = slice(b * T, (b + 1) * T)
            jq, qc = q_ch.take(A)
            for c in range(HALVES):
                i, bank = k.banks.take(k.pe)
                t = k.matmuls(bank, [(wqkv[:, h, c * P:(c + 1) * P], k.x_ch[:, h, cs]) for h in range(HALVES)],
                              t_w, *k.ch[b])
                js, mn = scratch.take(V)
                t1 = V.mark(V.after(t).tensor_scalar(mn[:], bank, col(k, "la_bq", c), 0.0, ALU.add, ALU.min))
                A.after(t1)
                t2 = A.mark(nc.scalar.activation(qc[:, c, :], bank, ACT.Relu, bias=col(k, "la_bq", c)))
                k.banks.release(i, t2)
                t = A.mark(nc.scalar.activation(mn[:], mn[:], ACT.Exp))
                t_q = V.mark(V.after(t).tensor_tensor(qc[:, c, :], qc[:, c, :], mn[:], ALU.add))
                scratch.release(js, t_q)
            jk, kp = k_phi.take(V)
            jv, va = v_aug.take(A)
            for n in range(TPB):
                i, bank = k.banks.take(k.pe)
                tile = slice((b * TPB + n) * P, (b * TPB + n + 1) * P)
                t = k.matmuls(bank, [(k.x_ch[:, h, tile], wqkv[:, h, D:3 * D]) for h in range(HALVES)], *k.ch[b])
                jt, kv = kv_tok.take(V)
                t = V.mark(V.after(t).tensor_tensor(kv[:], bank, row(k, "la_bkv"), ALU.add))
                k.banks.release(i, t)
                t_v = A.mark(A.after(t).copy(va[:, n, :, 0:P], kv[:, D:2 * D].rearrange("p (h c) -> p h c", c=P)))
                js, mn = scratch.take(V)
                t = V.mark(V.after(t).tensor_scalar(mn[:, 0:D], kv[:, 0:D], 0.0, None, ALU.min))
                t = A.mark(A.after(t).activation(mn[:, 0:D], mn[:, 0:D], ACT.Exp))
                t_k = V.mark(V.after(t).scalar_tensor_tensor(kp[:, n, :], kv[:, 0:D], 0.0, mn[:, 0:D], ALU.max, ALU.add))
                scratch.release(js, t_k)
                kv_tok.release(jt, t_k, t_v)
            i, bank = k.banks.take(k.pe)
            k.pe.after(t_k, t_v)
            for n in range(TPB):
                for h in range(HALVES):
                    ins = nc.tensor.matmul(bank[:, h * (P + 1):(h + 1) * (P + 1)], kp[:, n, h * P:(h + 1) * P],
                                           va[:, n, h, :], start=(n == 0 and h == 0), stop=(n == TPB - 1),
                                           skip_group_check=True)
            t = k.pe.mark(ins)
            k_phi.release(jk, t)
            v_aug.release(jv, t)
            jd, kd = kvd.take(V)
            V.after(t)
            for h in range(HALVES):
                o = h * (P + 1)
                V.mark(nc.vector.tensor_tensor(kd[:, h, 0:P], bank[:, o:o + P], const(k, "diag16"), ALU.mult))
                t_kd = V.mark(nc.vector.tensor_scalar(kd[:, h, P:CV], const(k, "head16"), bank[:, o + P:o + P + 1],
                                                      None, ALU.mult))
            k.banks.release(i, t_kd)
            jo, ot = o_tok.take(V)
            for n in range(TPB):
                i, bank = k.banks.take(k.pe)
                k.pe.after(t_kd, t_q)
                for h in range(HALVES):
                    ins = nc.tensor.matmul(bank[:, h * CV:(h + 1) * CV], qc[:, h, n * P:(n + 1) * P], kd[:, h, :],
                                           start=True, stop=True)
                t = k.pe.mark(ins)
                view = bank[:, 0:2 * CV].rearrange("p (h c) -> p h c", c=CV)
                jn, dn = den.take(V)
                dv = dn[:].rearrange("p (h a) -> p h a", h=2)
                t = V.mark(V.after(t).tensor_scalar(dv, view[:, :, P:CV], 1e-6, None, ALU.max))
                t = V.mark(V.after(t).reciprocal(dn[:], dn[:]))
                V.after(t)
                for h in range(HALVES):
                    t_o = V.mark(nc.vector.tensor_tensor(
                        ot[:, n, h * P:(h + 1) * P].rearrange("p (a c) -> p a c", c=N0),
                        view[:, h, 0:P].rearrange("p (a c) -> p a c", c=N0),
                        dn[:, 8 * h:8 * h + 8].unsqueeze(2).to_broadcast([P, 8, N0]), ALU.mult))
                den.release(jn, t_o)
                k.banks.release(i, t_o)
            kvd.release(jd, k.pe.last())
            q_ch.release(jq, k.pe.last())
            jc, oc = o_ch.take(A)
            for h in range(HALVES):
                i, bank = k.banks.take(k.pe)
                k.pe.after(t_o)
                for n in range(TPB):
                    ins = nc.tensor.transpose(bank[:, n * P:(n + 1) * P], ot[:, n, h * P:(h + 1) * P], const(k, "ident"))
                t = k.pe.mark(ins)
                t_oc = A.mark(A.after(t).copy(oc[:, h, :].rearrange("p (s m) -> p s m", s=N0),
                                              bank.rearrange("p (m s) -> p s m", s=N0)))
                k.banks.release(i, t_oc)
            o_tok.release(jo, k.pe.last())
            sem = k.sem("regrouped%d" % b)
            k.sp.after(t_oc)
            for hd in range(H0):
                nc.sync.dma_start(k.dram["regroup"][b, :, :, hd, :].rearrange("s v m -> v s m"),
                                  oc[(hd % 8) * N0:(hd % 8 + 1) * N0, hd // 8, :].rearrange("v (s m) -> v s m", s=N0)
                                  ).then_inc(sem, 16)
            t_out = (sem, 16 * H0)
            o_ch.release(jc, t_out)
            jr, rg = regrouped.take(k.sp)
            t_rg = k.load("regrouped%d" % b, (rg[:], k.dram["regroup"][b].rearrange("(g s) v h m -> (s v) g (h m)", g=2)),
                          after=(t_out,))
            regroup_of[b] = (jr, rg, t_rg)
        for b in range(B):
            jr, rg, t_rg = regroup_of[b]
            for n in range(TPB):
                i, bank = k.banks.take(k.pe)
                tile = b * TPB + n
                t = k.matmuls(bank[:, 0:D], [(rg[:, h, n * P:(n + 1) * P], wproj[:, h, :]) for h in range(HALVES)], t_rg)
                done[tile] = V.mark(V.after(t).tensor_tensor(a_tok[:, tile, :], bank[:, 0:D], row(k, "la_bproj"), ALU.add))
                k.banks.release(i, done[tile])
        done = layer_norm(k, a_tok, a_tok, done, 0)
        ready = {}
        over = lambda name: row(k, name).unsqueeze(1).to_broadcast([P, TPB, D])
        for b in range(B):
            a = a_tok[:, b * TPB:(b + 1) * TPB, :]
            xs = k.x_tok[:, b * TPB:(b + 1) * TPB, :]
            G = k.pool
            t = G.mark(G.after(*[done[b * TPB + n] for n in range(TPB)]).tensor_tensor(a, a, over("la_gamma"), ALU.mult))
            t = G.mark(G.after(t).tensor_tensor(a, a, over("la_beta"), ALU.add))
            t = V.mark(V.after(t).scalar_tensor_tensor(xs, xs, 2.0, a, ALU.mult, ALU.add))
            for n in range(TPB):
                ready[b * TPB + n] = t
        k.barrier()
    post_norm(k, ready)
    k.barrier()


SPLIT = 3 * NX
ROWS_X = SPLIT + 3


def run_beside(main, side):
    main, side = list(main), list(side)
    done = 0
    for n, step in enumerate(main):
        step()
        want = len(side) * (n + 1) // len(main)
        for other in side[done:want]:
            other()
        done = max(done, want)


def cross_attention(k):
    nc, V, A, G = k.nc, k.dve, k.act, k.pool
    scale = 1.0 / float(np.sqrt(np.float32(NX)))
    HU = HX // 2
    KTP = (KT + 1) // 2
    VC = NX + 1
    with ExitStack() as ctx:
        sb = lambda name, shape, dt=F32: k.sb(ctx, name, shape, dt)
        ring = lambda name, n, shape, dt=F32: Ring([sb("%s%d" % (name, i), shape, dt) for i in range(n)])
        wq, wo = sb("xa_wq", [P, HALVES, D]), sb("xa_wo", [P, HALVES, D])
        wk, wv = sb("xa_wk", [CP, HALVES, D]), sb("xa_wv", [CP, HALVES, D])
        t_w = k.load("xa_w", *[(w[:], k.dram["xa_" + n].rearrange("(h p) o -> p h o", h=2))
                               for n, w in (("q", wq), ("o", wo), ("k", wk), ("v", wv))])
        contexts = ring("xa_ctx", 1, [CP, HALVES, S2])
        keys_hl = ring("xa_keys_hl", 1, [P, 2, HALVES, S2], BF16)
        query_hl = ring("xa_query_hl", 1, [P, 2, HALVES, T], BF16)
        key_rows = [sb("xa_key_rows%d" % n, [ROWS_X, HU, S2], BF16) for n in range(2)]
        query_rows = ring("xa_query_rows", 2, [ROWS_X, HU, T], BF16)
        value_f32 = ring("xa_value_f32", 2, [P, 2, D])
        values = [sb("xa_values%d" % n, [P, KT, HX, 2 * VC], BF16) for n in range(2)]
        maxes, nmax = ring("xa_max", 2, [P, HU * TPB, 2]), ring("xa_nmax", 2, [P, HU * TPB])
        rest = ring("xa_rest", 2, [P, HU * TPB])
        parts = ring("xa_parts", 2, [P, TPB, 3, HU], BF16)
        parts_t = ring("xa_parts_t", 2, [3 * HU, T], BF16)
        ident_b = sb("xa_ident_b", [P, P], BF16)
        exps = ring("xa_exp", 3, [P, 2, T])
        highs, lows = ring("xa_high", 5, [P, 2, T], BF16), ring("xa_low", 5, [P, 2, T], BF16)
        o_rows = ring("xa_o_rows", 2, [2 * VC, T])
        rsum = ring("xa_rsum", 2, [P, TPB])
        o_tok, o_ch = ring("xa_o", 2, [P, TPB, D]), ring("xa_oc", 2, [P, HALVES, T])
        fold = sb("xa_fold", [2 * VC, VC])
        pairs = Ring([k.psum[:, 2 * n:2 * n + 2, :].rearrange("p b c -> p (b c)") for n in range(3)])
        banks = Ring([k.psum[:, n, :] for n in (6, 7)])

        t = V.mark(V.after(k.t_param).tensor_copy(ident_b[:], const(k, "ident")))
        t_fold = V.mark(nc.vector.tensor_copy(fold[:], const(k, "fold", 2 * VC)))
        for n in range(2):
            V.mark(nc.vector.memset(key_rows[n][SPLIT:ROWS_X], 1.0))
            V.mark(nc.vector.memset(values[n][:, :, :, NX:VC], 1.0))
            t_ones = V.mark(nc.vector.memset(values[n][:, :, :, 2 * VC - 1:2 * VC], 0.0))
        key_rows, values = Ring(key_rows), Ring(values)
        t_bias = G.mark(G.after(k.t_param, *[k.tok[i] for i in range(TILES)]).tensor_tensor(
            k.x_tok[:], k.x_tok[:], row(k, "xa_bo").unsqueeze(1).to_broadcast([P, TILES, D]), ALU.add))

        batch, unit, ready = {}, {}, {}

        def split(high, low, bank, bias, t):
            t = A.mark(A.after(t).activation(high, bank, ACT.Identity, bias=bias))
            return V.mark(V.after(t).scalar_tensor_tensor(low, bank, bias, high, ALU.add, ALU.subtract))

        def prepare_batch(b):
            s = batch[b] = {}

            def load():
                jc, s["ctx"] = contexts.take(k.sp)
                s["jc"] = jc
                s["t_ctx"] = k.load("xa_ctx%d" % b, (s["ctx"][:], k.dram["ctxT"][:, b, :].rearrange("(h p) s -> p h s", h=2)))
                s["jq"], s["q"] = query_hl.take(A)
                V.after(*query_hl.readers[s["jq"]])
                s["jk"], s["k"] = keys_hl.take(A)
                V.after(*keys_hl.readers[s["jk"]])

            def queries(c):
                i, bank = pairs.take(k.pe)
                bank = bank[:, 0:T]
                t = k.matmuls(bank, [(wq[:, h, c * P:(c + 1) * P], k.x_ch[:, h, b * T:(b + 1) * T]) for h in range(HALVES)],
                              t_w, *k.ch[b])
                s["t_q"] = split(s["q"][:, 0, c, :], s["q"][:, 1, c, :], bank, col(k, "xa_bq", c), t)
                pairs.release(i, s["t_q"])

            def keys(o, c0):
                c1 = min(c0 + 2 * BANK, S2)
                i, bank = pairs.take(k.pe)
                for a in range(c0, c1, BANK):
                    e = min(a + BANK, c1)
                    t = k.matmuls(bank[:, a - c0:e - c0], [(wk[:, h, o * P:(o + 1) * P], s["ctx"][:, h, a:e])
                                                           for h in range(HALVES)], s["t_ctx"], t_w)
                s["t_k"] = split(s["k"][:, 0, o, c0:c1], s["k"][:, 1, o, c0:c1], bank[:, 0:c1 - c0], col(k, "xa_bk", o), t)
                pairs.release(i, s["t_k"])

            def value(kt0):
                if kt0 == 0:
                    s["jv"], s["v"] = values.take(G)
                tiles = range(kt0, min(kt0 + 2, KT))
                rows = P if kt0 < KT - 1 else KLAST
                n = len(tiles)
                i, bank = pairs.take(k.pe)
                for kt in tiles:
                    t = k.matmuls(bank[0:rows, (kt - kt0) * D:(kt - kt0 + 1) * D],
                                  [(s["ctx"][:, h, kt * P:kt * P + rows], wv[:, h, :]) for h in range(HALVES)], s["t_ctx"], t_w)
                jf, vf = value_f32.take(V)
                t = V.mark(V.after(t).tensor_tensor(
                    vf[0:rows, 0:n, :], bank[0:rows, 0:n * D].rearrange("p (a d) -> p a d", d=D),
                    row(k, "xa_bv")[0:rows].unsqueeze(1).to_broadcast([rows, n, D]), ALU.add))
                pairs.release(i, t)
                src = vf[0:rows, 0:n, :].rearrange("p a (h c) -> p (a h) c", c=NX)
                dst = s["v"][0:rows, kt0:kt0 + n, :, :].rearrange("p a h c -> p (a h) c")
                t = G.mark(G.after(t, t_ones).tensor_copy(dst[:, :, 0:NX], src))
                s["t_v"] = G.mark(G.after(t).tensor_tensor(dst[:, :, VC:VC + NX], src, dst[:, :, 0:NX], ALU.subtract))
                value_f32.release(jf, s["t_v"])
                if kt0 + 2 >= KT:
                    contexts.release(s["jc"], k.pe.last())
                    s["jo"], s["o"] = o_tok.take(V)

            return ([load] + [lambda c=c: queries(c) for c in range(HALVES)]
                    + [lambda o=o, c0=c0: keys(o, c0) for o in range(HALVES) for c0 in range(0, S2, 2 * BANK)]
                    + [lambda kt=kt: value(kt) for kt in range(0, KT, 2)])

        def prepare_unit(u):
            b, half = divmod(u, 2)
            s = unit[u] = {}

            def stack():
                p = batch[b]
                s["jk"], kr = key_rows.take(k.sp)
                s["jq"], qr = query_rows.take(k.sp)
                moves = []
                for a in range(HU):
                    lanes = slice(a * NX, (a + 1) * NX)
                    for j, (qp, kp) in enumerate(((0, 0), (1, 0), (0, 1))):
                        rows = slice(j * NX, (j + 1) * NX)
                        moves.append((kr[rows, a, :], p["k"][lanes, kp, half, :]))
                        moves.append((qr[rows, a, :], p["q"][lanes, qp, half, :]))
                s["t_rows"] = k.load("xa_rows%d" % u, *moves, after=(p["t_k"], p["t_q"]))
                s["k"], s["q"] = kr, qr
                if half:
                    keys_hl.release(p["jk"], s["t_rows"], unit[u - 1]["t_rows"])
                    query_hl.release(p["jq"], s["t_rows"], unit[u - 1]["t_rows"])
                s["jm"], s["max"] = maxes.take(V)

            def maximum(a, qt, part):
                c0, c1 = ((0, 2 * BANK), (2 * BANK, S2))[part]
                i, bank = pairs.take(k.pe)
                k.pe.after(s["t_rows"])
                for x in range(c0, c1, BANK):
                    y = min(x + BANK, c1)
                    ins = nc.tensor.matmul(bank[:, x - c0:y - c0], s["q"][0:SPLIT, a, qt * P:(qt + 1) * P],
                                           s["k"][0:SPLIT, a, x:y], start=True, stop=True)
                t = k.pe.mark(ins)
                s["t_max"] = V.mark(V.after(t).tensor_reduce(s["max"][:, qt * HU + a, part:part + 1],
                                                             bank[:, 0:c1 - c0], AX.X, ALU.max))
                pairs.release(i, s["t_max"])

            def subtract_rows():
                jn, nm = nmax.take(V)
                jr, rs = rest.take(V)
                jp, pt = parts.take(V)
                part = lambda n: pt[:, :, n, :]
                grid = lambda a: a[:].rearrange("p (t a) -> p t a", a=HU)
                t = V.mark(V.after(s["t_max"]).tensor_tensor(nm[:], s["max"][:, :, 0], s["max"][:, :, 1], ALU.max))
                maxes.release(s["jm"], t)
                t = V.mark(V.after(t).tensor_scalar(nm[:], nm[:], -1.0, None, ALU.mult))
                t = V.mark(V.after(t).tensor_copy(part(0), grid(nm)))
                t = V.mark(V.after(t).tensor_tensor(grid(rs), grid(nm), part(0), ALU.subtract))
                t = V.mark(V.after(t).tensor_copy(part(1), grid(rs)))
                t = V.mark(V.after(t).tensor_tensor(part(2), grid(rs), part(1), ALU.subtract))
                nmax.release(jn, t)
                rest.release(jr, t)
                i, bank = banks.take(k.pe)
                k.pe.after(t)
                bank_b = bank.bitcast(BF16)
                for qt in range(TPB):
                    ins = nc.tensor.transpose(bank_b[0:3 * HU, qt * P:(qt + 1) * P],
                                              pt[:, qt, :, :].rearrange("p n a -> p (n a)"), ident_b[:])
                t = k.pe.mark(ins)
                parts.release(jp, t)
                jt, tt = parts_t.take(V)
                t = V.mark(V.after(t).tensor_copy(tt[:], bank_b[0:3 * HU, 0:T]))
                banks.release(i, t)
                s["t_rows3"] = k.load("xa_max%d" % u, *[(s["q"][SPLIT + n:SPLIT + n + 1, :, :], tt[n * HU:(n + 1) * HU, :])
                                                        for n in range(3)], after=(t,))
                parts_t.release(jt, s["t_rows3"])

            return ([stack] + [lambda a=a, qt=qt, part=part: maximum(a, qt, part)
                               for a in range(HU) for qt in range(TPB) for part in range(2)] + [subtract_rows])

        def attend(u):
            b, half = divmod(u, 2)
            s, p = unit[u], batch[b]
            steps = []
            flying = []

            def pair(a, kp):
                tiles = range(2 * kp, min(2 * kp + 2, KT))
                rows = P if kp < KTP - 1 else KLAST
                n = len(tiles)
                if kp == 0:
                    s["io"], s["bank"] = banks.take(k.pe)
                i, bank = pairs.take(k.pe)
                k.pe.after(s["t_rows3"])
                for m, kt in enumerate(tiles):
                    ins = nc.tensor.matmul(bank[0:rows, m * T:(m + 1) * T], s["k"][:, a, kt * P:kt * P + rows],
                                           s["q"][:, a, :], start=True, stop=True)
                t = k.pe.mark(ins)
                if a == HU - 1 and kp == KTP - 1:
                    key_rows.release(s["jk"], t)
                    query_rows.release(s["jq"], t)
                je, ex = exps.take(A)
                view = bank[0:rows, 0:n * T].rearrange("p (m q) -> p m q", q=T)
                t = A.mark(A.after(t).activation(ex[0:rows, 0:n, :], view, ACT.Exp, scale=scale))
                pairs.release(i, t)
                ih, hi = highs.take(A if kp % 2 else V)
                q = A if kp % 2 else V
                q.after(t)
                if kp % 2:
                    t = q.mark(nc.scalar.copy(hi[0:rows, 0:n, :], ex[0:rows, 0:n, :]))
                else:
                    t = q.mark(nc.vector.tensor_copy(hi[0:rows, 0:n, :], ex[0:rows, 0:n, :]))
                q = V if kp in (1, 4) else G
                il, lo = lows.take(q)
                e = nc.vector if q is V else nc.gpsimd
                q.after(t)
                t_low = q.mark(e.tensor_tensor(lo[0:rows, 0:n, :], ex[0:rows, 0:n, :], hi[0:rows, 0:n, :], ALU.subtract))
                exps.release(je, t_low)
                flying.append((a, kp, ih, hi, il, lo, t, t_low, s["io"], s["bank"]))

            def product():
                a, kp, ih, hi, il, lo, t_hi, t_lo, io, bank = flying.pop(0)
                tiles = range(2 * kp, min(2 * kp + 2, KT))
                rows = P if kp < KTP - 1 else KLAST
                k.pe.after(t_hi, t_lo, p["t_v"])
                hd = half * HU + a
                for m, kt in enumerate(tiles):
                    for x, piece in enumerate((hi, lo)):
                        ins = nc.tensor.matmul(bank[0:2 * VC, :], p["v"][0:rows, kt, hd, :], piece[0:rows, m, :],
                                               start=(kt == 0 and x == 0), stop=(kt == KT - 1 and x == 1))
                t = k.pe.mark(ins)
                highs.release(ih, t)
                lows.release(il, t)
                if kp < KTP - 1:
                    return
                jr, orow = o_rows.take(A)
                t = A.mark(A.after(t).copy(orow[:], bank[0:2 * VC, :]))
                banks.release(io, t)
                i, bank = banks.take(k.pe)
                k.pe.after(t, t_fold)
                for qt in range(TPB):
                    ins = nc.tensor.matmul(bank[:, qt * VC:(qt + 1) * VC], orow[:, qt * P:(qt + 1) * P], fold[:],
                                           start=True, stop=True)
                t = k.pe.mark(ins)
                o_rows.release(jr, t)
                view = bank[:, 0:TPB * VC].rearrange("p (t c) -> p t c", c=VC)
                js, rs = rsum.take(V)
                t = V.mark(V.after(t).reciprocal(rs[:], view[:, :, NX]))
                t = V.mark(V.after(t).tensor_tensor(p["o"][:, :, hd * NX:(hd + 1) * NX], view[:, :, 0:NX],
                                                    rs[:].unsqueeze(2).to_broadcast([P, TPB, NX]), ALU.mult))
                rsum.release(js, t)
                banks.release(i, t)
                p["t_o"] = t

            def step(a, kp):
                pair(a, kp)
                if len(flying) > 3:
                    product()

            for a in range(HU):
                for kp in range(KTP):
                    steps.append(lambda a=a, kp=kp: step(a, kp))
            def drain():
                while flying:
                    product()
                if half:
                    values.release(p["jv"], k.pe.last())
                    project(b)
            steps.append(drain)
            return steps

        def project(b):
            p = batch[b]
            jc, oc = o_ch.take(A)
            for h in range(HALVES):
                i, bank = pairs.take(k.pe)
                k.pe.after(p["t_o"])
                for n in range(TPB):
                    ins = nc.tensor.transpose(bank[:, n * P:(n + 1) * P], p["o"][:, n, h * P:(h + 1) * P], const(k, "ident"))
                t = k.pe.mark(ins)
                t_oc = A.mark(A.after(t).copy(oc[:, h, :], bank[:, 0:T]))
                pairs.release(i, t_oc)
            o_tok.release(p["jo"], k.pe.last())
            for n in range(0, TPB, 2):
                i, bank = pairs.take(k.pe)
                for m in range(2):
                    t = k.matmuls(bank[:, m * D:(m + 1) * D], [(oc[:, h, (n + m) * P:(n + m + 1) * P], wo[:, h, :])
                                                               for h in range(HALVES)], t_oc)
                tile = b * TPB + n
                t = V.mark(V.after(t, t_bias).tensor_tensor(
                    k.x_tok[:, tile:tile + 2, :], bank[:, 0:2 * D].rearrange("p (m d) -> p m d", d=D),
                    k.x_tok[:, tile:tile + 2, :], ALU.add))
                pairs.release(i, t)
                ready[tile] = ready[tile + 1] = t
            o_ch.release(jc, k.pe.last())

        for step in prepare_batch(0) + prepare_unit(0):
            step()
        for u in range(2 * B):
            side = []
            if u + 1 < 2 * B:
                if u % 2:
                    side += prepare_batch((u + 1) // 2)
                side += prepare_unit(u + 1)
            side += [lambda: None] * (len(side) // 12)
            run_beside(attend(u), side)
        k.barrier()
    post_norm(k, ready)
    k.barrier()


def windowed(k):
    kept = k.load("x_kept", (k.dram["kept"], k.x_tok[:]), after=[k.tok[i] for i in range(TILES)])
    for layer in range(2):
        windowed_layer(k, layer)
        k.barrier()
    with ExitStack() as ctx:
        x_in = k.sb(ctx, "x_in", [P, TILES, D])
        t = k.load("x_in", (x_in[:], k.dram["kept"]), after=(kept,))
        k.dve.after(t)
        ready = {i: k.dve.mark(k.nc.vector.tensor_tensor(k.x_tok[:, i, :], k.x_tok[:, i, :], x_in[:, i, :], ALU.add))
                 for i in range(TILES)}
        k.tok = layer_norm(k, k.x_tok, k.x_tok, ready, 0)
        k.barrier()


def windowed_attention(k, layer, ready):
    nc, V, A, G = k.nc, k.dve, k.act, k.pool
    half = NL // 2
    with ExitStack() as ctx:
        sb = lambda name, shape, dt=F32: k.sb(ctx, name + "_l%d" % layer, shape, dt)
        ring = lambda name, n, shape, dt=F32: Ring([sb("%s%d" % (name, i), shape, dt) for i in range(n)])
        wqkv, wo = sb("wqkv", [P, HALVES, 3 * INNER]), sb("wo", [P, 4, D])
        tab = sb("rotary", [P, TPB, 4, NL])
        mask, mask_b, ident_b = sb("mask", [P, 2 * P]), sb("mask_b", [P, 2 * P], BF16), sb("ident_b", [P, P], BF16)
        late = sb("late", [P, B, P])
        raws = ring("qk_raw", 1, [P, TPB, 2, INNER])
        squares = ring("qk_sq", 1, [P, 2 * INNER])
        norms = ring("qk_norm", 2, [P, TPB, 2 * HL])
        turned, other = ring("qk_rot", 2, [P, INNER]), ring("qk_other", 2, [P, INNER])
        q_pad = [sb("w_q%d" % n, [P, 2, 4, T]) for n in range(2)]
        k_ch, v_tok = ring("w_k", 2, [P, 4, T]), ring("w_v", 2, [P, TPB, INNER])
        probs, probs_t = ring("w_p", 2, [P, HL, 2 * P]), ring("w_pt", 2, [P, HL, 2, P])
        maxes, sums = ring("w_max", 2, [P, HL]), ring("w_sum", 2, [P, HL])
        o_ch = ring("w_oc", 2, [P, 4, P])

        t_w = k.load("win%d" % layer, (wqkv[:], k.dram["wqkv"][layer].rearrange("(h p) o -> p h o", p=P)),
                     (tab[:], k.dram["rotary"]), (mask[:], k.dram["mask"]),
                     (wo[:], k.dram["wo"][layer].rearrange("(c p) o -> p c o", p=P)))
        for n in range(2):
            t_zero = G.mark(nc.gpsimd.memset(q_pad[n][:], 0.0))
        q_pad = Ring(q_pad)
        V.after(t_w)
        V.mark(nc.vector.tensor_copy(mask_b[:], mask[:]))
        V.mark(nc.vector.tensor_copy(ident_b[:], const(k, "ident")))
        for n, name in ((0, "q_scale"), (2, "k_scale")):
            s = row(k, name, layer * NL, (layer + 1) * NL)
            wide = lambda a, w: a.unsqueeze(1).to_broadcast([P, TPB, w])
            V.mark(nc.vector.tensor_tensor(tab[:, :, n, :], tab[:, :, n, :], wide(s, NL), ALU.mult))
            V.mark(nc.vector.tensor_tensor(tab[:, :, n + 1, 0:half], tab[:, :, n + 1, 0:half], wide(s[:, half:NL], half), ALU.mult))
            t_tab = V.mark(nc.vector.tensor_tensor(tab[:, :, n + 1, half:NL], tab[:, :, n + 1, half:NL], wide(s[:, 0:half], half), ALU.mult))
        t_ch = [t for g in range(4) for t in k.ch[g]]
        V.after(*t_ch)
        V.mark(nc.vector.memset(late[:, :, 0:1], 0.0))
        t_late = V.mark(nc.vector.tensor_copy(late[:, :, 1:P], k.x_ch[:, 1, :].rearrange("p (b t) -> p b t", t=T)[:, :, 0:P - 1]))
        heads3 = lambda a: a.rearrange("p (h c) -> p h c", c=NL)
        batch = {}

        def produce(b):
            s = batch[b] = {"t": []}

            def project(w, which):
                if (w, which) == (0, 0):
                    s["jr"], s["raw"] = raws.take(A)
                    s["jn"], s["norm"] = norms.take(V)
                    s["q"], s["k"], s["v"] = q_pad.take(A), k_ch.take(A), v_tok.take(A)
                tile = b * TPB + w
                cols_w = slice(which * INNER, (which + 1) * INNER)
                i, bank = k.banks.take(k.pe)
                before = k.x_ch[:, 1, tile * P - 1:(tile + 1) * P - 1] if w else late[:, b, :]
                t = k.matmuls(bank, [(k.x_ch[:, 0, tile * P:(tile + 1) * P], wqkv[:, 0, cols_w]),
                                     (before, wqkv[:, 1, cols_w])], t_w, t_late)
                dst = s["v"][1][:, w, :] if which == 2 else s["raw"][:, w, which, :]
                t = A.mark(A.after(t).copy(dst, bank))
                k.banks.release(i, t)
                if which == 2:
                    s["t_v"] = t
                if which == 1:
                    js, sq = squares.take(A)
                    t = A.mark(A.after(t).activation(sq[:], s["raw"][:, w, :, :].rearrange("p a c -> p (a c)"), ACT.Square))
                    s["t_raw"] = t
                    s["t_ss"] = V.mark(V.after(t).tensor_reduce(s["norm"][:, w, :], sq[:].rearrange("p (h c) -> p h c", c=NL), AX.X, ALU.add))
                    squares.release(js, s["t_ss"])

            def invert():
                nm = s["norm"]
                t = A.mark(A.after(s["t_ss"]).activation(nm[:], nm[:], ACT.Sqrt))
                t = V.mark(V.after(t).tensor_scalar(nm[:], nm[:], 1e-12, None, ALU.max))
                s["t_n"] = V.mark(V.after(t).reciprocal(nm[:], nm[:]))

            def rotate(w, which):
                x3 = heads3(s["raw"][:, w, which, :])
                nm = s["norm"][:, w, which * HL:(which + 1) * HL]
                jo, ot = other.take(G)
                o3 = heads3(ot[:])
                wide = lambda a, n: a.unsqueeze(1).to_broadcast([P, HL, n])
                sin = tab[:, w, 2 * which + 1, :]
                G.after(s["t_raw"], t_tab)
                G.mark(nc.gpsimd.tensor_tensor(o3[:, :, 0:half], x3[:, :, half:NL], wide(sin[:, 0:half], half), ALU.mult))
                t2 = G.mark(nc.gpsimd.tensor_tensor(o3[:, :, half:NL], x3[:, :, 0:half], wide(sin[:, half:NL], half), ALU.mult))
                jt, tn = turned.take(V)
                t1 = V.mark(V.after(s["t_raw"], t_tab).tensor_tensor(heads3(tn[:]), x3, wide(tab[:, w, 2 * which, :], NL), ALU.mult))
                t = V.mark(V.after(t1, t2).tensor_tensor(tn[:], tn[:], ot[:], ALU.add))
                other.release(jo, t)
                t = V.mark(V.after(t, s["t_n"]).tensor_tensor(heads3(tn[:]), heads3(tn[:]), nm.unsqueeze(2).to_broadcast([P, HL, NL]), ALU.mult))
                s["turn", w, which] = (jt, tn, t)

            def turn(w, which):
                jt, tn, t = s["turn", w, which]
                i, bank = k.banks.take(k.pe)
                k.pe.after(t)
                for c in range(4):
                    ins = nc.tensor.transpose(bank[:, c * P:(c + 1) * P], tn[:, c * P:(c + 1) * P], const(k, "ident"))
                t = k.pe.mark(ins)
                turned.release(jt, t)
                view = bank.rearrange("p (c t) -> p c t", t=P)
                cw = slice(w * P, (w + 1) * P)
                if which:
                    t = A.mark(A.after(t).copy(s["k"][1][:, :, cw], view))
                else:
                    A.after(t, t_zero)
                    for x in range(2):
                        lanes = slice(NL * x, NL * (x + 1))
                        t = A.mark(nc.scalar.copy(s["q"][1][lanes, x, :, cw], view[lanes]))
                k.banks.release(i, t)
                s["t"].append(t)
                if (w, which) == (TPB - 1, 1):
                    norms.release(s["jn"], V.last())
                    raws.release(s["jr"], V.last(), G.last())

            steps = [lambda w=w, which=which: project(w, which) for w in range(TPB) for which in range(3)] + [invert]
            order = [(w, which) for w in range(TPB) for which in range(2)]
            for n, o in enumerate(order):
                steps.append(lambda o=o: rotate(*o))
                if n:
                    steps.append(lambda o=order[n - 1]: turn(*o))
            steps.append(lambda: turn(*order[-1]))
            return steps

        def attend(b):
            s = batch[b]
            window = {}

            def score(w):
                (_, qp), (_, kc) = s["q"], s["k"]
                a = 0 if w else 1
                lo = a * P
                k.pe.after(*k.score_free, *s["t"], t_tab)
                for bk in range(4):
                    out = k.psum[:, bk, :].rearrange("p (x j) -> p x j", x=2)[:, :, lo:2 * P]
                    nc.tensor.matmul(out, ident_b[:], mask_b[:, lo:2 * P].unsqueeze(1).to_broadcast([P, 2, 2 * P - lo]),
                                     start=True, stop=False, skip_group_check=True)
                for x in range(2):
                    for p in range(4):
                        out = k.psum[:, 2 * x + p // 2, (p % 2) * 2 * P + lo:(p % 2 + 1) * 2 * P]
                        ins = nc.tensor.matmul(out, qp[:, x, p, w * P:(w + 1) * P], kc[:, p, (w - 1) * P + lo:(w + 1) * P],
                                               start=False, stop=True, skip_group_check=True)
                t = k.pe.mark(ins)
                sc = k.psum[:, 0:4, :].rearrange("p b (x j) -> p (b x) j", x=2)[:, :, lo:2 * P]
                jm, mx = maxes.take(V)
                t = V.mark(V.after(t).tensor_reduce(mx[:], sc, AX.X, ALU.max))
                t = V.mark(V.after(t).tensor_scalar(mx[:], mx[:], -8.0, None, ALU.mult))
                jp, pr = probs.take(A)
                js, sm = sums.take(A)
                A.after(t)
                for x in range(HL):
                    t = A.mark(nc.scalar.activation(pr[:, x, lo:2 * P], sc[:, x, :], ACT.Exp, bias=mx[:, x:x + 1], scale=8.0,
                                                    accum_out=sm[:, x:x + 1]))
                k.score_free = (t,)
                maxes.release(jm, t)
                t = V.mark(V.after(t).reciprocal(sm[:], sm[:]))
                V.after(t)
                for x in range(HL):
                    t = V.mark(nc.vector.tensor_scalar(pr[:, x, lo:2 * P], pr[:, x, lo:2 * P], sm[:, x:x + 1], None, ALU.mult))
                sums.release(js, t)
                window[w] = {"a": a, "jp": jp, "p": pr, "t_p": t}

            def turn(w):
                m = window[w]
                jt, pt = probs_t.take(A)
                V.after(*probs_t.readers[jt])
                a, per = m["a"], 2 - m["a"]
                k.pe.after(m["t_p"])
                copied = []
                blocks = [(x, kk) for x in range(HL) for kk in range(a, 2)]
                for g in range(0, len(blocks), 4):
                    i, bank = k.banks.take(k.pe)
                    for n, (x, kk) in enumerate(blocks[g:g + 4]):
                        ins = nc.tensor.transpose(bank[:, n * P:(n + 1) * P], m["p"][:, x, kk * P:(kk + 1) * P], const(k, "ident"))
                    t = k.pe.mark(ins)
                    x0, cnt = blocks[g][0], 4 // per
                    t = evacuate(k, g // 4, pt[:, x0:x0 + cnt, a:2, :], bank.rearrange("p (x c q) -> p x c q", x=cnt, q=P), t)
                    k.banks.release(i, t)
                    copied.append(t)
                probs.release(m["jp"], k.pe.last())
                m["jt"], m["pt"], m["copied"] = jt, pt, copied

            def combine(w):
                m = window[w]
                vt = s["v"][1]
                io, obank = k.banks.take(k.pe)
                k.pe.after(*m["copied"], s["t_v"])
                for x in range(2):
                    for p in range(4):
                        hd = 2 * p + x
                        for kk in range(m["a"], 2):
                            ins = nc.tensor.matmul(obank[NL * x:NL * (x + 1), p * P:(p + 1) * P],
                                                   vt[:, w - 1 + kk, hd * NL:(hd + 1) * NL], m["pt"][:, 4 * x + p, kk, :],
                                                   start=(kk == m["a"]), stop=(kk == 1))
                t = k.pe.mark(ins)
                probs_t.release(m["jt"], t)
                jc, oc = o_ch.take(A)
                t = A.mark(A.after(t).copy(oc[:].rearrange("p c t -> p (c t)"), obank))
                k.banks.release(io, t)
                m["oc"] = (jc, oc, t)

            def output(w):
                jc, oc, t = window[w]["oc"]
                i, bank = k.banks.take(k.pe)
                t = k.matmuls(bank[:, 0:D], [(oc[:, c, :], wo[:, c, :]) for c in range(4)], t)
                o_ch.release(jc, t)
                tile = b * TPB + w
                ready[tile] = V.mark(V.after(t, *before).tensor_tensor(k.x_tok[:, tile, :], bank[:, 0:D], k.x_tok[:, tile, :], ALU.add))
                k.banks.release(i, ready[tile])
                if w == TPB - 1:
                    for rng, (j, _) in zip((q_pad, k_ch, v_tok), (s["q"], s["k"], s["v"])):
                        rng.release(j, k.pe.last())

            return [(score, w) for w in range(TPB)], [[(turn, w), (combine, w), (output, w)] for w in range(TPB)]

        before = [k.tok[i] for i in range(TILES)] if k.tok else []
        for step in produce(0):
            step()
        steps = []
        tail = []
        for b in range(B):
            scores, rest = attend_later(attend, b)
            side = produce(b + 1) if b + 1 < B else []
            main = []
            for w in range(TPB):
                main.append(scores[w])
                main += tail
                tail = rest[w]
            for step in main[0:4]:
                step()
            run_beside(main[4:], side)
        for step in tail:
            step()
        k.barrier()


def attend_later(attend, b):
    scores, rest = attend(b)
    call = lambda f, w: (lambda: f(w))
    return [call(f, w) for f, w in scores], [[call(f, w) for f, w in group] for group in rest]


def windowed_layer(k, layer):
    nc, V, A, G = k.nc, k.dve, k.act, k.pool
    ready = {}
    windowed_attention(k, layer, ready)

    with ExitStack() as ctx:
        sb = lambda name, shape, dt=F32: k.sb(ctx, name + "_f%d" % layer, shape, dt)
        w1, w2 = sb("w1", [P, HALVES, 2 * HID]), sb("w2", [P, HT, D])
        full = (HT - 1) * P
        t_w = k.load("ffn%d" % layer, (w1[:], k.dram["w1"][layer].rearrange("(h p) o -> p h o", p=P)),
                     (w2[:, 0:HT - 1, :], k.dram["w2"][layer][0:full].rearrange("(c p) o -> p c o", p=P)),
                     (w2[0:HLAST, HT - 1, :], k.dram["w2"][layer][full:HID]))
        late = sb("late_tok", [P, TILES, P])
        h_tok, h_ch = sb("h_tok", [P, TILES, D]), sb("h_ch", [P, HALVES, NTOK])
        stats = sb("late_stats", [P, TILES, 2, 6])
        gl = Ring([sb("gelu%d" % n, [P, BANK]) for n in range(2)])
        hidden = Ring([sb("hidden%d" % n, [P, HT, BANK]) for n in range(2)])
        t = V.mark(nc.vector.memset(late[0:1], 0.0))
        src = k.x_tok[:, :, P:D]
        pairs = [(late[1:P], src[0:P - 1])]
        pairs += [(late[0:1, b * TPB + 1:(b + 1) * TPB, :], src[P - 1:P, b * TPB:(b + 1) * TPB - 1, :]) for b in range(B)]
        t_late = k.load("late%d" % layer, *pairs, after=(t, *[ready[i] for i in range(TILES)]))
        V.after(t_late)
        for i in range(TILES):
            V.mark(nc.vector.bn_stats(stats[:, i, 0, :], k.x_tok[:, i, 0:P]))
            t = V.mark(nc.vector.bn_stats(stats[:, i, 1, :], late[:, i, :]))
        V.after(t)
        for i in range(TILES):
            t = V.mark(nc.vector.bn_aggr(k.mv[:, i, :], stats[:, i, :, :].rearrange("p a s -> p (a s)")))
        t = A.mark(A.after(t, k.t_eps).activation(k.std[:], k.mv[:, :, 1], ACT.Sqrt, bias=k.eps[:, 0:1]))
        t = V.mark(V.after(t).reciprocal(k.rstd[:], k.std[:]))
        V.after(t)
        done = {}
        for i in range(TILES):
            for c, s in ((0, k.x_tok[:, i, 0:P]), (1, late[:, i, :])):
                done[i] = V.mark(nc.vector.tensor_scalar(h_tok[:, i, c * P:(c + 1) * P], s, k.mv[:, i, 0:1],
                                                         k.rstd[:, i:i + 1], ALU.subtract, ALU.mult))
        t_b2 = G.mark(G.after(*[done[i] for i in range(TILES)]).tensor_tensor(
            k.x_tok[:], k.x_tok[:], row(k, "b2", layer * D, (layer + 1) * D).unsqueeze(1).to_broadcast([P, TILES, D]), ALU.add))
        h_ready = to_channels(k, h_tok, h_ch, done, scale=lambda h: col(k, "lg", 2 * layer + h),
                              bias=lambda h: col(k, "lb", 2 * layer + h))

        def second(g, jh, hd, t_h):
            for pair in range(2):
                i, bank = k.banks.take(k.pe)
                k.pe.after(t_h)
                for s in range(2):
                    m = 2 * pair + s
                    for ft in range(HT):
                        rows = P if ft < HT - 1 else HLAST
                        ins = nc.tensor.matmul(bank[:, s * D:(s + 1) * D], hd[0:rows, ft, m * P:(m + 1) * P],
                                               w2[0:rows, ft, :], start=(ft == 0), stop=(ft == HT - 1))
                t = k.pe.mark(ins)
                for s in range(2):
                    tile = 4 * g + 2 * pair + s
                    ready[tile] = V.mark(V.after(t, t_b2).tensor_tensor(
                        k.x_tok[:, tile, :], bank[:, s * D:(s + 1) * D], k.x_tok[:, tile, :], ALU.add))
                k.banks.release(i, ready[tile])
            hidden.release(jh, k.pe.last())

        pending = None
        for g in range(4):
            jh, hd = hidden.take(V)
            for ft in range(HT):
                rows = P if ft < HT - 1 else HLAST
                got = []
                for part in range(2):
                    i, bank = k.banks.take(k.pe)
                    o = part * HID + ft * P
                    t = k.matmuls(bank[0:rows, :], [(w1[:, h, o:o + rows], h_ch[:, h, g * BANK:(g + 1) * BANK])
                                                    for h in range(HALVES)], t_w, *h_ready[g])
                    got.append((i, bank, t))
                jg, gg = gl.take(A)
                t = A.mark(A.after(got[1][2]).activation(gg[0:rows, :], got[1][1][0:rows, :], ACT.Gelu,
                                                         bias=col(k, "b1g", HT * layer + ft, rows)))
                k.banks.release(got[1][0], t)
                t_h = V.mark(V.after(t, got[0][2]).scalar_tensor_tensor(
                    hd[0:rows, ft, :], got[0][1][0:rows, :], col(k, "b1a", HT * layer + ft, rows), gg[0:rows, :],
                    ALU.add, ALU.mult))
                k.banks.release(got[0][0], t_h)
                gl.release(jg, t_h)
            if pending:
                second(*pending)
            pending = (g, jh, hd, t_h)
        second(*pending)
        if layer == 0:
            k.ch = to_channels(k, k.x_tok, k.x_ch, ready)
        k.barrier()


STAGES = [rwkv, bitnet, experts, linear_attention, cross_attention, windowed]


def store(k):
    sem = k.sem("stored")
    k.sp.after(*[k.tok[i] for i in range(TILES)])
    k.nc.sync.dma_start(k.dram["out"].rearrange("(n p) d -> p n d", p=P), k.x_tok[:]).then_inc(sem, 16)
    k.nc.sync.wait_ge(sem, 16)


def build(nc, dram, stages=range(6)):
    dram["kept"] = nc.dram_tensor("kept", (P, TILES, D), F32, kind="Internal").ap()
    dram["regroup"] = nc.dram_tensor("regroup", (B, N0, N0, H0, T // N0), F32, kind="Internal").ap()
    k = Core(nc, dram)
    with k.ctx:
        setup(k)
        for n in stages:
            STAGES[n](k)
        store(k)


def host_layout(inp):
    f = lambda n: np.asarray(inp[n])
    chan = lambda a: np.asarray(a).reshape(-1, P).T

    def hidden(a):
        z = np.zeros((HT * P,), a.dtype)
        z[:HID] = a
        return z.reshape(HT, P).T

    b1 = f("L1_ffn_b1")
    cols = {
        "maa_k": chan(f("L0_attn_time_maa_k")), "maa_v": chan(f("L0_attn_time_maa_v")),
        "maa_r": chan(f("L0_attn_time_maa_r")), "maa_g": chan(f("L0_attn_time_maa_g")),
        "decay": chan(np.repeat(f("L0_attn_time_decay"), N0)),
        "b_d2v": chan(f("L0_xattn_b_d2v")), "b_img": chan(f("L0_xattn_b_img")), "b_txt": chan(f("L0_xattn_b_txt")),
        "b_att0": chan(f("L0_xattn_b_att0")), "b_att1": chan(f("L0_xattn_b_att1")), "b_f1": chan(f("L0_xattn_b_f1")),
        "moe_gamma": chan(f("L0_ffn_gamma")), "moe_beta": chan(f("L0_ffn_beta")), "moe_b1": chan(f("L0_ffn_b1")),
        "la_bq": chan(f("L1_attn_b_qkv")[:D]), "xa_bq": chan(f("L1_xattn_bq")), "xa_bk": chan(f("L1_xattn_bk")),
        "lg": chan(f("L1_ffn_ln_g")), "lb": chan(f("L1_ffn_ln_b")),
        "b1a": np.concatenate([hidden(b1[l, :HID]) for l in range(2)], 1),
        "b1g": np.concatenate([hidden(b1[l, HID:]) for l in range(2)], 1),
    }
    rows = {
        "decay": f("L0_attn_time_decay"), "faaaa": f("L0_attn_time_faaaa"), "ln_g": f("L0_attn_ln_g"),
        "ln_b": f("L0_attn_ln_b"), "b_att0": f("L0_xattn_b_att0"), "b_att1": f("L0_xattn_b_att1"),
        "b_f2": f("L0_xattn_b_f2"), "la_bkv": f("L1_attn_b_qkv")[D:], "la_bproj": f("L1_attn_b_proj"),
        "la_gamma": f("L1_attn_gamma"), "la_beta": f("L1_attn_beta"), "xa_bv": f("L1_xattn_bv"),
        "xa_bo": f("L1_xattn_bo"), "q_scale": f("L1_ffn_q_scale").reshape(-1),
        "k_scale": f("L1_ffn_k_scale").reshape(-1), "b2": f("L1_ffn_b2").reshape(-1),
    }
    x = f("x").reshape(NTOK, D)
    return {
        "const": shape_constants(), "rotary": rotary_tables(), "mask": window_mask(),
        "cols": np.concatenate([cols[n] for n, _ in COLS], 1), "rows": np.concatenate([rows[n] for n, _ in ROWS]),
        "x": x, "xT": x.T, "ctxT": f("ctx_768").transpose(2, 0, 1),
        **{"w_%sT" % n: f("L0_attn_w_" + n).T for n in "rkvgo"},
        **{"bn_" + n: f("L0_xattn_W_" + n).T for n in ("d2v", "img", "txt", "att0", "att1", "f1", "f2")},
        "moe_wg": f("L0_ffn_Wg"), "moe_w1": f("L0_ffn_W1"), "moe_w2": f("L0_ffn_W2"), "moe_b2": f("L0_ffn_b2"),
        "la_qkvT": f("L1_attn_W_qkv").T, "la_projT": f("L1_attn_W_proj").T,
        "xa_q": f("L1_xattn_Wq"), "xa_k": f("L1_xattn_Wk"), "xa_v": f("L1_xattn_Wv"), "xa_o": f("L1_xattn_Wo"),
        "wqkv": f("L1_ffn_wqkv"), "wo": f("L1_ffn_wo"), "w1": f("L1_ffn_w1"), "w2": f("L1_ffn_w2"),
    }


def kernel(**inputs):
    import concourse.bacc as bacc
    from concourse.bass_utils import run_bass_kernel_spmd

    nc = bacc.Bacc("TRN2", target_bir_lowering=False, num_devices=1)
    arrays = {n: np.ascontiguousarray(a) for n, a in host_layout(inputs).items()}
    dram = {n: nc.dram_tensor("in_" + n, a.shape, mybir.dt.from_np(a.dtype), kind="ExternalInput").ap()
            for n, a in arrays.items()}
    dram["out"] = nc.dram_tensor("out", (NTOK, D), F32, kind="ExternalOutput").ap()
    build(nc, dram)
    r = run_bass_kernel_spmd(nc, [{"in_" + n: a for n, a in arrays.items()}], core_ids=[0])
    return r.results[0]["out"].reshape(B, T, D)
```

```python
from contextlib import ExitStack

import numpy as np
import concourse.bass as bass
from concourse import mybir

F32 = mybir.dt.float32
BF16 = mybir.dt.bfloat16
ALU = mybir.AluOpType
ACT = mybir.ActivationFunctionType
AX = mybir.AxisListType

P = 128
B, T, D = 4, 512, 256
NTOK = B * T
TILES = NTOK // P
TPB = T // P
HALVES = D // P
BANK = 512
S2, DC = 1601, 192
CP = DC // 2
KT = -(-S2 // P)
KLAST = S2 - (KT - 1) * P
ROUND = 12582912.0
NE, FF = 8, 1024
H0, N0 = 16, 16
HX, NX = 8, 32
HL, NL = 8, 64
INNER = HL * NL
HID = int(D * 4 * 2 / 3)
HT = -(-HID // P)
HLAST = HID - (HT - 1) * P
MASKED = -1e30
PASSES = ((0, 0), (1, 0), (0, 1))


COLS = [("maa_k", 2), ("maa_v", 2), ("maa_r", 2), ("maa_g", 2), ("decay", 2), ("ln_g", 2), ("ln_b", 2),
        ("b_d2v", 2), ("b_img", 2), ("b_txt", 2), ("b_att0", 1), ("b_att1", 1), ("b_f1", 8),
        ("moe_gamma", 16), ("moe_beta", 16), ("moe_b1", 64), ("la_bq", 2), ("xa_bq", 2), ("xa_bk", 2),
        ("lg", 4), ("lb", 4), ("b1a", 2 * HT), ("b1g", 2 * HT)]
ROWS = [("decay", H0), ("faaaa", H0), ("b_att0", P), ("b_att1", P),
        ("b_f2", D), ("la_bkv", 2 * D), ("la_bproj", D), ("la_gamma", D), ("la_beta", D),
        ("xa_bv", D), ("xa_bo", D), ("q_scale", 2 * NL), ("k_scale", 2 * NL), ("b2", 2 * D)]
CONSTS = [("ident", P), ("expo", P), ("later", P), ("diag16", P), ("ramp", P), ("head16", 8),
          ("left", 1), ("ones", P), ("lower", 64), ("fold", NX + 1), ("shift", P), ("carry", P)]


def offsets(items):
    at, n = {}, 0
    for name, width in items:
        at[name] = (n, width)
        n += width
    return at, n


COL_AT, NCOL = offsets(COLS)
ROW_AT, NROW = offsets(ROWS)
CONST_AT, NCONST = offsets(CONSTS)


def shape_constants():
    c = np.zeros((P, NCONST), np.float32)

    def put(name, a):
        o, w = CONST_AT[name]
        c[:, o:o + w] = a

    j, t = np.arange(P)[:, None], np.arange(P)[None, :]
    put("ident", j == t)
    put("expo", np.maximum(t - j - 1, 0))
    put("later", t > j)
    put("diag16", j // N0 == t // N0)
    put("ramp", t + 0 * j)
    put("head16", j // N0 == np.arange(8)[None, :])
    put("left", P - 1 - j)
    put("ones", 1.0)
    e = np.arange(NE)
    put("lower", np.tile((e[None, :] < e[:, None]).astype(np.float32).reshape(1, 64), (P, 1)))
    put("shift", t == j + 1)
    put("carry", (j == P - 1) & (t == 0))
    put("fold", j % (NX + 1) == np.arange(NX + 1)[None, :])
    return c


def rotary_tables():
    f32 = np.float32
    half = np.arange(0, NL, 2, dtype=f32)
    inv = (f32(1.0) / f32(10000.0) ** (half / f32(NL))).astype(f32)
    t = np.arange(T, dtype=f32)
    fr = (t[:, None] * inv[None, :]).astype(f32)
    fr = np.concatenate([fr, fr], -1)
    base = ((half + f32(0.4 * NL)) / f32(1.4 * NL)).astype(f32)
    power = ((t - T // 2) / f32(P // 2)).astype(f32)
    sc = (base[None, :] ** power[:, None]).astype(f32)
    sc = np.concatenate([sc, sc], -1)
    sign = np.where(np.arange(NL) < NL // 2, -1.0, 1.0).astype(f32)
    cos, sin = np.cos(fr).astype(f32), np.sin(fr).astype(f32) * sign
    tab = np.stack([cos * sc, sin * sc, cos / sc, sin / sc], 1).astype(f32)
    return np.ascontiguousarray(tab.reshape(TPB, P, 4, NL).transpose(1, 0, 2, 3))


def window_mask():
    i, j = np.arange(P)[:, None], np.arange(2 * P)[None, :]
    return np.where((j >= i) & (j <= i + P), 0.0, MASKED).astype(np.float32)


class Queue:

    def __init__(self, engine, sem):
        self.engine, self.sem, self.count, self.seen = engine, sem, 0, {}

    def after(self, *tokens):
        need = {}
        for token in tokens:
            if token is not None:
                need[token[0]] = max(need.get(token[0], 0), token[1])
        for sem, value in need.items():
            if self.seen.get(sem, 0) < value:
                self.engine.wait_ge(sem, value)
                self.seen[sem] = value
        return self.engine

    def mark(self, instruction):
        instruction.then_inc(self.sem, 1)
        self.count += 1
        return self.sem, self.count

    def last(self):
        return (self.sem, self.count) if self.count else None


class Ring:

    def __init__(self, slots):
        self.slots = slots
        self.idle = [(i, ()) for i in range(len(slots))]
        self.readers = [()] * len(slots)

    def take(self, queue):
        i, tokens = self.idle.pop(0)
        self.readers[i] = tokens
        queue.after(*tokens)
        return i, self.slots[i]

    def release(self, i, *tokens):
        self.idle.append((i, tokens))


class Core:
    def __init__(self, nc, dram):
        self.nc, self.dram = nc, dram
        self.ctx = ExitStack()
        self.nsem = 0
        self.pe = Queue(nc.tensor, self.sem("pe_done"))
        self.dve = Queue(nc.vector, self.sem("dve_done"))
        self.act = Queue(nc.scalar, self.sem("act_done"))
        self.pool = Queue(nc.gpsimd, self.sem("pool_done"))
        self.sp = Queue(nc.sync, self.sem("sp_done"))
        self.stored = self.sem("stored")
        self.loads = []

    def sem(self, name):
        self.nsem += 1
        return self.ctx.enter_context(self.nc.semaphore(name))

    def sb(self, ctx, name, shape, dt=F32):
        return ctx.enter_context(self.nc.sbuf_tensor(name, list(shape), dt))

    def load(self, name, *pairs, after=()):
        sem = self.sem("loaded_" + name)
        self.sp.after(*after)
        for dst, src in pairs:
            self.nc.sync.dma_start(dst, src).then_inc(sem, 16)
        token = (sem, 16 * len(pairs))
        self.loads.append(token)
        return token

    def barrier(self):
        every = [q.last() for q in (self.pe, self.dve, self.act, self.pool)] + self.loads
        self.loads = []
        for q in (self.pe, self.dve, self.act, self.pool, self.sp):
            q.after(*every)

    def matmuls(self, out, pairs, *after, first=True, last=True, skip=False):
        eng = self.pe.after(*after)
        for n, (lhsT, rhs) in enumerate(pairs):
            ins = eng.matmul(out, lhsT, rhs, start=first and n == 0, stop=last and n == len(pairs) - 1,
                             skip_group_check=skip)
        return self.pe.mark(ins)


def setup(k):
    nc, ctx = k.nc, k.ctx
    k.psum = ctx.enter_context(nc.psum_tensor("psum", [P, 8, BANK], F32))
    k.x_tok = k.sb(ctx, "x_tok", [P, TILES, D])
    k.x_ch = k.sb(ctx, "x_ch", [P, HALVES, NTOK])
    k.const = k.sb(ctx, "const", [P, NCONST])
    k.cols = k.sb(ctx, "cols", [P, NCOL])
    k.rows = k.sb(ctx, "rows", [P, NROW])
    k.stats = k.sb(ctx, "ln_stats", [P, TILES, 6])
    k.mv = k.sb(ctx, "ln_mean_var", [P, TILES, 2])
    k.std = k.sb(ctx, "ln_std", [P, TILES])
    k.rstd = k.sb(ctx, "ln_rstd", [P, TILES])
    k.eps = k.sb(ctx, "eps", [P, 4])
    k.banks = Ring([k.psum[:, 4 + n, :] for n in range(4)])
    k.score_free = ()
    for n, v in enumerate((1e-5, 1e-6, 64e-5, 0.0)):
        t = k.dve.mark(nc.vector.memset(k.eps[:, n:n + 1], v))
    k.t_eps = t
    k.t_param = k.load("params", (k.const[:], k.dram["const"]), (k.cols[:], k.dram["cols"]),
                       (k.rows[:], k.dram["rows"].partition_broadcast(P)))
    k.ch = {}
    load_channels(k, 0)


def load_channels(k, b):
    cb = slice(b * T, (b + 1) * T)
    k.ch[b] = [k.load("x_ch%d" % b, (k.x_ch[:, :, cb], k.dram["xT"].rearrange("(h p) t -> p h t", p=P)[:, :, cb]))]


def load_rest(k):
    for b in range(1, B):
        load_channels(k, b)
    t = k.load("x_tok", (k.x_tok[:], k.dram["x"].rearrange("(n p) d -> p n d", p=P)))
    k.tok = {i: t for i in range(TILES)}


def const(k, name, rows=P):
    o, w = CONST_AT[name]
    return k.const[0:rows, o:o + w]


def col(k, name, n=0, rows=P):
    o, _ = COL_AT[name]
    return k.cols[0:rows, o + n:o + n + 1]


def row(k, name, a=0, b=None):
    o, w = ROW_AT[name]
    return k.rows[:, o + a:o + (w if b is None else b)]


def evacuate(k, n, out, bank, *after):
    if n % 2:
        return k.dve.mark(k.dve.after(*after).tensor_copy(out, bank))
    return k.act.mark(k.act.after(*after).copy(out, bank))


def layer_norm(k, src, dst, ready, eps_col, tiles=range(TILES)):
    done = {}
    tiles = list(tiles)
    for g in range(0, len(tiles), 4):
        group = tiles[g:g + 4]
        a, b = group[0], group[-1] + 1
        for i in group:
            t = k.dve.mark(k.dve.after(ready[i]).bn_stats(k.stats[:, i, :], src[:, i, :]))
        k.dve.after(t)
        for i in group:
            t = k.dve.mark(k.nc.vector.bn_aggr(k.mv[:, i, :], k.stats[:, i, :]))
        t = k.act.mark(k.act.after(t, k.t_eps, k.t_param).activation(
            k.std[:, a:b], k.mv[:, a:b, 1], ACT.Sqrt, bias=k.eps[:, eps_col:eps_col + 1]))
        t = k.dve.mark(k.dve.after(t).reciprocal(k.rstd[:, a:b], k.std[:, a:b]))
        k.dve.after(t)
        for i in group:
            done[i] = k.dve.mark(k.nc.vector.tensor_scalar(
                dst[:, i, :], src[:, i, :], k.mv[:, i, 0:1], k.rstd[:, i:i + 1],
                ALU.subtract, ALU.mult))
    return done


def to_channels(k, src, dst, ready, scale=None, bias=None, free=(), groups=range(4)):
    done = {}
    for g in groups:
        tokens = []
        for h in range(HALVES):
            i, bank = k.banks.take(k.pe)
            k.pe.after(k.t_param, *[ready[4 * g + m] for m in range(4)])
            for m in range(4):
                ins = k.nc.tensor.transpose(bank[:, m * P:(m + 1) * P],
                                            src[:, 4 * g + m, h * P:(h + 1) * P], const(k, "ident"))
            t = k.pe.mark(ins)
            out = dst[:, h, g * BANK:(g + 1) * BANK]
            if scale is None:
                t = evacuate(k, h, out, bank, t, *free)
            else:
                t = k.act.mark(k.act.after(t, *free).activation(out, bank, ACT.Identity,
                                                                scale=scale(h), bias=bias(h)))
            k.banks.release(i, t)
            tokens.append(t)
        done[g] = tokens
    return done


def mingle(main, side):
    steps, done = [], 0
    for n, step in enumerate(main):
        want = len(side) * (n + 1) // len(main)
        steps += [step] + side[done:want]
        done = want
    return steps


def run(steps):
    for step in steps:
        step()


def norm_group(k, ready, g):
    k.tok.update(layer_norm(k, k.x_tok, k.x_tok, ready, 0, range(4 * g, 4 * g + 4)))


def channels_group(k, g, *free):
    k.ch.update(to_channels(k, k.x_tok, k.x_ch, k.tok, free=free, groups=(g,)))


def rwkv(k):
    nc, A, V, G = k.nc, k.act, k.dve, k.pool
    with ExitStack() as ctx:
        sb = lambda name, shape, dt=F32: k.sb(ctx, name, shape, dt)
        ring = lambda name, n, shape, dt=F32: Ring([sb("%s%d" % (name, i), shape, dt) for i in range(n)])
        w = {n: sb("w_" + n, [P, HALVES, D]) for n in "rkvgo"}
        t_w = {n: k.load("w_" + n, (w[n][:], k.dram["w_%sT" % n].rearrange("(h p) o -> p h o", p=P))) for n in "rkvgo"}
        load_rest(k)
        rate_row, rate_col = sb("rate_row", [P, H0]), sb("rate_col", [P, 2])
        nrate_row, nrate_col = sb("nrate_row", [P, H0]), sb("nrate_col", [P, 2])
        wmat = sb("decay_mask", [P, H0, P])
        wkey = sb("key_decay", [P, H0])
        wquery = sb("query_decay", [P, 2, P])
        wstate = sb("state_decay", [P, 2])

        steps_x, mixes = ring("x_step", 2, [P, HALVES, T]), ring("mix", 3, [P, HALVES, T])
        r_heads = ring("r_heads", 3, [P, 8, P])
        r_state = ring("r_state", 2, [P, HALVES, T])
        r_ch, k_ch, gate = (ring(n, 2, [P, HALVES, T]) for n in ("r_ch", "k_ch", "gate"))
        k_tok = ring("k_tok", 2, [P, TPB, D])
        v_tok = [sb("v_tok%d" % n, [P, TPB, H0 // 2, 3, N0]) for n in range(2)]
        masked = ring("a_masked", 3, [P, 4, P])
        state = ring("state", 2, [P, HALVES, P])
        outer = ring("outer", 2, [P, HALVES, P])
        y_ch, sq_ch = ring("y_ch", 2, [P, HALVES, T]), ring("sq_ch", 1, [P, HALVES, T])
        std = ring("g_std", 1, [P, HALVES, T])
        score_banks = Ring([k.psum[:, n, :] for n in range(4)])
        for n in range(2):
            t_zero = G.mark(nc.gpsimd.memset(v_tok[n][:, :, :, 1, :], 0.0))
        v_tok = Ring(v_tok)
        batch, ready = {}, {}

        def produce(b):
            s = batch[b] = {}
            cb = slice(b * T, (b + 1) * T)

            def step_x():
                s["jx"], s["x"] = j, xx = steps_x.take(V)
                V.after(*k.ch[b])
                x = k.x_ch[:, :, cb]
                V.mark(nc.vector.tensor_tensor(xx[:, :, 1:T], x[:, :, 0:T - 1], x[:, :, 1:T], ALU.subtract))
                s["t_x"] = V.mark(nc.vector.tensor_scalar(xx[:, :, 0:1], x[:, :, 0:1], -1.0, None, ALU.mult))

            def mix(name):
                i, m = mixes.take(V)
                V.after(s["t_x"])
                for c in range(HALVES):
                    t = V.mark(nc.vector.scalar_tensor_tensor(m[:, c, :], s["x"][:, c, :], col(k, "maa_" + name, c),
                                                              k.x_ch[:, c, cb], ALU.mult, ALU.add))
                s["mix", name] = (i, m, t)
                if name == "g":
                    steps_x.release(s["jx"], t)
                    s["t_mixed"] = t

            def channels(name, c, out, finish):
                _, m, t_m = s["mix", name]
                i, bank = k.banks.take(k.pe)
                t = k.matmuls(bank, [(w[name][:, h, c * P:(c + 1) * P], m[:, h, :]) for h in range(HALVES)], t_m, t_w[name])
                t = finish(out[:, c, :], bank, t)
                k.banks.release(i, t)
                return t

            def tokens(name, pair, finish):
                _, m, t_m = s["mix", name]
                i, bank = k.banks.take(k.pe)
                for x in range(2):
                    tl = 2 * pair + x
                    t = k.matmuls(bank[:, x * D:(x + 1) * D], [(m[:, h, tl * P:(tl + 1) * P], w[name][:, h, :])
                                                               for h in range(HALVES)], t_m, t_w[name])
                t = finish(pair, bank, t)
                k.banks.release(i, t)
                return t

            def done(name):
                mixes.release(s["mix", name][0], k.pe.last())

            plain = lambda out, bank, t: A.mark(A.after(t).copy(out, bank))
            silu = lambda out, bank, t: A.mark(A.after(t).activation(out, bank, ACT.Silu))

            def receptance(c):
                if c == 0:
                    s["jr"], s["r"] = r_ch.take(A)
                    s["jrs"], s["rs"] = r_state.take(V)
                s["t_r"] = channels("r", c, s["r"], plain)
                s["t_rs"] = V.mark(V.after(s["t_r"], *t_tab).tensor_tensor(
                    s["rs"][:, c, :].rearrange("p (n t) -> p n t", t=P), s["r"][:, c, :].rearrange("p (n t) -> p n t", t=P),
                    wquery[:, c, :].unsqueeze(1).to_broadcast([P, TPB, P]), ALU.mult))
                if c:
                    done("r")

            def key(c):
                if c == 0:
                    s["jk"], s["k"] = k_ch.take(A)
                s["t_k"] = channels("k", c, s["k"], plain)

            def key_tokens(pair):
                if pair == 0:
                    s["jkt"], s["kt"] = k_tok.take(V)

                def finish(pair, bank, t):
                    wk = wkey[:].unsqueeze(1).unsqueeze(3).to_broadcast([P, 2, H0, N0])
                    return V.mark(V.after(t, *t_tab).tensor_tensor(
                        s["kt"][:, 2 * pair:2 * pair + 2, :].rearrange("p s (h n) -> p s h n", n=N0),
                        bank.rearrange("p (s h n) -> p s h n", s=2, n=N0), wk, ALU.mult))
                s["t_kt"] = tokens("k", pair, finish)
                if pair:
                    done("k")

            def value(pair):
                if pair == 0:
                    s["jv"], s["v"] = v_tok.take(A)

                def finish(pair, bank, t):
                    A.after(t, t_zero)
                    for x in range(2):
                        t = A.mark(nc.scalar.copy(s["v"][:, 2 * pair + x, :, 0:3:2, :],
                                                  bank[:, x * D:(x + 1) * D].rearrange("p (q x c) -> p q x c", x=2, c=N0)))
                    return t
                s["t_v"] = tokens("v", pair, finish)
                if pair:
                    done("v")

            def gates(c):
                if c == 0:
                    s["jg"], s["g"] = gate.take(A)
                s["t_g"] = channels("g", c, s["g"], silu)
                if c:
                    done("g")

            two = lambda f: [lambda n=n: f(n) for n in range(2)]
            return ([step_x, lambda: mix("r"), lambda: mix("k")] + two(receptance) + [lambda: mix("v")] + two(key)
                    + two(key_tokens) + [lambda: mix("g")] + two(value) + two(gates))

        def attend(b):
            s = batch[b]
            flying = []

            def open_chunk(c):
                tl = slice(c * P, (c + 1) * P)
                if c == 0:
                    s["jy"], s["y"] = y_ch.take(A)
                    js, st = state.take(G)
                    s["state"] = (js, st, G.mark(nc.gpsimd.memset(st[:], 0.0)))
                s["iy"], s["ybank"] = k.banks.take(k.pe)
                js, st, t_state = s["state"]
                k.pe.after(t_state, s["t_rs"])
                for h in range(HALVES):
                    ins = nc.tensor.matmul(s["ybank"][:, h * P:(h + 1) * P], st[:, h, :], s["rs"][:, h, tl],
                                           start=(h == 0), stop=False, skip_group_check=True)
                t_read = k.pe.mark(ins)
                if c == TPB - 1:
                    state.release(js, t_read)
                    return
                i, bank = k.banks.take(k.pe)
                k.pe.after(s["t_kt"], s["t_v"])
                for h in range(HALVES):
                    ins = nc.tensor.matmul(bank[:, h * P:(h + 1) * P], s["kt"][:, c, h * P:(h + 1) * P],
                                           s["v"][:, c, 4 * h:4 * h + 4, 0:3:2, :], start=True, stop=True)
                t = k.pe.mark(ins)
                jo, ou = outer.take(V)
                t = V.mark(V.after(t).tensor_tensor(ou[:], bank[:, 0:D].rearrange("p (h v) -> p h v", v=P),
                                                    const(k, "diag16").unsqueeze(1).to_broadcast([P, 2, P]), ALU.mult))
                k.banks.release(i, t)
                jn, new = state.take(V)
                V.after(t, t_state)
                for h in range(HALVES):
                    t = V.mark(nc.vector.scalar_tensor_tensor(new[:, h, :], st[:, h, :], wstate[:, h:h + 1],
                                                              ou[:, h, :], ALU.mult, ALU.add))
                outer.release(jo, t)
                state.release(js, t_read, t)
                s["state"] = (jn, new, t)

            def heads(c, h):
                jh, rh = r_heads.take(G)
                t = G.mark(G.after(s["t_r"]).tensor_tensor(
                    rh[:], s["r"][:, h, c * P:(c + 1) * P].unsqueeze(1).to_broadcast([P, 8, P]),
                    const(k, "head16").unsqueeze(2).to_broadcast([P, 8, P]), ALU.mult))
                s["heads", c, h] = (jh, rh, t)
                if (c, h) == (TPB - 1, 1):
                    r_ch.release(s["jr"], t, s["t_rs"])

            def score(c, q):
                h = q // 2
                if c == 0 and q == 0:
                    heads(0, 0)
                if q % 2 == 0:
                    nxt = (c, 1) if h == 0 else (c + 1, 0)
                    if nxt[0] < TPB:
                        heads(*nxt)
                if q == 0:
                    open_chunk(c)
                jh, rh, t_h = s["heads", c, h]
                i, bank = score_banks.take(k.pe)
                t = k.matmuls(bank, [(s["k"][:, h, c * P:(c + 1) * P], rh[:, 4 * (q % 2):4 * (q % 2) + 4, :])], s["t_k"], t_h)
                if q % 2:
                    r_heads.release(jh, t)
                ia, am = masked.take(V)
                t = V.mark(V.after(t, *t_tab).tensor_tensor(am[:], bank.rearrange("p (a t) -> p a t", t=P),
                                                            wmat[:, 4 * q:4 * q + 4, :], ALU.mult))
                score_banks.release(i, t)
                flying.append((c, q, ia, am, t, s["iy"], s["ybank"]))

            def product():
                c, q, ia, am, t, iy, ybank = flying.pop(0)
                k.pe.after(t, s["t_v"])
                for a in range(4):
                    hd = 4 * q + a
                    p, x = divmod(hd, 2)
                    at = 32 * (p % 4)
                    pad = s["v"][:, c, p, x:x + 2, :].rearrange("p x c -> p (x c)")
                    ins = nc.tensor.matmul(ybank[at:at + 32, (q // 2) * P:(q // 2 + 1) * P], pad, am[:, a, :],
                                           start=False, stop=False, skip_group_check=True)
                t = k.pe.mark(ins)
                masked.release(ia, t)
                if q == 3:
                    s["t_y"] = A.mark(A.after(t).copy(s["y"][:, :, c * P:(c + 1) * P],
                                                      ybank[:, 0:D].rearrange("p (h t) -> p h t", t=P)))
                    k.banks.release(iy, s["t_y"])
                if (c, q) == (TPB - 1, 3):
                    r_state.release(s["jrs"], t)
                    k_ch.release(s["jk"], t)
                    k_tok.release(s["jkt"], t)
                    v_tok.release(s["jv"], t)

            def step(c, q):
                score(c, q)
                if len(flying) > 2:
                    product()

            def drain():
                while flying:
                    product()
            return [lambda c=c, q=q: step(c, q) for c in range(TPB) for q in range(4)] + [drain]

        def finish(b):
            s = batch[b]
            y = lambda h: s["y"][:, h, :]

            def center(h):
                if h == 0:
                    s["jq"], s["sq"] = sq_ch.take(A)
                    s["js"], s["std"] = std.take(A)
                i, bank = k.banks.take(k.pe)
                t = k.matmuls(bank, [(const(k, "diag16"), y(h))], s["t_y"])
                t = V.mark(V.after(t).scalar_tensor_tensor(y(h), bank, -1.0 / N0, y(h), ALU.mult, ALU.add))
                k.banks.release(i, t)
                s["t_c", h] = t
                s["t_sq", h] = A.mark(A.after(t).activation(s["sq"][:, h, :], y(h), ACT.Square))

            def variance(h):
                i, bank = k.banks.take(k.pe)
                t = k.matmuls(bank, [(const(k, "diag16"), s["sq"][:, h, :])], s["t_sq", h])
                if h:
                    sq_ch.release(s["jq"], t)
                sd = s["std"][:, h, :]
                t = A.mark(A.after(t, k.t_eps).activation(sd, bank, ACT.Sqrt, scale=1.0 / N0, bias=k.eps[:, 2:3]))
                k.banks.release(i, t)
                s["t_sd", h] = t

            def invert(h, n):
                sd = s["std"][:, h, n * T // 2:(n + 1) * T // 2]
                s["t_inv", h] = V.mark(V.after(s["t_sd", h]).reciprocal(sd, sd))

            def gated(h):
                t = V.mark(V.after(s["t_inv", h]).scalar_tensor_tensor(y(h), y(h), col(k, "ln_g", h), s["std"][:, h, :],
                                                                      ALU.mult, ALU.mult))
                if h:
                    std.release(s["js"], t)
                t = V.mark(V.after(t, s["t_g"]).scalar_tensor_tensor(y(h), y(h), col(k, "ln_b", h), s["g"][:, h, :],
                                                                     ALU.add, ALU.mult))
                s["t_z", h] = t
                if h:
                    gate.release(s["jg"], t)

            def project(pair):
                i, bank = k.banks.take(k.pe)
                for x in range(2):
                    n = 2 * pair + x
                    t = k.matmuls(bank[:, x * D:(x + 1) * D], [(s["y"][:, h, n * P:(n + 1) * P], w["o"][:, h, :])
                                                               for h in range(HALVES)], s["t_z", 0], s["t_z", 1], t_w["o"])
                if pair:
                    y_ch.release(s["jy"], t)
                tile = b * TPB + 2 * pair
                t = V.mark(V.after(t, k.tok[tile]).tensor_tensor(
                    k.x_tok[:, tile:tile + 2, :], bank.rearrange("p (x d) -> p x d", x=2), k.x_tok[:, tile:tile + 2, :], ALU.add))
                k.banks.release(i, t)
                ready[tile] = ready[tile + 1] = t

            two = lambda f: [lambda n=n: f(n) for n in range(2)]
            inverts = [lambda h=h, n=n: invert(h, n) for h in range(HALVES) for n in range(2)]
            return (two(center) + two(variance) + inverts + two(gated) + two(project),
                    [lambda: norm_group(k, ready, b), lambda: channels_group(k, b, s["t_mixed"])])

        first = produce(0)
        run(first[0:3])

        t = A.mark(A.after(k.t_param).activation(rate_row[:], row(k, "decay"), ACT.Exp))
        o, _ = COL_AT["decay"]
        t = A.mark(nc.scalar.activation(rate_col[:], k.cols[:, o:o + 2], ACT.Exp))
        V.after(t)
        V.mark(nc.vector.tensor_scalar(nrate_row[:], rate_row[:], -1.0, None, ALU.mult))
        t = V.mark(nc.vector.tensor_scalar(nrate_col[:], rate_col[:], -1.0, None, ALU.mult))
        A.after(t)
        for h in range(H0):
            A.mark(nc.scalar.activation(wmat[:, h, :], const(k, "expo"), ACT.Exp, scale=nrate_row[:, h:h + 1]))
        for c in range(2):
            A.mark(nc.scalar.activation(wquery[:, c, :], const(k, "ramp"), ACT.Exp, scale=nrate_col[:, c:c + 1]))
        A.mark(nc.scalar.activation(wstate[:], nrate_col[:], ACT.Exp, scale=float(P)))
        t2 = A.mark(nc.scalar.activation(wkey[:], nrate_row[:], ACT.Exp, scale=const(k, "left")))
        t = G.mark(G.after(t2).tensor_tensor(wmat[:], wmat[:], const(k, "later").unsqueeze(1).to_broadcast([P, H0, P]), ALU.mult))
        V.after(t)
        for h in range(H0):
            t = V.mark(nc.vector.scalar_tensor_tensor(wmat[:, h, :], const(k, "ident"), row(k, "faaaa", h, h + 1),
                                                      wmat[:, h, :], ALU.mult, ALU.add))
        t_tab = (t, t2)
        run(first[3:])
        for b in range(B):
            side, last = finish(b - 1) if b else ([], [])
            side += last[0:1] + [lambda: None] * 2 + last[1:]
            projections = produce(b + 1) if b + 1 < B else []
            run(mingle(attend(b), mingle(side, projections) if b else projections))
        side, last = finish(B - 1)
        for step in side + last:
            step()
        k.barrier()


def attention(k, ctx, tag, items, scale, dv):
    nc, V, A = k.nc, k.dve, k.act
    probs = Ring([k.sb(ctx, "probs%d_%s" % (n, tag), [P, S2]) for n in range(2)])
    turned = Ring([k.sb(ctx, "probs_t%d_%s" % (n, tag), [P, KT, P]) for n in range(2)])
    maxes, nmax, sums, rsums = (k.sb(ctx, "softmax%d_%s" % (n, tag), [P, len(items), 2]) for n in range(4))
    scores = k.psum[:, 0:4, :].rearrange("p b c -> p (b c)")
    PARTS = ((0, 2 * BANK), (2 * BANK, S2))
    free = [k.score_free, k.score_free]

    def score(n, part):
        it = items[n]
        a, e = PARTS[part]
        k.pe.after(*free[part], *it["ready"])
        for c0 in range(a, e, BANK):
            c1 = min(c0 + BANK, e)
            pairs = list(zip(it["query"], it["keys"](c0, c1)))
            t = k.matmuls(scores[:, c0:c1], pairs)
        it["t_score", part] = t

    def maximum(n, part):
        it = items[n]
        a, e = PARTS[part]
        it["t_max", part] = V.mark(V.after(it["t_score", part]).tensor_reduce(
            maxes[:, n, part:part + 1], scores[:, a:e], AX.X, ALU.max))

    def exponentials(n):
        it = items[n]
        m = nmax[:, n, 0:1]
        t = V.mark(V.after(it["t_max", 1]).tensor_tensor(m, maxes[:, n, 0:1], maxes[:, n, 1:2], ALU.max))
        t = V.mark(V.after(t).tensor_scalar(m, m, -scale, None, ALU.mult))
        it["jp"], pr = probs.take(A)
        it["p"] = pr
        A.after(t)
        for part, (a, e) in enumerate(PARTS):
            t = A.mark(nc.scalar.activation(pr[:, a:e], scores[:, a:e], ACT.Exp, bias=m, scale=scale,
                                            accum_out=sums[:, n, part:part + 1]))
            free[part] = (t,)
            it["t_exp", part] = t
        k.score_free = free[1]

    def turn(n, g):
        it = items[n]
        if g == 0:
            it["jt"], it["pt"] = turned.take(A)
            V.after(*turned.readers[it["jt"]])
        i, bank = k.banks.take(k.pe)
        k.pe.after(it["t_exp", g // 2])
        tiles = range(4 * g, min(4 * g + 4, KT))
        for kt in tiles:
            rows = P if kt < KT - 1 else KLAST
            ins = nc.tensor.transpose(bank[0:rows, (kt % 4) * P:(kt % 4 + 1) * P],
                                      it["p"][:, kt * P:kt * P + rows], const(k, "ident"))
        it["t_turn", g] = k.pe.mark(ins)
        it["b", g] = (i, bank, tiles)
        if g == 3:
            probs.release(it["jp"], it["t_turn", g])

    def copy(n, g):
        it = items[n]
        i, bank, tiles = it["b", g]
        rows, cnt = (P, 4) if len(tiles) == 4 else (KLAST, 1)
        it["t_copy", g] = t = evacuate(k, g % 2, it["pt"][0:rows, 4 * g:4 * g + cnt, :].rearrange("p a q -> p (a q)"),
                                       bank[0:rows, 0:cnt * P], it["t_turn", g])
        k.banks.release(i, t)

    def products(n):
        it = items[n]
        io, obank = k.banks.take(k.pe)
        for kt in range(KT):
            k.pe.after(it["t_copy", kt // 4])
            rows = P if kt < KT - 1 else KLAST
            ins = nc.tensor.matmul(obank[:, 0:dv], it["pt"][0:rows, kt, :], it["value"](kt, rows),
                                   start=(kt == 0), stop=(kt == KT - 1))
        t = k.pe.mark(ins)
        turned.release(it["jt"], t)
        it["o"] = (obank, io, t)

    def finish(n):
        it = items[n]
        m = rsums[:, n, 0:1]
        t = V.mark(V.after(it["t_exp", 1]).tensor_tensor(m, sums[:, n, 0:1], sums[:, n, 1:2], ALU.add))
        t = V.mark(V.after(t).reciprocal(m, m))
        obank, io, t_o = it["o"]
        return it["finish"](obank, io, m, (t_o, t))

    later = None
    for part in range(2):
        score(0, part)
        maximum(0, part)
    exponentials(0)
    for n in range(len(items)):
        more = n + 1 < len(items)
        turn(n, 0)
        turn(n, 1)
        copy(n, 0)
        copy(n, 1)
        if more:
            score(n + 1, 0)
            maximum(n + 1, 0)
        if later:
            later()
        turn(n, 2)
        turn(n, 3)
        copy(n, 2)
        copy(n, 3)
        if more:
            score(n + 1, 1)
            maximum(n + 1, 1)
            exponentials(n + 1)
        products(n)
        later = finish(n)
        if "also" in items[n]:
            items[n]["also"]()
    later()


def bitnet(k):
    nc, V, A = k.nc, k.dve, k.act
    KEYS = B * S2
    CH = [(b * S2 + -(-n * S2 // 4), b * S2 + -(-(n + 1) * S2 // 4)) for b in range(B) for n in range(4)]
    WID = {"d2v": 0, "img": 1, "txt": 2, "att0": 3, "att1": 4, "f1": 5, "f2": 6}
    with ExitStack() as outer:
        wsum = k.sb(outer, "w_abs_sum", [P, 8])
        wscale, wthr, wnthr = (k.sb(outer, n, [P, 8]) for n in ("w_scale", "w_thr", "w_nthr"))
        mcols = k.sb(outer, "max_cols", [P, 40])
        mrow, mone = k.sb(outer, "max_row", [1, P]), k.sb(outer, "max_one", [1, 1])
        iscale, inv, s_out = (k.sb(outer, n, [P, 12]) for n in ("i_scale", "i_inv", "out_scale"))
        fused = k.sb(outer, "fused", [P, HALVES, NTOK])
        avg, avg_parts = k.sb(outer, "avg_img", [P, HALVES * B]), k.sb(outer, "avg_parts", [P, HALVES, B, 4])
        q = {n: k.sb(outer, "bn_q_" + n, [P, c, o], BF16) for n, c, o in (("f1", 4, FF), ("f2", 8, D))}
        t_zero = V.mark(nc.vector.memset(wsum[:], 0.0))
        t_zero = V.mark(nc.vector.memset(mcols[:], 0.0))

        def ternary(names, raw, shapes, tmp, *free):
            t_l = k.load("bn_" + names[0], *[(raw[n][0:p], k.dram["bn_" + n].rearrange("(c p) o -> p c o", p=p))
                                             for n, (p, c, o) in zip(names, shapes)], after=free)
            yield
            V.after(t_l, t_zero)
            for n, (p, c, o) in zip(names, shapes):
                j = WID[n]
                t = V.mark(nc.vector.tensor_reduce(wsum[0:p, j:j + 1], raw[n][0:p], AX.XY, ALU.add,
                                                   apply_absolute_value=True))
                yield
            i, bank = k.banks.take(k.pe)
            t = k.matmuls(bank[:, 0:8], [(const(k, "ones"), wsum[:])], t, k.t_param)
            V.after(t)
            for n, (p, c, o) in zip(names, shapes):
                j = slice(WID[n], WID[n] + 1)
                t = V.mark(nc.vector.tensor_scalar(wscale[:, j], bank[:, j], 1.0 / (p * c * o), 1e-5, ALU.mult, ALU.max))
            k.banks.release(i, t)
            V.after(t)
            a, b = WID[names[0]], WID[names[-1]] + 1
            V.mark(nc.vector.tensor_scalar(wthr[:, a:b], wscale[:, a:b], 0.5, None, ALU.mult))
            t = V.mark(nc.vector.tensor_scalar(wnthr[:, a:b], wscale[:, a:b], -0.5, None, ALU.mult))
            for n, (p, c, o) in zip(names, shapes):
                j = slice(WID[n], WID[n] + 1)
                low = tmp[0:p, 0:c * o].rearrange("p (c o) -> p c o", o=o)
                t = V.mark(V.after(t).tensor_scalar(low, raw[n][0:p], wnthr[0:p, j], None, ALU.is_lt))
                yield
                t = V.mark(V.after(t).scalar_tensor_tensor(q[n][0:p], raw[n][0:p], wthr[0:p, j], low,
                                                           ALU.is_gt, ALU.subtract))
                t_tern[n] = t
                yield

        t_tern = {}

        def input_scale(slot, first, end, *ready):
            s = slice(slot, slot + 1)
            t = V.mark(V.after(*ready).tensor_reduce(mcols[:, 39:40], mcols[:, first:end], AX.X, ALU.max))
            i, bank = k.banks.take(k.pe)
            t = k.pe.mark(k.pe.after(t).transpose(bank[0:1, 0:P], mcols[:, 39:40], const(k, "ident")))
            t = V.mark(V.after(t).tensor_reduce(mone[:], bank[0:1, 0:P], AX.X, ALU.max))
            k.banks.release(i, t)
            i, bank = k.banks.take(k.pe)
            t = k.matmuls(bank[:, 0:1], [(const(k, "ones", 1), mone[:])], t)
            t = V.mark(V.after(t).tensor_scalar(iscale[:, s], bank[:, 0:1], 1e-8, 1.0 / 127.0, ALU.max, ALU.mult))
            k.banks.release(i, t)
            return V.mark(V.after(t).reciprocal(inv[:, s], iscale[:, s]))

        def out_scale(slot, wname, use, *ready):
            t = V.mark(V.after(*ready).tensor_tensor(s_out[:, use:use + 1], iscale[:, slot:slot + 1],
                                                     wscale[:, WID[wname]:WID[wname] + 1], ALU.mult))
            return t

        def quantize(slot, dst, src, rows, scalar, *ready):
            s = slice(slot, slot + 1)
            if scalar:
                t = A.mark(A.after(*ready).mul(src, src, inv[0:rows, s]))
            else:
                t = V.mark(V.after(*ready).tensor_scalar(src, src, inv[0:rows, s], None, ALU.mult))
            return V.mark(V.after(t).tensor_scalar(dst, src, ROUND, ROUND, ALU.add, ALU.subtract))

        with ExitStack() as ctx:
            big = k.sb(ctx, "ctx_f32", [P, KEYS + B * KT * P])
            q8 = k.sb(ctx, "ctx_q8", [P, HALVES, KEYS], BF16)
            qx = k.sb(ctx, "text_q8", [P, HALVES, NTOK], BF16)
            wide = big[:, 0:HALVES * KEYS].rearrange("p (h s) -> p h s", h=HALVES)
            names, shapes = ["d2v", "img", "txt", "att0", "att1"], [(CP, 2, D), (P, 2, D), (P, 2, D), (P, 2, P), (P, 2, P)]
            raw, at = {}, 0
            for n, (_, c, o) in zip(names, shapes):
                raw[n] = fused[:].rearrange("p h t -> p (h t)")[:, at:at + c * o].rearrange("p (c o) -> p c o", o=o)
                at += c * o
            q.update({n: k.sb(ctx, "bn_q_" + n, [P, c, o], BF16) for n, (_, c, o) in zip(names, shapes)})
            small_weights = ternary(names, raw, shapes, k.sb(ctx, "tern_tmp", [P, 2 * D], BF16))
            next(small_weights)
            t_ctx = [k.load("ctx%d" % h, (wide[0:CP, h, :], k.dram["ctxT"].rearrange("c b s -> c (b s)")[h * CP:(h + 1) * CP, :]))
                     for h in range(HALVES)]

            TEXT = 36
            t = V.mark(V.after(t_zero, *k.ch[3]).tensor_reduce(mcols[:, TEXT:TEXT + 1], k.x_ch[:], AX.XY, ALU.max,
                                                               apply_absolute_value=True))
            t = input_scale(3, TEXT, TEXT + 1, t)
            for _ in small_weights:
                pass
            t_q = t_tern["att1"]
            t_s = out_scale(3, "txt", 4, t, t_q)
            V.after(t_s)
            t_x = {(g, h): quantize(3, qx[:, h, g * BANK:(g + 1) * BANK], k.x_ch[:, h, g * BANK:(g + 1) * BANK], P, h, t_s)
                   for g in range(4) for h in range(HALVES)}
            for g in range(4):
                for o in range(HALVES):
                    i, bank = k.banks.take(k.pe)
                    t = k.matmuls(bank, [(q["txt"][:, h, o * P:(o + 1) * P], qx[:, h, g * BANK:(g + 1) * BANK])
                                         for h in range(HALVES)], t_q, t_x[g, 0], t_x[g, 1])
                    t_fused = A.mark(A.after(t, t_s, t_q).activation(fused[:, o, g * BANK:(g + 1) * BANK], bank, ACT.Identity,
                                                                scale=s_out[:, 4:5], bias=col(k, "b_txt", o)))
                    k.banks.release(i, t_fused)

            for h in range(HALVES):
                t = V.mark(V.after(t_ctx[h], t_zero).tensor_reduce(mcols[0:CP, h:h + 1], wide[0:CP, h, :], AX.X, ALU.max,
                                                           apply_absolute_value=True))
            t = input_scale(0, 0, 2, t)
            t_s = out_scale(0, "d2v", 0, t)

            def quantize_keys(slot, rows, *ready):
                return [[quantize(slot, q8[0:rows, h, c0:c1], wide[0:rows, h, c0:c1], rows, h, *ready)
                         for h in range(HALVES)] for c0, c1 in CH]

            def dense(wname, rows, use, bname, ready, *after):
                n = 0
                for c, (c0, c1) in enumerate(CH):
                    for o in range(HALVES):
                        i, bank = k.banks.take(k.pe)
                        bank = bank[:, 0:c1 - c0]
                        t = k.matmuls(bank, [(q[wname][0:rows, h, o * P:(o + 1) * P], q8[0:rows, h, c0:c1])
                                             for h in range(HALVES)], *ready[c], *after)
                        t = A.mark(A.after(t, *ready[c], *after).activation(
                            wide[:, o, c0:c1], bank, ACT.Identity, scale=s_out[:, use:use + 1], bias=col(k, bname, o),
                            accum_out=avg_parts[:, o, c // 4, c % 4:c % 4 + 1]))
                        k.banks.release(i, t)
                        t = V.mark(V.after(t).tensor_reduce(mcols[:, n:n + 1], wide[:, o, c0:c1], AX.X, ALU.max,
                                                            apply_absolute_value=True))
                        n += 1
                return n, t

            n, t = dense("d2v", CP, 0, "b_d2v", quantize_keys(0, CP, t_s), t_q, t_s)
            t = input_scale(1, 0, n, t)
            t_s = out_scale(1, "img", 1, t)
            n, t = dense("img", P, 1, "b_img", quantize_keys(1, P, t_s, k.pe.last()), t_s)
            t = input_scale(2, 0, n, t)
            out_scale(2, "att0", 2, t)
            t_s = out_scale(2, "att1", 3, t)
            t_q8 = quantize_keys(2, P, t_s, k.pe.last())
            t = V.mark(V.after(A.last()).tensor_reduce(avg[:].rearrange("p (h b) -> p h b", b=B), avg_parts[:], AX.X, ALU.add))
            t_avg = V.mark(V.after(t).tensor_scalar(avg[:], avg[:], 1.0 / S2, None, ALU.mult))

            keys = big[:, 0:KEYS]
            values = big[:, KEYS:KEYS + B * KT * P].rearrange("p (b t d) -> p b t d", b=B, t=KT)
            qsum = k.sb(ctx, "query_sum", [P, NTOK])
            o_tok = Ring([k.sb(ctx, "o_tok%d" % n, [P, P]) for n in range(2)])
            for layer in range(2):
                wq, sc = q["att%d" % layer], s_out[:, 2 + layer:3 + layer]
                bcol, brow = col(k, "b_att%d" % layer), row(k, "b_att%d" % layer)
                t_keys = []
                for c, (c0, c1) in enumerate(CH):
                    i, bank = k.banks.take(k.pe)
                    t = k.matmuls(bank[:, 0:c1 - c0], [(wq[:, h, :], q8[:, h, c0:c1]) for h in range(HALVES)], *t_q8[c])
                    t = A.mark(A.after(t, *t_q8[c]).activation(keys[:, c0:c1], bank[:, 0:c1 - c0], ACT.Identity, scale=sc, bias=bcol))
                    k.banks.release(i, t)
                    t_keys.append(t)
                for b in range(B):
                    for g in range(0, KT, 4):
                        i, bank = k.banks.take(k.pe)
                        tiles = range(g, min(g + 4, KT))
                        for kt in tiles:
                            rows = P if kt < KT - 1 else KLAST
                            a = b * S2 + kt * P
                            for h in range(HALVES):
                                ins = nc.tensor.matmul(bank[0:rows, (kt - g) * P:(kt - g + 1) * P], q8[:, h, a:a + rows],
                                                       wq[:, h, :], start=(h == 0), stop=(h == 1))
                        t = k.pe.mark(ins)
                        rows, cnt = (P, 4) if len(tiles) == 4 else (KLAST, 1)
                        t_val = V.mark(V.after(t, t_avg, *t_q8[-1]).scalar_tensor_tensor(
                            values[0:rows, b, g:g + cnt, :], bank[0:rows, 0:cnt * P].rearrange("p (a d) -> p a d", d=P),
                            sc[0:rows], brow[0:rows].unsqueeze(1).to_broadcast([rows, cnt, P]), ALU.mult, ALU.add))
                        k.banks.release(i, t_val)
                t_qs = V.mark(V.after(V.last(), t_fused).tensor_tensor(qsum[:], fused[:, 0, :], fused[:, 1, :], ALU.add))
                items = []

                def item(b, qt):
                    tile = b * TPB + qt
                    cols_q = slice(tile * P, (tile + 1) * P)

                    def finish(obank, io, rsum, after):
                        jo, o = o_tok.take(V)
                        t_o = V.mark(V.after(*after).tensor_scalar(o[:], obank[:, 0:P], rsum, None, ALU.mult))
                        k.banks.release(io, t_o)

                        def add():
                            i, bank = k.banks.take(k.pe)
                            t = k.pe.mark(k.pe.after(t_o).transpose(bank[:, 0:P], o[:], const(k, "ident")))
                            o_tok.release(jo, t)
                            t = V.mark(V.after(t, t_qs).scalar_tensor_tensor(
                                fused[:, :, cols_q], bank[:, 0:P].unsqueeze(1).to_broadcast([P, 2, P]), 0.1,
                                fused[:, :, cols_q], ALU.mult, ALU.add))
                            k.banks.release(i, t)
                        return add

                    return {"query": [qsum[:, cols_q]], "keys": lambda c0, c1: [keys[:, b * S2 + c0:b * S2 + c1]],
                            "value": lambda kt, rows: values[0:rows, b, kt, :], "finish": finish,
                            "ready": (t_qs, t_keys[-1], t_val)}

                items = [item(b, qt) for b in range(B) for qt in range(TPB)]
                if layer:
                    space = q8[:].rearrange("p h s -> p (h s)")[:, 0:2 * (4 * FF + 8 * D)].bitcast(F32)
                    raw = {"f1": space[:, 0:4 * FF].rearrange("p (c o) -> p c o", o=FF),
                           "f2": space[:, 4 * FF:4 * FF + 8 * D].rearrange("p (c o) -> p c o", o=D)}
                    last_weights = ternary(["f1", "f2"], raw, [(P, 4, FF), (P, 8, D)],
                                           qx[:].rearrange("p h t -> p (h t)"), k.pe.last())
                    next(last_weights)
                    for n in range(3, 15, 2):
                        items[n]["also"] = lambda: next(last_weights)
                with ExitStack() as actx:
                    attention(k, actx, "bn%d" % layer, items, 1.0 / 16.0, P)
                    k.barrier()

        with ExitStack() as ctx:
            qf = k.sb(ctx, "fused_q8", [P, HALVES, NTOK], BF16)
            qavg = k.sb(ctx, "avg_q8", [P, HALVES * B], BF16)
            hid = k.sb(ctx, "hidden", [P, 8, NTOK])
            qh = k.sb(ctx, "hidden_q8", [P, 8, NTOK], BF16)
            hbias = k.sb(ctx, "hidden_bias", [P, 8, B])
            t = V.mark(nc.vector.tensor_reduce(mcols[:, 0:1], fused[:], AX.XY, ALU.max, apply_absolute_value=True))
            t = V.mark(nc.vector.tensor_reduce(mcols[:, 1:2], avg[:], AX.X, ALU.max, apply_absolute_value=True))
            t = input_scale(4, 0, 2, t)
            t_s = out_scale(4, "f1", 5, t)
            t_a = quantize(4, qavg[:], avg[:], P, 0, t_s)
            t_f = [[quantize(4, qf[:, h, b * T:(b + 1) * T], fused[:, h, b * T:(b + 1) * T], P, h, t_s)
                    for h in range(HALVES)] for b in range(B)]
            i, bank = k.banks.take(k.pe)
            k.pe.after(t_a)
            for ft in range(8):
                for h in range(HALVES):
                    ins = nc.tensor.matmul(bank[:, ft * B:(ft + 1) * B], q["f1"][:, 2 + h, ft * P:(ft + 1) * P],
                                           qavg[:, h * B:(h + 1) * B], start=(h == 0), stop=(h == 1))
            t = k.pe.mark(ins)
            o, _ = COL_AT["b_f1"]
            t_hb = V.mark(V.after(t).scalar_tensor_tensor(
                hbias[:], bank[:, 0:8 * B].rearrange("p (f b) -> p f b", b=B), s_out[:, 5:6],
                k.cols[:, o:o + 8].unsqueeze(2).to_broadcast([P, 8, B]), ALU.mult, ALU.add))
            k.banks.release(i, t_hb)
            n = 0
            for b in range(B):
                for ft in range(8):
                    i, bank = k.banks.take(k.pe)
                    cs = slice(b * T, (b + 1) * T)
                    t = k.matmuls(bank, [(q["f1"][:, h, ft * P:(ft + 1) * P], qf[:, h, cs]) for h in range(HALVES)], *t_f[b])
                    t = A.mark(A.after(t, t_hb).activation(hid[:, ft, cs], bank, ACT.Relu, scale=s_out[:, 5:6],
                                                           bias=hbias[:, ft, b:b + 1]))
                    k.banks.release(i, t)
                    t = V.mark(V.after(t).tensor_reduce(mcols[:, n:n + 1], hid[:, ft, cs], AX.X, ALU.max))
                    n += 1
            t_xb = k.pool.mark(k.pool.after(k.t_param).tensor_tensor(
                k.x_tok[:], k.x_tok[:], row(k, "b_f2").unsqueeze(1).to_broadcast([P, TILES, D]), ALU.add))
            t = input_scale(5, 0, n, t)
            t_s = out_scale(5, "f2", 6, t)
            t_h = [[quantize(5, qh[:, f:f + 4, b * T:(b + 1) * T], hid[:, f:f + 4, b * T:(b + 1) * T], P, f, t_s)
                    for f in (0, 4)] for b in range(B)]
            ready = {}
            for tile in range(TILES):
                i, bank = k.banks.take(k.pe)
                t = k.matmuls(bank[:, 0:D], [(qh[:, ft, tile * P:(tile + 1) * P], q["f2"][:, ft, :]) for ft in range(8)],
                              *t_h[tile // TPB])
                ready[tile] = V.mark(V.after(t, t_xb).scalar_tensor_tensor(
                    k.x_tok[:, tile, :], bank[:, 0:D], s_out[:, 6:7], k.x_tok[:, tile, :], ALU.mult, ALU.add))
                k.banks.release(i, ready[tile])
                if tile % 4 == 3:
                    norm_group(k, ready, tile // 4)
                    if tile > 4:
                        channels_group(k, tile // 4 - 1)
            channels_group(k, B - 1)
            k.barrier()


def experts(k):
    nc, V, A, G = k.nc, k.dve, k.act, k.pool
    with ExitStack() as ctx:
        sb = lambda name, shape, dt=F32: k.sb(ctx, name, shape, dt)
        raw1, raw2 = Ring([sb("moe_w1_f32", [P, HALVES, FF])]), Ring([sb("moe_w2_f32", [P, 8, D])])
        w1s = Ring([sb("moe_w1_%d" % n, [P, 2, HALVES, FF], BF16) for n in range(2)])
        w2s = Ring([sb("moe_w2_%d" % n, [P, 2, 8, D], BF16) for n in range(2)])
        wg, b2 = sb("moe_wg", [P, HALVES, NE]), sb("moe_b2", [NE, D])
        t_g = k.load("moe_g", (wg[:], k.dram["moe_wg"].rearrange("(h p) e -> p h e", p=P)), (b2[:], k.dram["moe_b2"]))
        xhat_tok, xhat = sb("xhat_tok", [P, TILES, D]), sb("xhat", [P, HALVES, NTOK])
        normed_f32 = xhat_tok[:].rearrange("p t d -> p (t d)").rearrange("p (h n) -> p h n", h=HALVES)
        normed = Ring([sb("normed%d" % n, [P, 2, HALVES, NTOK], BF16) for n in range(2)])
        hidden = Ring([sb("moe_h%d" % n, [P, 2, 8, BANK], BF16) for n in range(2)])
        acts = Ring([sb("moe_act%d" % n, [P, BANK]) for n in range(3)])
        sc = sb("gate_scores", [P, TILES, NE])
        gate, top = sb("gate_w", [P, TILES, NE]), sb("gate_top", [P, TILES])
        gsum = sb("gate_sum", [P, TILES])

        def load_expert(e):
            i1, w1 = raw1.take(k.sp)
            i2, w2 = raw2.take(k.sp)
            t = k.load("moe%d" % e, (w1[:], k.dram["moe_w1"][e].rearrange("(h p) f -> p h f", p=P)),
                       (w2[:], k.dram["moe_w2"][e].rearrange("(f p) d -> p f d", p=P)))
            return i1, w1, i2, w2, t

        def split(high, low, src, *ready):
            t = A.mark(A.after(*ready).copy(high, src))
            return (G.mark(G.after(t).tensor_tensor(low, src, high, ALU.subtract)),)

        def split_expert(e, part):
            j1, r1, j2, r2, t = loaded[e]
            if part == 0:
                own = weights[e] = {}
                for name, ring in (("w1", w1s), ("w2", w2s)):
                    own["j" + name], own[name] = j, w = ring.take(A)
                    G.after(*ring.readers[j])
                own["t"] = []
            own = weights[e]
            if part < 2:
                own["t"] += split(own["w1"][:, 0, part, :], own["w1"][:, 1, part, :], r1[:, part, :], t)
            else:
                f = slice(4 * part - 8, 4 * part - 4)
                own["t"] += split(own["w2"][:, 0, f, :], own["w2"][:, 1, f, :], r2[:, f, :], t)
            if part == 3:
                raw1.release(j1, V.last(), G.last(), A.last())
                raw2.release(j2, V.last(), G.last(), A.last())
                if e + 1 < NE:
                    loaded.append(load_expert(e + 1))

        def make_normed(e, g, *ready):
            if g == 0:
                j, nm = normed.take(A)
                G.after(*normed.readers[j])
                inputs[e] = (j, nm, {})
            _, nm, tokens = inputs[e]
            cg = slice(g * BANK, (g + 1) * BANK)
            A.after(*ready)
            for h in range(HALVES):
                t = A.mark(nc.scalar.activation(normed_f32[:, h, cg], xhat[:, h, cg], ACT.Identity,
                                                scale=col(k, "moe_gamma", 2 * e + h), bias=col(k, "moe_beta", 2 * e + h)))
            tokens[g] = split(nm[:, 0, :, cg], nm[:, 1, :, cg], normed_f32[:, :, cg], t)
            return tokens[g]

        loaded, weights, inputs = [load_expert(0)], {}, {}

        t_hat = layer_norm(k, k.x_tok, xhat_tok, k.tok, 1)
        i, bank = k.banks.take(k.pe)
        k.pe.after(t_g, *[t for g in range(4) for t in k.ch[g]])
        for tile in range(TILES):
            for h in range(HALVES):
                ins = nc.tensor.matmul(bank[:, tile * NE:(tile + 1) * NE], k.x_ch[:, h, tile * P:(tile + 1) * P],
                                       wg[:, h, :], start=(h == 0), stop=(h == 1))
        t = k.pe.mark(ins)
        t_hc = to_channels(k, xhat_tok, xhat, t_hat)
        for part in range(4):
            split_expert(0, part)
        for g in range(4):
            make_normed(0, g, *[t for h in t_hc.values() for t in h])
        t = V.mark(V.after(t).tensor_copy(sc[:], bank[:, 0:TILES * NE].rearrange("p (t e) -> p t e", e=NE)))
        k.banks.release(i, t)
        V.after(t)
        shape = [P, TILES, NE, NE]
        jc, space = hidden.take(V)
        n = TILES * NE * NE
        cmp1, cmp2 = (space[:, x].rearrange("p f t -> p (f t)").bitcast(F32)[:, 0:n].rearrange("p (t a b) -> p t a b", a=NE, b=NE)
                      for x in range(2))
        mine = sc[:].unsqueeze(3).to_broadcast(shape)
        other = sc[:].unsqueeze(2).to_broadcast(shape)
        flat = lambda a: a.rearrange("p t a b -> p t (a b)")
        V.mark(nc.vector.tensor_tensor(cmp1, other, mine, ALU.is_gt))
        t = V.mark(nc.vector.tensor_tensor(cmp2, other, mine, ALU.is_equal))
        V.mark(nc.vector.tensor_reduce(top[:], sc[:], AX.X, ALU.max))
        t = V.mark(V.after(t).tensor_tensor(flat(cmp2), flat(cmp2), const(k, "lower").unsqueeze(1).to_broadcast([P, TILES, 64]), ALU.mult))
        t = V.mark(V.after(t).tensor_tensor(flat(cmp1), flat(cmp1), flat(cmp2), ALU.add))
        t = V.mark(V.after(t).tensor_reduce(gate[:], cmp1, AX.X, ALU.add))
        t1 = V.mark(V.after(t).tensor_scalar(gate[:], gate[:], 1.5, None, ALU.is_lt))
        t = V.mark(nc.vector.tensor_tensor(sc[:], sc[:], top[:].unsqueeze(2).to_broadcast([P, TILES, NE]), ALU.subtract))
        t = A.mark(A.after(t).activation(sc[:], sc[:], ACT.Exp))
        t = V.mark(V.after(t, t1).tensor_tensor(gate[:], gate[:], sc[:], ALU.mult))
        t = V.mark(V.after(t).tensor_reduce(gsum[:], gate[:], AX.X, ALU.add))
        t = V.mark(V.after(t).reciprocal(top[:], gsum[:]))
        t_gate = V.mark(V.after(t).tensor_tensor(gate[:], gate[:], top[:].unsqueeze(2).to_broadcast([P, TILES, NE]), ALU.mult))
        t = V.mark(V.after(t_gate).tensor_reduce(gsum[:], gate[:], AX.X, ALU.add))
        hidden.release(jc, t_gate)
        t_gsum = V.mark(V.after(t).tensor_scalar(gsum[:], gsum[:], 1.0, None, ALU.add))

        ready = {}

        def residual():
            for tile in range(TILES):
                m = tile % 4
                if m == 0:
                    i, bank = k.banks.take(k.pe)
                    k.pe.after(t_gate)
                    for n in range(4):
                        ins = nc.tensor.transpose(bank[0:NE, n * P:(n + 1) * P], gate[:, tile + n, :], const(k, "ident"))
                    t = k.pe.mark(ins)
                    ja, gates = acts.take(A)
                    t_gc = A.mark(A.after(t).copy(gates[0:NE, :], bank[0:NE, :]))
                    k.banks.release(i, t_gc)
                i, bank = k.banks.take(k.pe)
                t = k.matmuls(bank[:, 0:D], [(gates[0:NE, m * P:(m + 1) * P], b2[:])], t_gc, t_g)
                if m == 3:
                    acts.release(ja, t)
                ready[tile] = V.mark(V.after(t, t_gsum, t_hat[tile]).scalar_tensor_tensor(
                    k.x_tok[:, tile, :], k.x_tok[:, tile, :], gsum[:, tile:tile + 1], bank[:, 0:D], ALU.mult, ALU.add))
                k.banks.release(i, ready[tile])

        def second(e, g, ih, h, t_h):
            w2, t_w = weights[e]["w2"], weights[e]["t"]
            for pair in range(2):
                i, bank = k.banks.take(k.pe)
                k.pe.after(*t_w, *t_h)
                for s in range(2):
                    m = 2 * pair + s
                    t = k.matmuls(bank[:, s * D:(s + 1) * D], [(h[:, x, ft, m * P:(m + 1) * P], w2[:, y, ft, :])
                                                               for ft in range(8) for x, y in PASSES])
                for s in range(2):
                    tile = 4 * g + 2 * pair + s
                    ready[tile] = t = V.mark(V.after(t, ready[tile]).scalar_tensor_tensor(
                        k.x_tok[:, tile, :], bank[:, s * D:(s + 1) * D], gate[:, tile, e:e + 1], k.x_tok[:, tile, :],
                        ALU.mult, ALU.add))
                k.banks.release(i, t)
            hidden.release(ih, k.pe.last())
            if g == 3:
                w1s.release(weights[e]["jw1"], k.pe.last())
                w2s.release(weights[e]["jw2"], k.pe.last())

        pending = None
        for e in range(NE):
            w1, t_w = weights[e]["w1"], weights[e]["t"]
            inn, nm, t_n = inputs[e]
            for g in range(4):
                ih, hd = hidden.take(A)
                G.after(*hidden.readers[ih])
                t_h = []
                for ft in range(8):
                    i, bank = k.banks.take(k.pe)
                    cf = slice(ft * P, (ft + 1) * P)
                    cg = slice(g * BANK, (g + 1) * BANK)
                    t = k.matmuls(bank, [(w1[:, y, h, cf], nm[:, x, h, cg]) for h in range(HALVES) for x, y in PASSES],
                                  *t_w, *t_n[g])
                    ja, act = acts.take(V)
                    t = V.mark(V.after(t).tensor_scalar(act[:], bank, col(k, "moe_b1", 8 * e + ft), 0.0, ALU.add, ALU.max))
                    k.banks.release(i, t)
                    t, = split(hd[:, 0, ft, :], hd[:, 1, ft, :], act[:], t)
                    acts.release(ja, t)
                    t_h.append(t)
                if not ready:
                    residual()
                if pending:
                    second(*pending)
                if e == NE - 1 and g:
                    norm_group(k, ready, g - 1)
                    if g > 1:
                        channels_group(k, g - 2)
                if e + 1 < NE:
                    split_expert(e + 1, g)
                    make_normed(e + 1, g, *t_n[g])
                pending = (e, g, ih, hd, t_h[-2:])
            normed.release(inn, k.pe.last())
        second(*pending)
        channels_group(k, B - 2)
        norm_group(k, ready, B - 1)
        channels_group(k, B - 1)
        k.barrier()


def linear_attention(k):
    nc, V, A = k.nc, k.dve, k.act
    CV = P + 8
    with ExitStack() as ctx:
        sb = lambda name, shape, dt=F32: k.sb(ctx, name, shape, dt)
        two = lambda name, shape: Ring([sb("%s%d" % (name, n), shape) for n in range(2)])
        wqkv, wproj = sb("la_wqkv", [P, HALVES, 3 * D]), sb("la_wproj", [P, HALVES, D])
        t_w = k.load("la_w", (wqkv[:], k.dram["la_qkvT"].rearrange("(h p) o -> p h o", p=P)),
                     (wproj[:], k.dram["la_projT"].rearrange("(h p) o -> p h o", p=P)))
        q_ch = two("la_q", [P, HALVES, T])
        scratch = two("la_min", [P, BANK])
        kv_tok = two("la_kv", [P, 2 * D])
        k_phi = two("la_k", [P, TPB, D])
        v_aug = [sb("la_v%d" % n, [P, TPB, HALVES, P + 1]) for n in range(2)]
        kvd = two("la_kvd", [P, HALVES, CV])
        den = two("la_den", [P, H0])
        o_tok, o_ch = two("la_o", [P, TPB, D]), two("la_oc", [P, HALVES, T])
        a_tok = sb("la_out", [P, TILES, D])
        regrouped = Ring([sb("la_rg%d" % n, [P, HALVES, T]) for n in range(B)])
        regroup_of, last_reads = {}, {}
        for n in range(2):
            V.mark(nc.vector.memset(v_aug[n][:, :, :, P:P + 1], 1.0))
        v_aug = Ring(v_aug)
        done, ready, closing = {}, {}, {}
        over = lambda name: row(k, name).unsqueeze(1).to_broadcast([P, TPB, D])
        G = k.pool

        def attend(b):
            cs = slice(b * T, (b + 1) * T)
            jq, qc = q_ch.take(A)
            for c in range(HALVES):
                i, bank = k.banks.take(k.pe)
                t = k.matmuls(bank, [(wqkv[:, h, c * P:(c + 1) * P], k.x_ch[:, h, cs]) for h in range(HALVES)],
                              t_w, *k.ch[b])
                js, mn = scratch.take(V)
                t1 = V.mark(V.after(t).tensor_scalar(mn[:], bank, col(k, "la_bq", c), 0.0, ALU.add, ALU.min))
                A.after(t1)
                t2 = A.mark(nc.scalar.activation(qc[:, c, :], bank, ACT.Relu, bias=col(k, "la_bq", c)))
                k.banks.release(i, t2)
                t = A.mark(nc.scalar.activation(mn[:], mn[:], ACT.Exp))
                t_q = V.mark(V.after(t).tensor_tensor(qc[:, c, :], qc[:, c, :], mn[:], ALU.add))
                scratch.release(js, t_q)
            jk, kp = k_phi.take(V)
            jv, va = v_aug.take(A)
            for n in range(TPB):
                i, bank = k.banks.take(k.pe)
                tile = slice((b * TPB + n) * P, (b * TPB + n + 1) * P)
                t = k.matmuls(bank, [(k.x_ch[:, h, tile], wqkv[:, h, D:3 * D]) for h in range(HALVES)], *k.ch[b])
                jt, kv = kv_tok.take(V)
                t = V.mark(V.after(t).tensor_tensor(kv[:], bank, row(k, "la_bkv"), ALU.add))
                k.banks.release(i, t)
                t_v = A.mark(A.after(t).copy(va[:, n, :, 0:P], kv[:, D:2 * D].rearrange("p (h c) -> p h c", c=P)))
                js, mn = scratch.take(V)
                t = V.mark(V.after(t).tensor_scalar(mn[:, 0:D], kv[:, 0:D], 0.0, None, ALU.min))
                t = A.mark(A.after(t).activation(mn[:, 0:D], mn[:, 0:D], ACT.Exp))
                t_k = V.mark(V.after(t).scalar_tensor_tensor(kp[:, n, :], kv[:, 0:D], 0.0, mn[:, 0:D], ALU.max, ALU.add))
                scratch.release(js, t_k)
                kv_tok.release(jt, t_k, t_v)
            last_reads[b] = (k.pe.last(),)
            yield
            i, bank = k.banks.take(k.pe)
            k.pe.after(t_k, t_v)
            for n in range(TPB):
                for h in range(HALVES):
                    ins = nc.tensor.matmul(bank[:, h * (P + 1):(h + 1) * (P + 1)], kp[:, n, h * P:(h + 1) * P],
                                           va[:, n, h, :], start=(n == 0 and h == 0), stop=(n == TPB - 1),
                                           skip_group_check=True)
            t = k.pe.mark(ins)
            k_phi.release(jk, t)
            v_aug.release(jv, t)
            jd, kd = kvd.take(V)
            V.after(t)
            for h in range(HALVES):
                o = h * (P + 1)
                V.mark(nc.vector.tensor_tensor(kd[:, h, 0:P], bank[:, o:o + P], const(k, "diag16"), ALU.mult))
                t_kd = V.mark(nc.vector.tensor_scalar(kd[:, h, P:CV], const(k, "head16"), bank[:, o + P:o + P + 1],
                                                      None, ALU.mult))
            k.banks.release(i, t_kd)
            yield
            jo, ot = o_tok.take(V)
            for n in range(TPB):
                i, bank = k.banks.take(k.pe)
                k.pe.after(t_kd, t_q)
                for h in range(HALVES):
                    ins = nc.tensor.matmul(bank[:, h * CV:(h + 1) * CV], qc[:, h, n * P:(n + 1) * P], kd[:, h, :],
                                           start=True, stop=True)
                t = k.pe.mark(ins)
                view = bank[:, 0:2 * CV].rearrange("p (h c) -> p h c", c=CV)
                jn, dn = den.take(V)
                dv = dn[:].rearrange("p (h a) -> p h a", h=2)
                t = V.mark(V.after(t).tensor_scalar(dv, view[:, :, P:CV], 1e-6, None, ALU.max))
                t = V.mark(V.after(t).reciprocal(dn[:], dn[:]))
                V.after(t)
                for h in range(HALVES):
                    t_o = V.mark(nc.vector.tensor_tensor(
                        ot[:, n, h * P:(h + 1) * P].rearrange("p (a c) -> p a c", c=N0),
                        view[:, h, 0:P].rearrange("p (a c) -> p a c", c=N0),
                        dn[:, 8 * h:8 * h + 8].unsqueeze(2).to_broadcast([P, 8, N0]), ALU.mult))
                den.release(jn, t_o)
                k.banks.release(i, t_o)
            kvd.release(jd, k.pe.last())
            q_ch.release(jq, k.pe.last())
            yield
            jc, oc = o_ch.take(A)
            for h in range(HALVES):
                i, bank = k.banks.take(k.pe)
                k.pe.after(t_o)
                for n in range(TPB):
                    ins = nc.tensor.transpose(bank[:, n * P:(n + 1) * P], ot[:, n, h * P:(h + 1) * P], const(k, "ident"))
                t = k.pe.mark(ins)
                t_oc = A.mark(A.after(t).copy(oc[:, h, :].rearrange("p (s m) -> p s m", s=N0),
                                              bank.rearrange("p (m s) -> p s m", s=N0)))
                k.banks.release(i, t_oc)
            o_tok.release(jo, k.pe.last())
            sem = k.sem("regrouped%d" % b)
            k.sp.after(t_oc)
            for hd in range(H0):
                nc.sync.dma_start(k.dram["regroup"][b, :, :, hd, :].rearrange("s v m -> v s m"),
                                  oc[(hd % 8) * N0:(hd % 8 + 1) * N0, hd // 8, :].rearrange("v (s m) -> v s m", s=N0)
                                  ).then_inc(sem, 16)
            t_out = (sem, 16 * H0)
            o_ch.release(jc, t_out)
            jr, rg = regrouped.take(k.sp)
            t_rg = k.load("regrouped%d" % b, (rg[:], k.dram["regroup"][b].rearrange("(g s) v h m -> (s v) g (h m)", g=2)),
                          after=(t_out,))
            regroup_of[b] = (jr, rg, t_rg)
            yield

        def project(b):
            jr, rg, t_rg = regroup_of[b]
            for n in range(TPB):
                i, bank = k.banks.take(k.pe)
                tile = b * TPB + n
                t = k.matmuls(bank[:, 0:D], [(rg[:, h, n * P:(n + 1) * P], wproj[:, h, :]) for h in range(HALVES)], t_rg)
                done[tile] = V.mark(V.after(t).tensor_tensor(a_tok[:, tile, :], bank[:, 0:D], row(k, "la_bproj"), ALU.add))
                k.banks.release(i, done[tile])
            done.update(layer_norm(k, a_tok, a_tok, done, 0, range(b * TPB, (b + 1) * TPB)))
            a = a_tok[:, b * TPB:(b + 1) * TPB, :]
            t = V.mark(V.after(*[done[b * TPB + n] for n in range(TPB)]).tensor_tensor(a, a, over("la_gamma"), ALU.mult))
            closing[b] = G.mark(G.after(t).tensor_tensor(a, a, over("la_beta"), ALU.add))

        def close(b):
            xs = k.x_tok[:, b * TPB:(b + 1) * TPB, :]
            t = V.mark(V.after(closing[b], *[k.tok[b * TPB + n] for n in range(TPB)]).scalar_tensor_tensor(
                xs, xs, 2.0, a_tok[:, b * TPB:(b + 1) * TPB, :], ALU.mult, ALU.add))
            ready.update({b * TPB + n: t for n in range(TPB)})
            norm_group(k, ready, b)

        parts = [attend(b) for b in range(B)]
        next(parts[0])
        for b in range(B):
            if b + 1 < B:
                next(parts[b + 1])
            next(parts[b])
            next(parts[b])
            if b:
                project(b - 1)
            next(parts[b])
            if b > 2:
                channels_group(k, b - 3, *last_reads[b - 3])
            if b > 1:
                close(b - 2)
        channels_group(k, B - 3, *last_reads[B - 3])
        close(B - 2)
        project(B - 1)
        close(B - 1)
        channels_group(k, B - 2, *last_reads[B - 2])
        channels_group(k, B - 1, *last_reads[B - 1])
        k.barrier()


SPLIT = 3 * NX
ROWS_X = SPLIT + 3


def cross_attention(k):
    nc, V, A, G = k.nc, k.dve, k.act, k.pool
    scale = 1.0 / float(np.sqrt(np.float32(NX)))
    HU = HX // 2
    KTP = (KT + 1) // 2
    VC = NX + 1
    with ExitStack() as ctx:
        sb = lambda name, shape, dt=F32: k.sb(ctx, name, shape, dt)
        ring = lambda name, n, shape, dt=F32: Ring([sb("%s%d" % (name, i), shape, dt) for i in range(n)])
        wq, wo = sb("xa_wq", [P, HALVES, D]), sb("xa_wo", [P, HALVES, D])
        wk, wv = sb("xa_wk", [CP, HALVES, D]), sb("xa_wv", [CP, HALVES, D])
        t_w = k.load("xa_w", *[(w[:], k.dram["xa_" + n].rearrange("(h p) o -> p h o", h=2))
                               for n, w in (("q", wq), ("o", wo), ("k", wk), ("v", wv))])
        contexts = ring("xa_ctx", 1, [CP, HALVES, S2])
        keys_hl = ring("xa_keys_hl", 1, [P, 2, HALVES, S2], BF16)
        query_hl = ring("xa_query_hl", 1, [P, 2, HALVES, T], BF16)
        key_rows = [sb("xa_key_rows%d" % n, [ROWS_X, HU, S2], BF16) for n in range(2)]
        query_rows = ring("xa_query_rows", 2, [ROWS_X, HU, T], BF16)
        value_f32 = ring("xa_value_f32", 2, [P, 2, D])
        values = [sb("xa_values%d" % n, [P, KT, HX, 2 * VC], BF16) for n in range(2)]
        maxes, nmax = ring("xa_max", 2, [P, HU * TPB, 2]), ring("xa_nmax", 2, [P, HU * TPB])
        rest = ring("xa_rest", 2, [P, HU * TPB])
        parts = ring("xa_parts", 2, [P, TPB, 3, HU], BF16)
        parts_t = ring("xa_parts_t", 2, [3 * HU, T], BF16)
        ident_b = sb("xa_ident_b", [P, P], BF16)
        exps = ring("xa_exp", 4, [P, 2, T])
        highs, lows = ring("xa_high", 5, [P, 2, T], BF16), ring("xa_low", 5, [P, 2, T], BF16)
        o_rows = ring("xa_o_rows", 2, [2 * VC, T])
        rsum = ring("xa_rsum", 2, [P, TPB])
        o_tok, o_ch = ring("xa_o", 2, [P, TPB, D]), ring("xa_oc", 1, [P, HALVES, T])
        fold = sb("xa_fold", [2 * VC, VC])
        pairs = Ring([k.psum[:, 2 * n:2 * n + 2, :].rearrange("p b c -> p (b c)") for n in range(3)])
        banks = Ring([k.psum[:, n, :] for n in (6, 7)])

        t = V.mark(V.after(k.t_param).tensor_copy(ident_b[:], const(k, "ident")))
        t_fold = V.mark(nc.vector.tensor_copy(fold[:], const(k, "fold", 2 * VC)))
        for n in range(2):
            V.mark(nc.vector.memset(key_rows[n][SPLIT:ROWS_X], 1.0))
            V.mark(nc.vector.memset(values[n][:, :, :, NX:VC], 1.0))
            t_ones = V.mark(nc.vector.memset(values[n][:, :, :, 2 * VC - 1:2 * VC], 0.0))
        key_rows, values = Ring(key_rows), Ring(values)
        t_bias = G.mark(G.after(k.t_param, *[k.tok[i] for i in range(TILES)]).tensor_tensor(
            k.x_tok[:], k.x_tok[:], row(k, "xa_bo").unsqueeze(1).to_broadcast([P, TILES, D]), ALU.add))

        batch, unit, ready = {}, {}, {}

        def split(high, low, bank, bias, t):
            t = A.mark(A.after(t).activation(high, bank, ACT.Identity, bias=bias))
            return V.mark(V.after(t).scalar_tensor_tensor(low, bank, bias, high, ALU.add, ALU.subtract))

        def prepare_batch(b):
            s = batch[b] = {}

            def load():
                jc, s["ctx"] = contexts.take(k.sp)
                s["jc"] = jc
                s["t_ctx"] = k.load("xa_ctx%d" % b, (s["ctx"][:], k.dram["ctxT"][:, b, :].rearrange("(h p) s -> p h s", h=2)))
                s["jq"], s["q"] = query_hl.take(A)
                V.after(*query_hl.readers[s["jq"]])
                s["jk"], s["k"] = keys_hl.take(A)
                V.after(*keys_hl.readers[s["jk"]])

            def queries(c):
                i, bank = pairs.take(k.pe)
                bank = bank[:, 0:T]
                t = k.matmuls(bank, [(wq[:, h, c * P:(c + 1) * P], k.x_ch[:, h, b * T:(b + 1) * T]) for h in range(HALVES)],
                              t_w, *k.ch[b])
                s["t_read"] = t
                s["t_q"] = split(s["q"][:, 0, c, :], s["q"][:, 1, c, :], bank, col(k, "xa_bq", c), t)
                pairs.release(i, s["t_q"])

            def keys(o, c0):
                c1 = min(c0 + 2 * BANK, S2)
                i, bank = pairs.take(k.pe)
                for a in range(c0, c1, BANK):
                    e = min(a + BANK, c1)
                    t = k.matmuls(bank[:, a - c0:e - c0], [(wk[:, h, o * P:(o + 1) * P], s["ctx"][:, h, a:e])
                                                           for h in range(HALVES)], s["t_ctx"], t_w)
                s["t_k"] = split(s["k"][:, 0, o, c0:c1], s["k"][:, 1, o, c0:c1], bank[:, 0:c1 - c0], col(k, "xa_bk", o), t)
                pairs.release(i, s["t_k"])

            def value(kt0):
                if kt0 == 0:
                    s["jv"], s["v"] = values.take(G)
                tiles = range(kt0, min(kt0 + 2, KT))
                rows = P if kt0 < KT - 1 else KLAST
                n = len(tiles)
                i, bank = pairs.take(k.pe)
                for kt in tiles:
                    t = k.matmuls(bank[0:rows, (kt - kt0) * D:(kt - kt0 + 1) * D],
                                  [(s["ctx"][:, h, kt * P:kt * P + rows], wv[:, h, :]) for h in range(HALVES)], s["t_ctx"], t_w)
                jf, vf = value_f32.take(V)
                t = V.mark(V.after(t).tensor_tensor(
                    vf[0:rows, 0:n, :], bank[0:rows, 0:n * D].rearrange("p (a d) -> p a d", d=D),
                    row(k, "xa_bv")[0:rows].unsqueeze(1).to_broadcast([rows, n, D]), ALU.add))
                pairs.release(i, t)
                src = vf[0:rows, 0:n, :].rearrange("p a (h c) -> p (a h) c", c=NX)
                dst = s["v"][0:rows, kt0:kt0 + n, :, :].rearrange("p a h c -> p (a h) c")
                t = G.mark(G.after(t, t_ones).tensor_copy(dst[:, :, 0:NX], src))
                s["t_v"] = G.mark(G.after(t).tensor_tensor(dst[:, :, VC:VC + NX], src, dst[:, :, 0:NX], ALU.subtract))
                value_f32.release(jf, s["t_v"])
                if kt0 + 2 >= KT:
                    contexts.release(s["jc"], k.pe.last())
                    s["jo"], s["o"] = o_tok.take(V)

            return ([load] + [lambda c=c: queries(c) for c in range(HALVES)]
                    + [lambda o=o, c0=c0: keys(o, c0) for o in range(HALVES) for c0 in range(0, S2, 2 * BANK)]
                    + [lambda kt=kt: value(kt) for kt in range(0, KT, 2)])

        def prepare_unit(u):
            b, half = divmod(u, 2)
            s = unit[u] = {}

            def stack():
                p = batch[b]
                s["jk"], kr = key_rows.take(k.sp)
                s["jq"], qr = query_rows.take(k.sp)
                moves = []
                for a in range(HU):
                    lanes = slice(a * NX, (a + 1) * NX)
                    for j, (qp, kp) in enumerate(((0, 0), (1, 0), (0, 1))):
                        rows = slice(j * NX, (j + 1) * NX)
                        moves.append((kr[rows, a, :], p["k"][lanes, kp, half, :]))
                        moves.append((qr[rows, a, :], p["q"][lanes, qp, half, :]))
                s["t_rows"] = k.load("xa_rows%d" % u, *moves, after=(p["t_k"], p["t_q"]))
                s["k"], s["q"] = kr, qr
                if half:
                    keys_hl.release(p["jk"], s["t_rows"], unit[u - 1]["t_rows"])
                    query_hl.release(p["jq"], s["t_rows"], unit[u - 1]["t_rows"])
                s["jm"], s["max"] = maxes.take(V)

            def maximum(a, qt, part):
                c0, c1 = ((0, 2 * BANK), (2 * BANK, S2))[part]
                i, bank = pairs.take(k.pe)
                k.pe.after(s["t_rows"])
                for x in range(c0, c1, BANK):
                    y = min(x + BANK, c1)
                    ins = nc.tensor.matmul(bank[:, x - c0:y - c0], s["q"][0:SPLIT, a, qt * P:(qt + 1) * P],
                                           s["k"][0:SPLIT, a, x:y], start=True, stop=True)
                t = k.pe.mark(ins)
                s["t_max"] = V.mark(V.after(t).tensor_reduce(s["max"][:, qt * HU + a, part:part + 1],
                                                             bank[:, 0:c1 - c0], AX.X, ALU.max))
                pairs.release(i, s["t_max"])

            def subtract_rows():
                jn, nm = nmax.take(V)
                jr, rs = rest.take(V)
                jp, pt = parts.take(V)
                part = lambda n: pt[:, :, n, :]
                grid = lambda a: a[:].rearrange("p (t a) -> p t a", a=HU)
                t = V.mark(V.after(s["t_max"]).tensor_tensor(nm[:], s["max"][:, :, 0], s["max"][:, :, 1], ALU.max))
                maxes.release(s["jm"], t)
                t = V.mark(V.after(t).tensor_scalar(nm[:], nm[:], -1.0, None, ALU.mult))
                t = V.mark(V.after(t).tensor_copy(part(0), grid(nm)))
                t = V.mark(V.after(t).tensor_tensor(grid(rs), grid(nm), part(0), ALU.subtract))
                t = V.mark(V.after(t).tensor_copy(part(1), grid(rs)))
                t = V.mark(V.after(t).tensor_tensor(part(2), grid(rs), part(1), ALU.subtract))
                nmax.release(jn, t)
                rest.release(jr, t)
                i, bank = banks.take(k.pe)
                k.pe.after(t)
                bank_b = bank.bitcast(BF16)
                for qt in range(TPB):
                    ins = nc.tensor.transpose(bank_b[0:3 * HU, qt * P:(qt + 1) * P],
                                              pt[:, qt, :, :].rearrange("p n a -> p (n a)"), ident_b[:])
                t = k.pe.mark(ins)
                parts.release(jp, t)
                jt, tt = parts_t.take(V)
                t = V.mark(V.after(t).tensor_copy(tt[:], bank_b[0:3 * HU, 0:T]))
                banks.release(i, t)
                s["t_rows3"] = k.load("xa_max%d" % u, *[(s["q"][SPLIT + n:SPLIT + n + 1, :, :], tt[n * HU:(n + 1) * HU, :])
                                                        for n in range(3)], after=(t,))
                parts_t.release(jt, s["t_rows3"])

            return ([stack] + [lambda a=a, qt=qt, part=part: maximum(a, qt, part)
                               for a in range(HU) for qt in range(TPB) for part in range(2)] + [subtract_rows])

        def attend(u):
            b, half = divmod(u, 2)
            s, p = unit[u], batch[b]
            steps = []
            fresh, flying = [], []

            def pair(a, kp):
                tiles = range(2 * kp, min(2 * kp + 2, KT))
                rows = P if kp < KTP - 1 else KLAST
                n = len(tiles)
                if kp == 0:
                    s["io"], s["bank"] = banks.take(k.pe)
                i, bank = pairs.take(k.pe)
                k.pe.after(s["t_rows3"])
                for m, kt in enumerate(tiles):
                    ins = nc.tensor.matmul(bank[0:rows, m * T:(m + 1) * T], s["k"][:, a, kt * P:kt * P + rows],
                                           s["q"][:, a, :], start=True, stop=True)
                t = k.pe.mark(ins)
                if a == HU - 1 and kp == KTP - 1:
                    key_rows.release(s["jk"], t)
                    query_rows.release(s["jq"], t)
                je, ex = exps.take(A)
                view = bank[0:rows, 0:n * T].rearrange("p (m q) -> p m q", q=T)
                t = A.mark(A.after(t).activation(ex[0:rows, 0:n, :], view, ACT.Exp, scale=scale))
                pairs.release(i, t)
                fresh.append((a, kp, rows, n, je, ex, t, s["io"], s["bank"]))

            def halve():
                a, kp, rows, n, je, ex, t, io, bank = fresh.pop(0)
                ih, hi = highs.take(A if kp in (1, 3, 4, 6) else V)
                q = A if kp in (1, 3, 4, 6) else V
                q.after(t)
                if q is A:
                    t = q.mark(nc.scalar.copy(hi[0:rows, 0:n, :], ex[0:rows, 0:n, :]))
                else:
                    t = q.mark(nc.vector.tensor_copy(hi[0:rows, 0:n, :], ex[0:rows, 0:n, :]))
                q = V if kp == 3 else G
                il, lo = lows.take(q)
                e = nc.vector if q is V else nc.gpsimd
                q.after(t)
                t_low = q.mark(e.tensor_tensor(lo[0:rows, 0:n, :], ex[0:rows, 0:n, :], hi[0:rows, 0:n, :], ALU.subtract))
                exps.release(je, t_low)
                flying.append((a, kp, ih, hi, il, lo, t, t_low, io, bank))

            def product():
                a, kp, ih, hi, il, lo, t_hi, t_lo, io, bank = flying.pop(0)
                tiles = range(2 * kp, min(2 * kp + 2, KT))
                rows = P if kp < KTP - 1 else KLAST
                k.pe.after(t_hi, t_lo, p["t_v"])
                hd = half * HU + a
                for m, kt in enumerate(tiles):
                    for x, piece in enumerate((hi, lo)):
                        ins = nc.tensor.matmul(bank[0:2 * VC, :], p["v"][0:rows, kt, hd, :], piece[0:rows, m, :],
                                               start=(kt == 0 and x == 0), stop=(kt == KT - 1 and x == 1))
                t = k.pe.mark(ins)
                highs.release(ih, t)
                lows.release(il, t)
                if kp < KTP - 1:
                    return
                jr, orow = o_rows.take(A)
                t = A.mark(A.after(t).copy(orow[:], bank[0:2 * VC, :]))
                banks.release(io, t)
                i, bank = banks.take(k.pe)
                k.pe.after(t, t_fold)
                for qt in range(TPB):
                    ins = nc.tensor.matmul(bank[:, qt * VC:(qt + 1) * VC], orow[:, qt * P:(qt + 1) * P], fold[:],
                                           start=True, stop=True)
                t = k.pe.mark(ins)
                o_rows.release(jr, t)
                view = bank[:, 0:TPB * VC].rearrange("p (t c) -> p t c", c=VC)
                js, rs = rsum.take(V)
                t = V.mark(V.after(t).reciprocal(rs[:], view[:, :, NX]))
                t = V.mark(V.after(t).tensor_tensor(p["o"][:, :, hd * NX:(hd + 1) * NX], view[:, :, 0:NX],
                                                    rs[:].unsqueeze(2).to_broadcast([P, TPB, NX]), ALU.mult))
                rsum.release(js, t)
                banks.release(i, t)
                p["t_o"] = t

            def step(a, kp):
                if len(flying) > 3:
                    product()
                if fresh:
                    halve()
                pair(a, kp)

            for a in range(HU):
                for kp in range(KTP):
                    steps.append(lambda a=a, kp=kp: step(a, kp))
            def drain():
                while fresh:
                    halve()
                while flying:
                    product()
                if half:
                    values.release(p["jv"], k.pe.last())
                    project(b)
            steps.append(drain)
            return steps

        def project(b):
            p = batch[b]
            jc, oc = o_ch.take(A)
            for h in range(HALVES):
                i, bank = pairs.take(k.pe)
                k.pe.after(p["t_o"])
                for n in range(TPB):
                    ins = nc.tensor.transpose(bank[:, n * P:(n + 1) * P], p["o"][:, n, h * P:(h + 1) * P], const(k, "ident"))
                t = k.pe.mark(ins)
                t_oc = A.mark(A.after(t).copy(oc[:, h, :], bank[:, 0:T]))
                pairs.release(i, t_oc)
            o_tok.release(p["jo"], k.pe.last())
            for n in range(0, TPB, 2):
                i, bank = pairs.take(k.pe)
                for m in range(2):
                    t = k.matmuls(bank[:, m * D:(m + 1) * D], [(oc[:, h, (n + m) * P:(n + m + 1) * P], wo[:, h, :])
                                                               for h in range(HALVES)], t_oc)
                tile = b * TPB + n
                t = V.mark(V.after(t, t_bias).tensor_tensor(
                    k.x_tok[:, tile:tile + 2, :], bank[:, 0:2 * D].rearrange("p (m d) -> p m d", d=D),
                    k.x_tok[:, tile:tile + 2, :], ALU.add))
                pairs.release(i, t)
                ready[tile] = ready[tile + 1] = t
            o_ch.release(jc, k.pe.last())
            norm_group(k, ready, b)

        def finish_channels(b):
            k.ch[b] = []
            for h in range(HALVES):
                i, bank = pairs.take(k.pe)
                k.pe.after(*[k.tok[b * TPB + n] for n in range(TPB)])
                for n in range(TPB):
                    ins = nc.tensor.transpose(bank[:, n * P:(n + 1) * P], k.x_tok[:, b * TPB + n, h * P:(h + 1) * P], const(k, "ident"))
                t = k.pe.mark(ins)
                t = A.mark(A.after(t, batch[b]["t_read"]).copy(k.x_ch[:, h, b * T:(b + 1) * T], bank[:, 0:T]))
                pairs.release(i, t)
                k.ch[b].append(t)

        for step in prepare_batch(0) + prepare_unit(0):
            step()
        for u in range(2 * B):
            side = []
            if u + 1 < 2 * B:
                if u % 2:
                    side += prepare_batch((u + 1) // 2)
                side += prepare_unit(u + 1)
            side += [lambda: None] * (len(side) // 12)
            if u > 1 and u % 2 == 0:
                side.insert(len(side) // 2, lambda: finish_channels(u // 2 - 1))
            run(mingle(attend(u), side))
        finish_channels(B - 1)
        k.barrier()


def windowed(k):
    kept = None
    for layer in range(2):
        with ExitStack() as ctx:
            w1 = k.sb(ctx, "w1_f32_%d" % layer, [P, HALVES, 2 * HID])
            ready = {}
            t_w1, kept = windowed_attention(k, layer, ready, w1, kept)
            gated_ffn(k, layer, ready, w1, t_w1, kept)


def windowed_attention(k, layer, ready, w1, kept):
    nc, V, A, G = k.nc, k.dve, k.act, k.pool
    half = NL // 2
    WU, UNITS = 2, TILES // 2
    LAG = 3
    with ExitStack() as ctx:
        sb = lambda name, shape, dt=F32: k.sb(ctx, name + "_l%d" % layer, shape, dt)
        ring = lambda name, n, shape, dt=F32: Ring([sb("%s%d" % (name, i), shape, dt) for i in range(n)])
        wqkv, wo = sb("wqkv", [P, 2, HALVES, 3 * INNER], BF16), sb("wo", [P, 4, D])
        shifted, x_hl = ring("x_shifted", 1, [P, WU * P]), ring("x_hl", 2, [P, 2, HALVES, WU * P], BF16)
        tab = sb("rotary", [P, TPB, 4, NL])
        mask, mask_b, ident_b = sb("mask", [P, 2 * P]), sb("mask_b", [P, 2 * P], BF16), sb("ident_b", [P, P], BF16)
        raws = ring("qk_raw", 2, [P, WU, 2, INNER])
        squares = ring("qk_sq", 1, [P, 2 * INNER])
        norms = ring("qk_norm", 3, [P, WU, 2 * HL])
        turned, other = ring("qk_rot", LAG + 2, [P, INNER]), ring("qk_other", 2, [P, INNER])
        q_pad = [sb("w_q%d" % n, [P, 2, 4, WU * P]) for n in range(2)]
        k_ch, v_tok = ring("w_k", 3, [P, 4, WU * P]), ring("w_v", 5, [P, WU, INNER])
        probs, probs_t = ring("w_p", 2, [P, HL, 2 * P]), ring("w_pt", 2, [P, HL, 2, P])
        maxes, sums = ring("w_max", 2, [P, HL]), ring("w_sum", 2, [P, HL])
        o_ch = ring("w_oc", 2, [P, 4, P])

        for n in range(2):
            t_zero = G.mark(nc.gpsimd.memset(q_pad[n][:], 0.0))
        q_pad = Ring(q_pad)

        t_w = []
        for h in range(HALVES):
            j, buf = raws.take(k.sp)
            src = buf[:].rearrange("p w a c -> p (w a c)")[:, 0:3 * INNER]
            t = k.load("wqkv%d_%d" % (layer, h), (src, k.dram["wqkv"][layer, h * P:(h + 1) * P, :]))
            t = A.mark(A.after(t).copy(wqkv[:, 0, h, :], src))
            t_w.append(V.mark(V.after(t).tensor_tensor(wqkv[:, 1, h, :], src, wqkv[:, 0, h, :], ALU.subtract)))
            raws.release(j, t_w[-1])
        t_tables = k.load("win%d" % layer, (tab[:], k.dram["rotary"]), (mask[:], k.dram["mask"]))
        t_wo = k.load("wo%d" % layer, (wo[:], k.dram["wo"][layer].rearrange("(c p) o -> p c o", p=P)))
        if layer == 0:
            kept = k.load("x_kept", (k.dram["kept"], k.x_tok[:]), after=[k.tok[i] for i in range(TILES)])
        t_w1 = k.load("w1_%d" % layer, (w1[:], k.dram["w1"][layer].rearrange("(h p) o -> p h o", p=P)))
        V.after(t_tables)
        V.mark(nc.vector.tensor_copy(mask_b[:], mask[:]))
        V.mark(nc.vector.tensor_copy(ident_b[:], const(k, "ident")))
        for n, name in ((0, "q_scale"), (2, "k_scale")):
            s = row(k, name, layer * NL, (layer + 1) * NL)
            wide = lambda a, w: a.unsqueeze(1).to_broadcast([P, TPB, w])
            V.mark(nc.vector.tensor_tensor(tab[:, :, n, :], tab[:, :, n, :], wide(s, NL), ALU.mult))
            V.mark(nc.vector.tensor_tensor(tab[:, :, n + 1, 0:half], tab[:, :, n + 1, 0:half], wide(s[:, half:NL], half), ALU.mult))
            t_tab = V.mark(nc.vector.tensor_tensor(tab[:, :, n + 1, half:NL], tab[:, :, n + 1, half:NL], wide(s[:, 0:half], half), ALU.mult))
        t_ch = [t for g in range(4) for t in k.ch[g]]

        def split_x(u):
            s = unit[u]
            c0, n = u * WU * P, WU * P
            j, sh = shifted.take(V)
            first = (u * WU) % TPB == 0
            if first:
                V.mark(nc.vector.memset(sh[:, 0:1], 0.0))
            t = V.mark(V.after(*t_ch).tensor_copy(sh[:, first:n], k.x_ch[:, 1, c0 - 1 + first:c0 + n - 1]))
            s["jx"], x = x_hl.take(A)
            G.after(*x_hl.readers[s["jx"]])
            A.after(t, V.last(), *t_ch)
            lows = []
            for h, src in enumerate((k.x_ch[:, 0, c0:c0 + n], sh[:])):
                t = A.mark(nc.scalar.copy(x[:, 0, h, :], src))
                lows.append(G.mark(G.after(t).tensor_tensor(x[:, 1, h, :], src, x[:, 0, h, :], ALU.subtract)))
            shifted.release(j, lows[-1])
            s["x"], s["t_x"] = x, lows
        heads3 = lambda a: a.rearrange("p (h c) -> p h c", c=NL)
        unit = {}
        free = [None, None]

        def produce(u):
            s = unit[u] = {"t": []}

            def project(w, which):
                if (w, which) == (0, 0):
                    s["jr"], s["raw"] = raws.take(A)
                    s["jn"], s["norm"] = norms.take(V)
                    s["v"] = v_tok.take(A)
                cols_w = slice(which * INNER, (which + 1) * INNER)
                i, bank = k.banks.take(k.pe)
                t = k.matmuls(bank, [(s["x"][:, x, h, w * P:(w + 1) * P], wqkv[:, y, h, cols_w])
                                     for h in range(HALVES) for x, y in PASSES], *t_w, *s["t_x"])
                if (w, which) == (WU - 1, 2):
                    x_hl.release(s["jx"], t)
                dst = s["v"][1][:, w, :] if which == 2 else s["raw"][:, w, which, :]
                t = A.mark(A.after(t).copy(dst, bank))
                k.banks.release(i, t)
                if which == 2:
                    s["t_v"] = t
                if which == 1:
                    js, sq = squares.take(A)
                    t = A.mark(A.after(t).activation(sq[:], s["raw"][:, w, :, :].rearrange("p a c -> p (a c)"), ACT.Square))
                    s["t_raw"] = t
                    s["t_ss"] = V.mark(V.after(t).tensor_reduce(s["norm"][:, w, :], sq[:].rearrange("p (h c) -> p h c", c=NL), AX.X, ALU.add))
                    squares.release(js, s["t_ss"])

            def invert():
                nm = s["norm"]
                t = A.mark(A.after(s["t_ss"]).activation(nm[:], nm[:], ACT.Sqrt))
                t = V.mark(V.after(t).tensor_scalar(nm[:], nm[:], 1e-12, None, ALU.max))
                s["t_n"] = V.mark(V.after(t).reciprocal(nm[:], nm[:]))

            def rotate(w, which):
                x3 = heads3(s["raw"][:, w, which, :])
                nm = s["norm"][:, w, which * HL:(which + 1) * HL]
                jo, ot = other.take(G)
                o3 = heads3(ot[:])
                wide = lambda a, n: a.unsqueeze(1).to_broadcast([P, HL, n])
                tw = (u * WU + w) % TPB
                sin = tab[:, tw, 2 * which + 1, :]
                G.after(s["t_raw"], t_tab)
                G.mark(nc.gpsimd.tensor_tensor(o3[:, :, 0:half], x3[:, :, half:NL], wide(sin[:, 0:half], half), ALU.mult))
                t2 = G.mark(nc.gpsimd.tensor_tensor(o3[:, :, half:NL], x3[:, :, 0:half], wide(sin[:, half:NL], half), ALU.mult))
                jt, tn = turned.take(V)
                t1 = V.mark(V.after(s["t_raw"], t_tab).tensor_tensor(heads3(tn[:]), x3, wide(tab[:, tw, 2 * which, :], NL), ALU.mult))
                t = V.mark(V.after(t1, t2).tensor_tensor(tn[:], tn[:], ot[:], ALU.add))
                other.release(jo, t)
                t = V.mark(V.after(t, s["t_n"]).tensor_tensor(heads3(tn[:]), heads3(tn[:]), nm.unsqueeze(2).to_broadcast([P, HL, NL]), ALU.mult))
                s["turn", w, which] = (jt, tn, t)

            def turn(w, which):
                jt, tn, t = s["turn", w, which]
                if w == 0:
                    name, rng = (("q", q_pad), ("k", k_ch))[which]
                    s[name] = rng.take(A)
                i, bank = k.banks.take(k.pe)
                k.pe.after(t)
                for c in range(4):
                    ins = nc.tensor.transpose(bank[:, c * P:(c + 1) * P], tn[:, c * P:(c + 1) * P], const(k, "ident"))
                t = k.pe.mark(ins)
                turned.release(jt, t)
                view = bank.rearrange("p (c t) -> p c t", t=P)
                cw = slice(w * P, (w + 1) * P)
                if which:
                    t = A.mark(A.after(t).copy(s["k"][1][:, :, cw], view))
                else:
                    A.after(t, t_zero)
                    for x in range(2):
                        lanes = slice(NL * x, NL * (x + 1))
                        t = A.mark(nc.scalar.copy(s["q"][1][lanes, x, :, cw], view[lanes]))
                k.banks.release(i, t)
                s["t"].append(t)
                if (w, which) == (WU - 1, 1):
                    norms.release(s["jn"], V.last())
                    raws.release(s["jr"], V.last(), G.last())

            order = [(w, which) for w in range(WU) for which in range(2)]
            second = []
            for n, o in enumerate(order):
                second.append(lambda o=o: rotate(*o))
                if n >= LAG:
                    second.append(lambda o=order[n - LAG]: turn(*o))
            for o in order[-LAG:]:
                second.append(lambda o=o: turn(*o))
            projects = [lambda w=w, which=which: project(w, which) for w in range(WU) for which in range(3)]
            following = [lambda: split_x(u + 1)] if u + 1 < UNITS else []
            return projects[:4] + following + projects[4:] + [invert], second

        def attend(u):
            s = unit[u]
            window = {}

            def score(w):
                qp = s["q"][1]
                a = 0 if (u * WU + w) % TPB else 1
                lo = a * P
                if a:
                    keys = [(s["k"][1][:, :, 0:P], P, 2 * P)]
                elif w:
                    keys = [(s["k"][1], 0, 2 * P)]
                else:
                    keys = [(unit[u - 1]["k"][1][:, :, P:2 * P], 0, P), (s["k"][1][:, :, 0:P], P, 2 * P)]
                m = window[w] = {"a": a}
                k.pe.after(*s["t"], t_tab)
                for x in range(2):
                    k.pe.after(free[x])
                    for bk in (2 * x, 2 * x + 1):
                        out = k.psum[:, bk, :].rearrange("p (x j) -> p x j", x=2)[:, :, lo:2 * P]
                        nc.tensor.matmul(out, ident_b[:], mask_b[:, lo:2 * P].unsqueeze(1).to_broadcast([P, 2, 2 * P - lo]),
                                         start=True, stop=False, skip_group_check=True)
                    for p in range(4):
                        for kc, c0, c1 in keys:
                            out = k.psum[:, 2 * x + p // 2, (p % 2) * 2 * P + c0:(p % 2) * 2 * P + c1]
                            ins = nc.tensor.matmul(out, qp[:, x, p, w * P:(w + 1) * P], kc[:, p, :],
                                                   start=False, stop=True, skip_group_check=True)
                    m["t_s", x] = k.pe.mark(ins)
                if w == 0 and u:
                    k_ch.release(unit[u - 1]["k"][0], m["t_s", 1])
                if w == WU - 1:
                    q_pad.release(s["q"][0], m["t_s", 1])

            def softmax(w):
                m = window[w]
                lo = m["a"] * P
                jm, mx = maxes.take(V)
                m["jp"], pr = probs.take(A)
                js, sm = sums.take(A)
                m["p"] = pr
                sc = k.psum[:, 0:4, :].rearrange("p b (x j) -> p (b x) j", x=2)[:, :, lo:2 * P]
                halves = (slice(0, 4), slice(4, 8))
                for x, h in enumerate(halves):
                    t = V.mark(V.after(m["t_s", x]).tensor_reduce(mx[:, h], sc[:, h], AX.X, ALU.max))
                    t = V.mark(V.after(t).tensor_scalar(mx[:, h], mx[:, h], -8.0, None, ALU.mult))
                    A.after(t)
                    for i in range(4 * x, 4 * x + 4):
                        t = A.mark(nc.scalar.activation(pr[:, i, lo:2 * P], sc[:, i, :], ACT.Exp, bias=mx[:, i:i + 1],
                                                        scale=8.0, accum_out=sm[:, i:i + 1]))
                    free[x] = t
                maxes.release(jm, t)
                for x, h in enumerate(halves):
                    t = V.mark(V.after(free[x]).reciprocal(sm[:, h], sm[:, h]))
                    V.after(t)
                    for i in range(4 * x, 4 * x + 4):
                        t = V.mark(nc.vector.tensor_scalar(pr[:, i, lo:2 * P], pr[:, i, lo:2 * P], sm[:, i:i + 1], None, ALU.mult))
                    m["t_p", x] = t
                sums.release(js, t)

            def turn(w):
                m = window[w]
                jt, pt = probs_t.take(A)
                V.after(*probs_t.readers[jt])
                a, per = m["a"], 2 - m["a"]
                copied = []
                blocks = [(x, kk) for x in range(HL) for kk in range(a, 2)]
                for g in range(0, len(blocks), 4):
                    i, bank = k.banks.take(k.pe)
                    k.pe.after(m["t_p", blocks[g][0] // 4])
                    for n, (x, kk) in enumerate(blocks[g:g + 4]):
                        ins = nc.tensor.transpose(bank[:, n * P:(n + 1) * P], m["p"][:, x, kk * P:(kk + 1) * P], const(k, "ident"))
                    t = k.pe.mark(ins)
                    x0, cnt = blocks[g][0], 4 // per
                    t = evacuate(k, g // 4, pt[:, x0:x0 + cnt, a:2, :], bank.rearrange("p (x c q) -> p x c q", x=cnt, q=P), t)
                    k.banks.release(i, t)
                    copied.append(t)
                probs.release(m["jp"], k.pe.last())
                m["jt"], m["pt"], m["copied"] = jt, pt, copied

            def combine(w):
                m = window[w]
                at = lambda kk: (s["v"][1][:, w - 1 + kk] if w - 1 + kk >= 0 else unit[u - 1]["v"][1][:, WU - 1])
                io, obank = k.banks.take(k.pe)
                k.pe.after(*m["copied"], s["t_v"])
                for x in range(2):
                    for p in range(4):
                        hd = 2 * p + x
                        for kk in range(m["a"], 2):
                            ins = nc.tensor.matmul(obank[NL * x:NL * (x + 1), p * P:(p + 1) * P],
                                                   at(kk)[:, hd * NL:(hd + 1) * NL], m["pt"][:, 4 * x + p, kk, :],
                                                   start=(kk == m["a"]), stop=(kk == 1))
                t = k.pe.mark(ins)
                probs_t.release(m["jt"], t)
                if w == 0 and u:
                    v_tok.release(unit[u - 1]["v"][0], t)
                jc, oc = o_ch.take(A)
                t = A.mark(A.after(t).copy(oc[:].rearrange("p c t -> p (c t)"), obank))
                k.banks.release(io, t)
                m["oc"] = (jc, oc, t)

            def output(w):
                jc, oc, t = window[w]["oc"]
                i, bank = k.banks.take(k.pe)
                t = k.matmuls(bank[:, 0:D], [(oc[:, c, :], wo[:, c, :]) for c in range(4)], t, t_wo)
                o_ch.release(jc, t)
                tile = u * WU + w
                ready[tile] = V.mark(V.after(t, *before).tensor_tensor(k.x_tok[:, tile, :], bank[:, 0:D], k.x_tok[:, tile, :], ALU.add))
                k.banks.release(i, ready[tile])

            return [[lambda w=w, f=f: f(w) for f in (score, softmax, turn, combine, output)] for w in range(WU)]

        before = [kept] + [k.tok[i] for i in range(TILES)]
        steps = [produce(u) for u in range(UNITS)]
        split_x(0)
        run(steps[0][0] + steps[0][1] + steps[1][0])
        tail, last = [], []
        for u in range(UNITS):
            main = []
            for score, softmax, turn, combine, output in attend(u):
                main += [score] + tail[0:1] + [softmax] + tail[1:2] + last
                last, tail = tail[2:], [turn, combine, output]
            rotations = steps[u + 1][1] if u + 1 < UNITS else []
            projections = steps[u + 2][0] if u + 2 < UNITS else []
            run(mingle(main, mingle(rotations, projections)))
        run(last + tail)
        k.barrier()
        return t_w1, kept


def gated_ffn(k, layer, ready, w1_f32, t_w1, kept):
    nc, V, A, G = k.nc, k.dve, k.act, k.pool
    with ExitStack() as ctx:
        sb = lambda name, shape, dt=F32: k.sb(ctx, name + "_f%d" % layer, shape, dt)
        ring = lambda name, n, shape, dt=F32: Ring([sb("%s%d" % (name, i), shape, dt) for i in range(n)])
        w2_f32 = sb("w2_f32", [P, HT, D])
        w1, w2 = sb("w1", [P, 2, HALVES, 2 * HID], BF16), sb("w2", [P, 2, HT, D], BF16)
        h_tok, stats = ring("h_tok", 2, [P, TPB, D]), ring("h_stats", 2, [P, TPB, 2, 6])
        values = ring("h_f32", 3, [P, BANK])
        h_ch = ring("h_ch", 2, [P, 2, HALVES, BANK], BF16)
        gates, acts = ring("gelu", 2, [P, BANK]), ring("h_act", 3, [P, BANK])
        hidden = ring("hidden", 2, [P, 2, HT, BANK], BF16)
        full = (HT - 1) * P
        t_w2 = k.load("w2_%d" % layer, (w2_f32[:, 0:HT - 1, :], k.dram["w2"][layer][0:full].rearrange("(c p) o -> p c o", p=P)),
                      (w2_f32[0:HLAST, HT - 1, :], k.dram["w2"][layer][full:HID]))

        if layer:
            x_in = sb("x_in", [P, TILES, D])
            t_in = k.load("x_in", (x_in[:], k.dram["kept"]), after=(kept,))

        def split(high, low, src, *after):
            t = A.mark(A.after(*after).copy(high, src))
            return G.mark(G.after(t).tensor_tensor(low, src, high, ALU.subtract))

        group = {}

        def normalise(g):
            s = group[g] = {}
            x = k.x_tok[:, 4 * g:4 * g + 4, :]
            i, late = k.banks.take(k.pe)
            k.pe.after(*[ready[4 * g + n] for n in range(4)])
            nc.tensor.matmul(late, const(k, "shift"), x[:, :, P:D], start=True, stop=False, skip_group_check=True)
            t = k.pe.mark(nc.tensor.matmul(late[:, P:4 * P], const(k, "carry"), x[:, 0:3, P:D],
                                           start=False, stop=True, skip_group_check=True))
            js, st = stats.take(V)
            jh, ht = h_tok.take(V)
            s["h"] = (jh, ht)
            V.after(t, ready[4 * g + 3])
            for n in range(TPB):
                V.mark(nc.vector.bn_stats(st[:, n, 0, :], x[:, n, 0:P]))
                t = V.mark(nc.vector.bn_stats(st[:, n, 1, :], late[:, n * P:(n + 1) * P]))
            V.after(t)
            for n in range(TPB):
                t = V.mark(nc.vector.bn_aggr(k.mv[:, 4 * g + n, :], st[:, n, :, :].rearrange("p a s -> p (a s)")))
            stats.release(js, t)
            tiles = slice(4 * g, 4 * g + 4)
            t = A.mark(A.after(t, k.t_eps).activation(k.std[:, tiles], k.mv[:, tiles, 1], ACT.Sqrt, bias=k.eps[:, 0:1]))
            t = V.mark(V.after(t).reciprocal(k.rstd[:, tiles], k.std[:, tiles]))
            V.after(t)
            for n in range(TPB):
                tile = 4 * g + n
                for c, src in ((0, x[:, n, 0:P]), (1, late[:, n * P:(n + 1) * P])):
                    t = V.mark(nc.vector.tensor_scalar(ht[:, n, c * P:(c + 1) * P], src, k.mv[:, tile, 0:1],
                                                       k.rstd[:, tile:tile + 1], ALU.subtract, ALU.mult))
            k.banks.release(i, t)
            s["t_b2"] = G.mark(G.after(t).tensor_tensor(
                x, x, row(k, "b2", layer * D, (layer + 1) * D).unsqueeze(1).to_broadcast([P, TPB, D]), ALU.add))
            if layer:
                s["t_b2"] = G.mark(G.after(s["t_b2"], t_in).tensor_tensor(x, x, x_in[:, tiles, :], ALU.add))
            s["t_h"] = t

        def transpose(g):
            s = group[g]
            jh, ht = s["h"]
            s["jc"], s["ch"] = h_ch.take(A)
            V.after(*h_ch.readers[s["jc"]])
            G.after(*h_ch.readers[s["jc"]])
            s["t_ch"] = []
            for h in range(HALVES):
                i, bank = k.banks.take(k.pe)
                k.pe.after(s["t_h"])
                for n in range(TPB):
                    ins = nc.tensor.transpose(bank[:, n * P:(n + 1) * P], ht[:, n, h * P:(h + 1) * P], const(k, "ident"))
                t = k.pe.mark(ins)
                jv, v = values.take(A)
                t = A.mark(A.after(t).activation(v[:], bank, ACT.Identity, scale=col(k, "lg", 2 * layer + h),
                                                 bias=col(k, "lb", 2 * layer + h)))
                k.banks.release(i, t)
                t = V.mark(V.after(t).tensor_copy(s["ch"][:, 0, h, :], v[:]))
                t = V.mark(V.after(t).tensor_tensor(s["ch"][:, 1, h, :], v[:], s["ch"][:, 0, h, :], ALU.subtract))
                values.release(jv, t)
                s["t_ch"].append(t)
            h_tok.release(jh, k.pe.last())

        def first(g, ft):
            s = group[g]
            if ft == 0:
                s["jh"], s["hid"] = hidden.take(A)
                V.after(*hidden.readers[s["jh"]])
                G.after(*hidden.readers[s["jh"]])
                s["t_hid"] = []
            rows = P if ft < HT - 1 else HLAST
            got = []
            for part in range(2):
                i, bank = k.banks.take(k.pe)
                o = part * HID + ft * P
                t = k.matmuls(bank[0:rows, :], [(w1[:, y, h, o:o + rows], s["ch"][:, x, h, :])
                                                for h in range(HALVES) for x, y in PASSES], *t_w1s, *s["t_ch"])
                got.append((i, bank, t))
            jg, gg = gates.take(A)
            t = A.mark(A.after(got[1][2]).activation(gg[0:rows, :], got[1][1][0:rows, :], ACT.Gelu,
                                                     bias=col(k, "b1g", HT * layer + ft, rows)))
            k.banks.release(got[1][0], t)
            ja, act = acts.take(V)
            t = V.mark(V.after(t, got[0][2]).scalar_tensor_tensor(
                act[0:rows, :], got[0][1][0:rows, :], col(k, "b1a", HT * layer + ft, rows), gg[0:rows, :], ALU.add, ALU.mult))
            k.banks.release(got[0][0], t)
            gates.release(jg, t)
            hd = s["hid"]
            t = split(hd[0:rows, 0, ft, :], hd[0:rows, 1, ft, :], act[0:rows, :], t)
            acts.release(ja, t)
            s["t_hid"].append(t)
            if ft == HT - 1:
                h_ch.release(s["jc"], got[1][2])

        def second(g, pair):
            s = group[g]
            hd = s["hid"]
            i, bank = k.banks.take(k.pe)
            k.pe.after(*s["t_hid"], *t_w2s)
            for n in range(2):
                m = slice((2 * pair + n) * P, (2 * pair + n + 1) * P)
                t = k.matmuls(bank[:, n * D:(n + 1) * D],
                              [(hd[0:(P if ft < HT - 1 else HLAST), x, ft, m], w2[0:(P if ft < HT - 1 else HLAST), y, ft, :])
                               for ft in range(HT) for x, y in PASSES])
            tile = 4 * g + 2 * pair
            t = V.mark(V.after(t, s["t_b2"]).tensor_tensor(k.x_tok[:, tile:tile + 2, :], bank.rearrange("p (n d) -> p n d", n=2),
                                                           k.x_tok[:, tile:tile + 2, :], ALU.add))
            ready[tile] = ready[tile + 1] = t
            k.banks.release(i, t)
            if pair:
                hidden.release(s["jh"], k.pe.last())
                if layer:
                    tiles = range(4 * g, 4 * g + 4)
                    k.tok.update(layer_norm(k, k.x_tok, k.x_tok, ready, 0, tiles))
                    store(k, g)

        normalise(0)
        t_w1s = [split(w1[:, 0, h, :], w1[:, 1, h, :], w1_f32[:, h, :], t_w1) for h in range(HALVES)]
        transpose(0)
        normalise(1)
        t_w2s = [split(w2[:, 0, 0:HT - 1, :], w2[:, 1, 0:HT - 1, :], w2_f32[:, 0:HT - 1, :], t_w2),
                 split(w2[0:HLAST, 0, HT - 1, :], w2[0:HLAST, 1, HT - 1, :], w2_f32[0:HLAST, HT - 1, :], t_w2)]
        for g in range(B):
            main = [lambda ft=ft: first(g, ft) for ft in range(HT)]
            side = [lambda pair=pair: second(g - 1, pair) for pair in range(2)] if g else []
            if g + 1 < B:
                side.append(lambda: transpose(g + 1))
            if g + 2 < B:
                side.append(lambda: normalise(g + 2))
            run(mingle(main, side))
        for pair in range(2):
            second(B - 1, pair)
        if layer == 0:
            k.ch = to_channels(k, k.x_tok, k.x_ch, ready)
            k.tok = dict(ready)
        k.barrier()


STAGES = [rwkv, bitnet, experts, linear_attention, cross_attention, windowed]


def store(k, g):
    tiles = slice(4 * g, 4 * g + 4)
    k.sp.after(*[k.tok[4 * g + n] for n in range(4)])
    k.nc.sync.dma_start(k.dram["out"].rearrange("(n p) d -> p n d", p=P)[:, tiles, :], k.x_tok[:, tiles, :]).then_inc(k.stored, 16)


def build(nc, dram, stages=range(6)):
    dram["kept"] = nc.dram_tensor("kept", (P, TILES, D), F32, kind="Internal").ap()
    dram["regroup"] = nc.dram_tensor("regroup", (B, N0, N0, H0, T // N0), F32, kind="Internal").ap()
    k = Core(nc, dram)
    with k.ctx:
        setup(k)
        for n in stages:
            STAGES[n](k)
        nc.sync.wait_ge(k.stored, 16 * 4)


def host_layout(inp):
    f = lambda n: np.asarray(inp[n])
    chan = lambda a: np.asarray(a).reshape(-1, P).T

    def hidden(a):
        z = np.zeros((HT * P,), a.dtype)
        z[:HID] = a
        return z.reshape(HT, P).T

    b1 = f("L1_ffn_b1")
    cols = {
        "maa_k": chan(f("L0_attn_time_maa_k")), "maa_v": chan(f("L0_attn_time_maa_v")),
        "maa_r": chan(f("L0_attn_time_maa_r")), "maa_g": chan(f("L0_attn_time_maa_g")),
        "decay": chan(np.repeat(f("L0_attn_time_decay"), N0)),
        "ln_g": chan(f("L0_attn_ln_g")), "ln_b": chan(f("L0_attn_ln_b")),
        "b_d2v": chan(f("L0_xattn_b_d2v")), "b_img": chan(f("L0_xattn_b_img")), "b_txt": chan(f("L0_xattn_b_txt")),
        "b_att0": chan(f("L0_xattn_b_att0")), "b_att1": chan(f("L0_xattn_b_att1")), "b_f1": chan(f("L0_xattn_b_f1")),
        "moe_gamma": chan(f("L0_ffn_gamma")), "moe_beta": chan(f("L0_ffn_beta")), "moe_b1": chan(f("L0_ffn_b1")),
        "la_bq": chan(f("L1_attn_b_qkv")[:D]), "xa_bq": chan(f("L1_xattn_bq")), "xa_bk": chan(f("L1_xattn_bk")),
        "lg": chan(f("L1_ffn_ln_g")), "lb": chan(f("L1_ffn_ln_b")),
        "b1a": np.concatenate([hidden(b1[l, :HID]) for l in range(2)], 1),
        "b1g": np.concatenate([hidden(b1[l, HID:]) for l in range(2)], 1),
    }
    rows = {
        "decay": f("L0_attn_time_decay"), "faaaa": f("L0_attn_time_faaaa"),
        "b_att0": f("L0_xattn_b_att0"), "b_att1": f("L0_xattn_b_att1"),
        "b_f2": f("L0_xattn_b_f2"), "la_bkv": f("L1_attn_b_qkv")[D:], "la_bproj": f("L1_attn_b_proj"),
        "la_gamma": f("L1_attn_gamma"), "la_beta": f("L1_attn_beta"), "xa_bv": f("L1_xattn_bv"),
        "xa_bo": f("L1_xattn_bo"), "q_scale": f("L1_ffn_q_scale").reshape(-1),
        "k_scale": f("L1_ffn_k_scale").reshape(-1), "b2": f("L1_ffn_b2").reshape(-1),
    }
    x = f("x").reshape(NTOK, D)
    return {
        "const": shape_constants(), "rotary": rotary_tables(), "mask": window_mask(),
        "cols": np.concatenate([cols[n] for n, _ in COLS], 1), "rows": np.concatenate([rows[n] for n, _ in ROWS]),
        "x": x, "xT": x.T, "ctxT": f("ctx_768").transpose(2, 0, 1),
        **{"w_%sT" % n: f("L0_attn_w_" + n).T for n in "rkvgo"},
        **{"bn_" + n: f("L0_xattn_W_" + n).T for n in ("d2v", "img", "txt", "att0", "att1", "f1", "f2")},
        "moe_wg": f("L0_ffn_Wg"), "moe_w1": f("L0_ffn_W1"), "moe_w2": f("L0_ffn_W2"), "moe_b2": f("L0_ffn_b2"),
        "la_qkvT": f("L1_attn_W_qkv").T, "la_projT": f("L1_attn_W_proj").T,
        "xa_q": f("L1_xattn_Wq"), "xa_k": f("L1_xattn_Wk"), "xa_v": f("L1_xattn_Wv"), "xa_o": f("L1_xattn_Wo"),
        "wqkv": f("L1_ffn_wqkv"), "wo": f("L1_ffn_wo"), "w1": f("L1_ffn_w1"), "w2": f("L1_ffn_w2"),
    }


def kernel(**inputs):
    import concourse.bacc as bacc
    from concourse.bass_utils import run_bass_kernel_spmd

    nc = bacc.Bacc("TRN2", target_bir_lowering=False, num_devices=1)
    arrays = {n: np.ascontiguousarray(a) for n, a in host_layout(inputs).items()}
    dram = {n: nc.dram_tensor("in_" + n, a.shape, mybir.dt.from_np(a.dtype), kind="ExternalInput").ap()
            for n, a in arrays.items()}
    dram["out"] = nc.dram_tensor("out", (NTOK, D), F32, kind="ExternalOutput").ap()
    build(nc, dram)
    r = run_bass_kernel_spmd(nc, [{"in_" + n: a for n, a in arrays.items()}], core_ids=[0])
    return r.results[0]["out"].reshape(B, T, D)
```
